# Optimizing a Trainium2 kernel written in Bass

```python
import numpy as np
import jax
import jax.numpy as jnp

def _softmax(x, axis=-1):
    return jax.nn.softmax(x, axis=axis)

def _gelu(x):
    return jax.nn.gelu(x, approximate=True)

def _silu(x):
    return jax.nn.silu(x)

def _sigmoid(x):
    return jax.nn.sigmoid(x)

def _layernorm(x, axis=-1, eps=1e-05):
    m = jnp.mean(x, axis=axis, keepdims=True)
    v = jnp.var(x, axis=axis, keepdims=True)
    return (x - m) / jnp.sqrt(v + eps)

def _scatter_add(tgt, idx, src, axis=0):
    return tgt.at[idx].add(src)

def _segment_sum(src, seg, n):
    return jax.ops.segment_sum(src, seg, n)
kernel_name = 'mk_decoder_postln_d1_seqx_r8_675d49'

def setup_inputs(seed: int=0):
    np.random.seed(seed)
    _w = jnp.asarray

    def _rec_inputs():
        import jax
        import jax.numpy as jnp
        _rk = jax.random.key(seed)
        x = -0.000125 + 0.9999 * jax.random.normal(jax.random.fold_in(_rk, 1), (4, 256, 256), jnp.float32)
        _lenS = 256 - jax.random.randint(jax.random.fold_in(_rk, 7), (4,), 0, max(1, 256 // 4) + 1, jnp.int32)
        _lenS2 = 256 - jax.random.randint(jax.random.fold_in(_rk, 8), (4,), 0, max(1, 256 // 4) + 1, jnp.int32)
        itok_BxS_13_99985 = jax.random.randint(jax.random.fold_in(_rk, 11), (4, 256), 13, 99986, jnp.int32)
        _ctx_2048P = jax.random.normal(jax.random.fold_in(_rk, 12), (4, 16, 256), jnp.float32)
        _ctx_2048c = jax.random.dirichlet(jax.random.fold_in(_rk, 512), 0.3 * jnp.ones((16,), jnp.float32), (4, 256))
        _ctx_2048t = jnp.einsum('bsk,bkd->bsd', _ctx_2048c, _ctx_2048P)
        _ctx_2048t = _ctx_2048t * jax.lax.rsqrt(jnp.mean(jnp.square(_ctx_2048t)) + 1e-12) * 0.953939
        ctx_2048 = 6.82029e-06 + 0.0200006 * (_ctx_2048t + 0.3 * jax.random.normal(jax.random.fold_in(_rk, 612), (4, 256, 256), jnp.float32))
        return (x, itok_BxS_13_99985, ctx_2048)
    x, itok_BxS_13_99985, ctx_2048 = _rec_inputs()

    def _L0_attn_setup():
        import math
        import jax, jax.numpy as jnp
        import numpy as np
        D_MODEL = 256
        NUM_HEADS = 16
        key = jax.random.key(seed)
        k1, k2, k3, k4, k5 = jax.random.split(key, 5)
        s = 1.0 / math.sqrt(D_MODEL)
        return {'in_features': jax.random.normal(k1, (2, 256, D_MODEL), dtype=jnp.float32), 'q_proj': jax.random.normal(k2, (D_MODEL, D_MODEL), dtype=jnp.float32) * s, 'k_proj': jax.random.normal(k3, (D_MODEL, D_MODEL), dtype=jnp.float32) * s, 'v_proj': jax.random.normal(k4, (D_MODEL, D_MODEL), dtype=jnp.float32) * s, 'o_proj': jax.random.normal(k5, (D_MODEL, D_MODEL), dtype=jnp.float32) * s}
    _L0_attn_all = _L0_attn_setup()
    _L0_attn_in = {k: v for k, v in _L0_attn_all.items() if k in ('q_proj', 'k_proj', 'v_proj', 'o_proj')}
    del _L0_attn_all

    def _L0_xattn_setup():
        import jax, jax.numpy as jnp
        import numpy as np
        B, S, D = (4, 512, 256)
        E = 4
        F = 1024 // E
        VOCAB = 12500
        key = jax.random.key(seed)
        k1, k2, k3, k4, k5 = jax.random.split(key, 5)
        hidden_states = jax.random.normal(k1, (B, S, D), dtype=jnp.float32)
        token_ids = jax.random.randint(k2, (B, S), 0, VOCAB, dtype=jnp.int64)
        Wg = jax.random.normal(k3, (E, F, D), dtype=jnp.float32) * 0.02
        Wu = jax.random.normal(k4, (E, F, D), dtype=jnp.float32) * 0.02
        Wd = jax.random.normal(k5, (E, D, F), dtype=jnp.float32) * 0.02
        return {'hidden_states': hidden_states, 'token_ids': token_ids, 'Wg': Wg, 'Wu': Wu, 'Wd': Wd}
    _L0_xattn_all = _L0_xattn_setup()
    _L0_xattn_in = {k: v for k, v in _L0_xattn_all.items() if k in ()}
    del _L0_xattn_all

    def _L0_ffn_setup():
        import jax, jax.numpy as jnp
        import numpy as np
        D_MODEL = 256
        D_FF = 1024
        N_EXPERTS = 4
        B, S = (2, 256)
        key = jax.random.key(seed)
        ks = jax.random.split(key, 6)
        scale = 0.02
        return {'hidden_states': jax.random.normal(ks[0], (B, S, D_MODEL), dtype=jnp.float32), 'Wr': jax.random.normal(ks[1], (D_MODEL, N_EXPERTS), dtype=jnp.float32) * scale, 'br': jnp.zeros((N_EXPERTS,), dtype=jnp.float32), 'Wg': jax.random.normal(ks[2], (N_EXPERTS, D_MODEL, D_FF), dtype=jnp.float32) * scale, 'Wu': jax.random.normal(ks[3], (N_EXPERTS, D_MODEL, D_FF), dtype=jnp.float32) * scale, 'Wd': jax.random.normal(ks[4], (N_EXPERTS, D_FF, D_MODEL), dtype=jnp.float32) * scale}
    _L0_ffn_all = _L0_ffn_setup()
    _L0_ffn_in = {k: v for k, v in _L0_ffn_all.items() if k in ('Wr', 'br', 'Wg', 'Wu', 'Wd')}
    del _L0_ffn_all
    return {'x': x, 'itok_BxS_13_99985': itok_BxS_13_99985, 'ctx_2048': ctx_2048, 'L0_attn_q_proj': _L0_attn_in['q_proj'], 'L0_attn_k_proj': _L0_attn_in['k_proj'], 'L0_attn_v_proj': _L0_attn_in['v_proj'], 'L0_attn_o_proj': _L0_attn_in['o_proj'], 'L0_ffn_Wr': _L0_ffn_in['Wr'], 'L0_ffn_br': _L0_ffn_in['br'], 'L0_ffn_Wg': _L0_ffn_in['Wg'], 'L0_ffn_Wu': _L0_ffn_in['Wu'], 'L0_ffn_Wd': _L0_ffn_in['Wd']}

def reference(x, itok_BxS_13_99985, ctx_2048, L0_attn_q_proj, L0_attn_k_proj, L0_attn_v_proj, L0_attn_o_proj, L0_ffn_Wr, L0_ffn_br, L0_ffn_Wg, L0_ffn_Wu, L0_ffn_Wd):
    import jax
    import jax.numpy as jnp

    def _L0_attn_ref(in_features, q_proj, k_proj, v_proj, o_proj):
        import math
        import jax, jax.numpy as jnp
        import numpy as np
        D_MODEL = 256
        NUM_HEADS = 16
        B, S, D = in_features.shape
        H = NUM_HEADS
        d_k = D // H

        def proj(W):
            return (in_features @ W.T).reshape(B, S, H, d_k).transpose(0, 2, 1, 3)
        Q, K, V = (proj(q_proj), proj(k_proj), proj(v_proj))
        scores = jnp.einsum('bhqd,bhkd->bhqk', Q, K) / math.sqrt(d_k)
        causal = jnp.triu(jnp.ones((S, S), dtype=bool), k=1)
        scores = jnp.where(causal, -jnp.inf, scores)
        attn = jax.nn.softmax(scores, axis=-1)
        out = jnp.einsum('bhqk,bhkd->bhqd', attn, V)
        out = out.transpose(0, 2, 1, 3).reshape(B, S, D)
        return out @ o_proj.T

    def _L0_xattn_ref(hidden_states, token_ids, Wg, Wu, Wd):
        import jax, jax.numpy as jnp
        import numpy as np
        B, S, D = (4, 512, 256)
        E = 4
        F = 1024 // E
        VOCAB = 12500
        tokens_per_expert = VOCAB // E
        tid = jnp.clip(token_ids, 0, VOCAB - 1)
        expert_ids = jnp.minimum(tid // tokens_per_expert, E - 1)
        out = jnp.zeros_like(hidden_states)
        for e in range(E):
            g = jax.nn.silu(jnp.einsum('bsd,fd->bsf', hidden_states, Wg[e]))
            u = jnp.einsum('bsd,fd->bsf', hidden_states, Wu[e])
            y = jnp.einsum('bsf,df->bsd', g * u, Wd[e])
            out = jnp.where((expert_ids == e)[..., None], y, out)
        return out

    def _L0_ffn_ref(hidden_states, Wr, br, Wg, Wu, Wd):
        import jax, jax.numpy as jnp
        import numpy as np
        D_MODEL = 256
        D_FF = 1024
        N_EXPERTS = 4
        B, S = (2, 256)
        b, s, d = hidden_states.shape
        x = hidden_states.reshape(-1, d)
        logits = x @ Wr + br
        probs = jax.nn.softmax(logits, axis=-1)
        top_w, top_idx = jax.lax.top_k(probs, 1)
        g = jnp.einsum('td,edf->tef', x, Wg)
        u = jnp.einsum('td,edf->tef', x, Wu)
        h = jax.nn.silu(g) * u
        y = jnp.einsum('tef,efd->ted', h, Wd)
        sel = jnp.take_along_axis(y, top_idx[:, :, None], axis=1)[:, 0]
        out = sel * top_w
        return out.reshape(b, s, d)
    x = _layernorm(x + _L0_attn_ref(x, L0_attn_q_proj, L0_attn_k_proj, L0_attn_v_proj, L0_attn_o_proj), axis=-1)
    x = _layernorm(x + _L0_xattn_ref(x, itok_BxS_13_99985, ctx_2048, ctx_2048, ctx_2048), axis=-1)
    x = _layernorm(x + _L0_ffn_ref(x, L0_ffn_Wr, L0_ffn_br, L0_ffn_Wg, L0_ffn_Wu, L0_ffn_Wd), axis=-1)
    return x

_drawn_inputs = setup_inputs


def setup_inputs(seed=0):
    import zlib

    import numpy as np

    out = dict(_drawn_inputs(seed))
    spreads = {'L0_ffn_br': (0.0, 0.8)}
    factors = {'L0_ffn_Wr': 5.642, 'L0_ffn_Wg': 4.766, 'L0_ffn_Wu': 4.685, 'L0_ffn_Wd': 4.697}
    for name, (base, spread) in spreads.items():
        noise = np.random.default_rng([zlib.crc32(name.encode()), seed]).standard_normal(out[name].shape)
        drawn = base * np.exp(spread * noise) if base else spread * noise
        out[name] = jnp.asarray(drawn.astype(out[name].dtype))
    for name, factor in factors.items():
        out[name] = (out[name] * factor).astype(out[name].dtype)
    return out
```

```python
from contextlib import ExitStack

import numpy as np
import concourse.bass as bass
import concourse.mybir as mybir

F32, F16, BF16, I32 = mybir.dt.float32, mybir.dt.float16, mybir.dt.bfloat16, mybir.dt.int32
ALU, ACT, AX = mybir.AluOpType, mybir.ActivationFunctionType, mybir.AxisListType

P = 128
B, S, D = 4, 256, 256
H, DK = 16, 16
E, F = 4, 1024
T = B * S
NT = T // P
TB = S // P
NK = D // P
NF = F // P
NS = NT + E - 1
G = 4
NG = H // G
PAIRS = H // 2
VT = 3 * TB
SLOT = 64
ROW = D + 2
VOCAB_PART = 12500 // E
W_SCALE = 256.0
EPS = 1e-5
NEG = -3.0e38
PAD_TOKEN = 4096.0
CH = 1024
NCTX = E * NK * D // CH
EW = 2 * NK * F + NF * D
NCH = NCTX + E * EW // CH
RING = 4
DOWN = 2 * NK * F


def build(nc, x_tok, xT, ids, wqkvT, woT, ctxT, Wr, br, Wf, out):
    ctx = ExitStack()
    with ctx:
        def sb(name, shape, dt):
            return ctx.enter_context(nc.sbuf_tensor(name, shape, dt))

        def sem(name):
            return ctx.enter_context(nc.semaphore(name))

        wf_hi = sb("wf_hi", [P, E * EW], F16)
        wf_lo = sb("wf_lo", [P, E * EW], F16)
        ring = sb("ring", [P, RING * CH], F32)
        xT_hi = sb("xT_hi", [P, NK * T], F16)
        xT_lo = sb("xT_lo", [P, NK * T], F16)
        ctx_hi, ctx_lo = xT_hi, xT_lo
        X1 = sb("X1", [P, NT, ROW], F32)
        identF = sb("identF", [P, P], F32)
        identH = sb("identH", [P, P], F16)
        identB = sb("identB", [P, P], BF16)
        before = sb("before", [P, P], F16)
        ones = sb("ones", [P, P], F16)
        maskS = sb("maskS", [P, G, P], BF16)
        maskT = sb("maskT", [P, G, P], BF16)
        fill = sb("fill", [P, ROW], F32)
        steps = sb("steps", [P, NT], F32)
        tiles = sb("tiles", [P, NS], F32)
        reset = sb("reset", [P, E, NS], F32)
        minus_half = sb("minus_half", [P, NS], F32)
        ids_sb = sb("ids_sb", [P, NT], I32)
        ge = sb("ge", [P, E + 1, NT], F32)
        oh = sb("oh", [P, NS, E], F16)
        cnt = sb("cnt", [P, E, NS], F32)
        run = sb("run", [P, E, NS], F32)
        over = sb("over", [P, E, NT], F32)
        nt_e = sb("nt_e", [P, E], F32)
        end_e = sb("end_e", [P, E], F32)
        base_e = sb("base_e", [P, E], F32)
        where = sb("where", [P, NS, E], F32)
        pos = sb("pos", [P, NS], F32)
        pos_i = sb("pos_i", [P, NS], I32)
        tile_ge = sb("tile_ge", [P, NS, E - 1], F32)
        tile_e = sb("tile_e", [P, NS], F32)
        tile_i = sb("tile_i", [P, 2, NS], I32)
        wr_sb = sb("wr_sb", [P, NK, E], F32)
        br_sb = sb("br_sb", [P, E], F32)
        lg = sb("lg", [P, NS, E], F32)
        ex = sb("ex", [P, NS, E], F32)
        taken = sb("taken", [P, NS], F32)
        ohf = sb("ohf", [P, NS, E], F32)
        top = sb("top", [P, NS], F32)
        valid = sb("valid", [P, NS], F32)
        out_i = sb("out_i", [P, NS], I32)
        st = sb("st", [P, 2, 6], F32)
        mv = sb("mv", [P, 2, 2], F32)
        veps = sb("veps", [P, 2], F32)
        rstd = sb("rstd", [P, 2], F32)

        ARENA = 72 * 1024
        arena = sb("arena", [P, ARENA // 4], F32)
        at = [0]

        def carve(shape, dt):
            n = int(np.prod(shape))
            size = n * (4 if dt in (F32, I32) else 2)
            a = arena[:, at[0] // 4:(at[0] + size) // 4]
            at[0] += size
            assert at[0] <= ARENA, at[0]
            if dt != F32:
                a = a.bitcast(dt)
            names = "abcd"[:len(shape)]
            return a.rearrange(f"p ({' '.join(names)}) -> p {' '.join(names)}", **dict(zip(names, shape)))

        wqkv_hi = carve([NK, 3 * D], F16)
        wqkv_lo = carve([NK, 3 * D], F16)
        wo_hi = carve([NK, D], F16)
        wo_lo = carve([NK, D], F16)
        QT = [carve([H, S], F16) for _ in range(2)]
        KT = [carve([PAIRS, S], F16) for _ in range(2)]
        Qs = [carve([H, 4, DK], F16) for _ in range(2)]
        Ks = [carve([H, 4, DK], F16) for _ in range(2)]
        Vs = carve([VT, H, 2 * DK + 2], F16)
        Pf = carve([3, G * P], F32)
        Ph = [carve([3, G * P], F16) for _ in range(2)]
        Pl = [carve([3, G * P], F16) for _ in range(2)]
        On = carve([TB, D], F32)
        Oa = carve([TB * G, DK], F32)
        Or = carve([TB * G], F32)
        OT_hi = carve([TB, NK, P], F16)
        OT_lo = carve([TB, NK, P], F16)
        Mx = carve([TB, 2, PAIRS], F32)
        Mn = carve([TB * 2, 2, PAIRS], F16)
        mT = carve([S], F16)
        used_attention = at[0]
        at[0] = 0
        XS = carve([NS, ROW], F32)
        X2 = carve([NS, ROW], F32)
        a_hi = [carve([NK, P], F16) for _ in range(2)]
        a_lo = [carve([NK, P], F16) for _ in range(2)]
        sg = carve([F], F32)
        hh = carve([F], F32)
        h_hi = carve([NF, P], F16)
        h_lo = carve([NF, P], F16)
        x2T = carve([NK, P], F32)
        res = [carve([D], F32) for _ in range(2)]
        fin = [carve([D], F32) for _ in range(2)]

        ps = ctx.enter_context(nc.psum_tensor("ps", [P, 8, 512], F32))

        def ps16(k, rows=slice(0, P)):
            return ps[rows, k, :].bitcast(F16)

        sorted2 = nc.dram_tensor("sorted2", [NS * P, ROW], F32, kind="Internal").ap()
        sorted3 = nc.dram_tensor("sorted3", [NS * P, ROW], F32, kind="Internal").ap()

        in_ids, in_wqkv, in_wo, in_xtok, in_r = (sem(n) for n in ("in_ids", "in_wqkv", "in_wo", "in_xtok", "in_r"))
        in_xT = [sem(f"in_xT{b}") for b in range(B)]
        in_ch = [sem(f"in_ch{r}") for r in range(RING)]
        const_z, const_r, fillrow = sem("const_z"), sem("const_r"), sem("fillrow")
        filled = sem("filled")
        w_hi, w_lo, x_hi, x_lo, c_hi, c_lo = (sem(n) for n in ("w_hi", "w_lo", "x_hi", "x_lo", "c_hi", "c_lo"))
        proj_qk, proj_v, qkv_hi, qkv_lo = (sem(n) for n in ("proj_qk", "proj_v", "qkv_hi", "qkv_lo"))
        kT_rdy, qT_rdy, kT_done, q_even, q_odd = (sem(n) for n in ("kT_rdy", "qT_rdy", "kT_done", "q_even", "q_odd"))
        s_rdy, maxed, m_neg, mT_rdy, mT_done, m_row = (sem(n) for n in (
            "s_rdy", "maxed", "m_neg", "mT_rdy", "mT_done", "m_row"))
        st_rdy, exped, p_lo, av_rdy, o_read, o_norm = (sem(n) for n in (
            "st_rdy", "exped", "p_lo", "av_rdy", "o_read", "o_norm"))
        oT_rdy, oT_hi, oT_lo, wo_rdy, res1, mv1, rs1, x1_rdy = (sem(n) for n in (
            "oT_rdy", "oT_hi", "oT_lo", "wo_rdy", "res1", "mv1", "rs1", "x1_rdy"))
        link_v, link_g = sem("link_v"), sem("link_g")
        oh_rdy, cnt_rdy, pos_rdy, tile_rdy = (sem(n) for n in ("oh_rdy", "cnt_rdy", "pos_rdy", "tile_rdy"))
        scat2, scat3 = sem("scat2"), sem("scat3")
        scat_out = [sem(f"scat_out{i}") for i in range(2)]
        ld2 = [sem(f"ld2_{i}") for i in range(NS)]
        ld3 = [sem(f"ld3_{i}") for i in range(NS)]
        a2T, a2hi, a2lo, z_rdy, sg2, h2, h2T, h2hi, h2lo, y2, r2, mv2, rs2, x2_rdy, x2T_rdy, x2T_sb, lg_rdy = (
            sem(n) for n in ("a2T", "a2hi", "a2lo", "z_rdy", "sg2", "h2", "h2T", "h2hi", "h2lo", "y2", "r2", "mv2",
                             "rs2", "x2_rdy", "x2T_rdy", "x2T_sb", "lg_rdy"))
        lg_sb, ex_rdy, w_rdy = sem("lg_sb"), sem("ex_rdy"), sem("w_rdy")
        a3T, a3hi, a3lo, gu_a, gu_b, sg3, h3, h3T, h3hi, h3lo, y3, r3, mv3, rs3, f3 = (
            sem(n) for n in ("a3T", "a3hi", "a3lo", "gu_a", "gu_b", "sg3", "h3", "h3T", "h3hi", "h3lo", "y3",
                             "r3", "mv3", "rs3", "f3"))

        def chunk_dst(c, hi):
            if c < NCTX:
                return (ctx_hi if hi else ctx_lo)[:, c * CH:(c + 1) * CH]
            c -= NCTX
            return (wf_hi if hi else wf_lo)[:, c * CH:(c + 1) * CH]

        def chunk_src(c):
            return ring[:, (c % RING) * CH:(c % RING + 1) * CH]

        xT_st = ring[:, 0:NK * T].rearrange("p (k t) -> p k t", k=NK)
        wqkv_st = ring[:, NK * T:NK * (T + 3 * D)].rearrange("p (k n) -> p k n", k=NK)
        wo_st = ring[:, NK * (T + 3 * D):NK * (T + 4 * D)].rearrange("p (k n) -> p k n", k=NK)
        xTv_hi = xT_hi[:, :].rearrange("p (k t) -> p k t", k=NK)
        xTv_lo = xT_lo[:, :].rearrange("p (k t) -> p k t", k=NK)

        def chunks_of_step(b, g):
            n = b * NG + g
            return [n] if n < ATT_CHUNKS else []

        ORDER = list(range(NCTX, NCH))
        ATT_CHUNKS = 14
        CTX_AT = 8
        ORDER = ORDER[:CTX_AT] + list(range(NCTX)) + ORDER[CTX_AT:]

        def slot_of(n):
            return n % RING

        def ring_of(n):
            return ring[:, slot_of(n) * CH:(slot_of(n) + 1) * CH]

        block = ctx.enter_context(nc.Block())

        @block.sync
        def _(sp):
            sp.dma_start(ids_sb[:, :], ids).then_inc(in_ids, 16)
            sp.dma_start(wqkv_st, wqkvT).then_inc(in_wqkv, 16)
            for b in range(B):
                sp.dma_start(xT_st[:, :, b * S:(b + 1) * S], xT[:, :, b * S:(b + 1) * S]).then_inc(in_xT[b], 16)
            sp.dma_start(wo_st, woT).then_inc(in_wo, 16)
            sp.dma_start(X1[:, :, 0:D], x_tok).then_inc(in_xtok, 16)
            sp.dma_start(wr_sb[:, :, :], Wr).then_inc(in_r, 16)
            sp.dma_start(br_sb[:, :], br.partition_broadcast(P)).then_inc(in_r, 16)
            sp.wait_ge(fillrow, 1)
            for scratch in (sorted2, sorted3):
                sp.dma_start(scratch.rearrange("(n p) d -> p n d", p=P),
                             fill[:, :].unsqueeze(1).to_broadcast([P, NS, ROW])).then_inc(filled, 16)

            def load(n):
                if n >= NCH:
                    return
                if n < RING:
                    if slot_of(n) * CH < NK * T:
                        sp.wait_ge(x_lo, B)
                    else:
                        sp.wait_ge(w_lo, 2)
                else:
                    sp.wait_ge(c_lo, n - RING + 1)
                c = ORDER[n]
                src = (ctxT[:, c * CH:(c + 1) * CH] if c < NCTX else
                       Wf[:, (c - NCTX) * CH:(c - NCTX + 1) * CH])
                sp.dma_start(ring_of(n), src).then_inc(in_ch[slot_of(n)], 16)

            def max_rows(b):
                sp.wait_ge(mT_done, b + 1)
                for par in range(2):
                    for part in range(2):
                        row = par * SLOT + 3 * DK + part
                        src = (par * 2 + part) * PAIRS
                        sp.dma_start(QT[b % 2][row:row + 1, par::2, :],
                                     mT[src:src + PAIRS, :]).then_inc(m_row, 16)

            max_rows(0)
            n = 0
            for b in range(B):
                while n < RING + min(NG * (b + 1), ATT_CHUNKS):
                    load(n)
                    n += 1
                if b + 1 < B:
                    max_rows(b + 1)
            sp.wait_ge(scat2, 16 * NT)
            for i in range(NS):
                sp.dma_start(XS[:, i, :], sorted2[i * P:(i + 1) * P, :]).then_inc(ld2[i], 16)
            while n < NCH:
                load(n)
                n += 1
            sp.wait_ge(scat3, 16 * NS)
            for i in range(NS):
                sp.dma_start(XS[:, i, :], sorted3[i * P:(i + 1) * P, :]).then_inc(ld3[i], 16)

        @block.gpsimd
        def _(pool):
            g = nc.gpsimd
            links = [0]

            def link(ins):
                links[0] += 1
                ins.then_inc(link_g, 1)
                pool.wait_ge(link_g, links[0])

            g.iota(tiles[:, :], pattern=[[1, NS]], base=0, channel_multiplier=0,
                   allow_small_or_imprecise_dtypes=True)
            g.iota(steps[:, :], pattern=[[P, NT]], base=0, channel_multiplier=0,
                   allow_small_or_imprecise_dtypes=True)
            g.memset(reset[:, :, :], 1.0)
            g.memset(ones[:, :], 1.0)
            link(g.memset(before[:, :], 0.0))
            g.memset(reset[:, :, 0:1], 0.0)
            g.affine_select(out=before[:, :], in_=before[:, :], compare_op=ALU.is_ge, fill=1.0,
                            base=0, pattern=[[-1, P]], channel_multiplier=1).then_inc(const_r, 1)
            for j in range(2):
                g.memset(Qs[j][:, :, 3, :], 0.0)
                g.memset(Ks[j][:, :, 3, :], 0.0)
            g.memset(Vs[:, :, :, 2 * DK:2 * DK + 2], 1.0)
            for m in (identF, identH, identB):
                g.memset(m[:, :], 0.0)
            g.memset(maskS[:, :, :], 0.0)
            link(g.memset(maskT[:, :, :], 0.0))
            for j in range(2):
                g.memset(Ks[j][:, :, 3, 0:2], 1.0)
            for m in (identF, identH, identB):
                g.affine_select(out=m[:, :], in_=m[:, :], compare_op=ALU.not_equal, fill=1.0,
                                base=0, pattern=[[-1, P]], channel_multiplier=1)
            g.affine_select(out=maskS[:, :, :], in_=maskS[:, :, :], compare_op=ALU.is_ge, fill=NEG,
                            base=0, pattern=[[0, G], [-1, P]], channel_multiplier=1)
            link(g.affine_select(out=maskT[:, :, :], in_=maskT[:, :, :], compare_op=ALU.is_ge, fill=NEG,
                                 base=0, pattern=[[0, G], [1, P]], channel_multiplier=-1))
            for q in QT:
                link(g.memset(q[SLOT:P, 0::2, :], 0.0))
                link(g.memset(q[0:SLOT, 1::2, :], 0.0))
            g.memset(fill[:, :], 0.0).then_inc(const_z, 1)
            pool.wait_ge(const_z, 1)
            g.memset(fill[:, D:D + 1], PAD_TOKEN).then_inc(fillrow, 1)
            g.memset(minus_half[:, :], -0.5)
            g.memset(X1[:, :, D + 1:D + 2], 0.0)
            link(g.iota(X1[:, :, D], pattern=[[P, NT]], base=0, channel_multiplier=1,
                        allow_small_or_imprecise_dtypes=True))

            def inv_std(var, n, out_sem):
                link(g.tensor_scalar(veps[:, 0:n], var, EPS, None, ALU.add))
                g.tensor_tensor(rstd[:, 0:n], veps[:, 0:n], minus_half[:, 0:n], ALU.pow).then_inc(out_sem, 1)

            pool.wait_ge(filled, 32)
            pool.wait_ge(pos_rdy, 1)
            for b in range(B):
                pool.wait_ge(mv1, TB * (b + 1))
                inv_std(mv[:, :, 1], TB, rs1)
                for j in range(TB):
                    tt = TB * b + j
                    pool.wait_ge(x1_rdy, tt + 1)
                    g.indirect_dma_start(sorted2[:, :], bass.IndirectOffsetOnAxis(ap=pos_i[:, tt:tt + 1], axis=0),
                                         X1[:, tt, :], None, bounds_check=NS * P - 1,
                                         oob_is_err=False).then_inc(scat2, 16)
            for i in range(NS):
                pool.wait_ge(mv2, i + 1)
                link(g.tensor_scalar(veps[:, i % 2:i % 2 + 1], mv[:, i % 2, 1:2], EPS, None, ALU.add))
                g.tensor_tensor(rstd[:, i % 2:i % 2 + 1], veps[:, i % 2:i % 2 + 1], minus_half[:, 0:1],
                                ALU.pow).then_inc(rs2, 1)
            pool.wait_ge(pos_rdy, 2)
            pool.wait_ge(w_rdy, 1)
            for i in range(NS):
                g.indirect_dma_start(sorted3[:, :], bass.IndirectOffsetOnAxis(ap=pos_i[:, i:i + 1], axis=0),
                                     X2[:, i, :], None, bounds_check=NS * P - 1,
                                     oob_is_err=False).then_inc(scat3, 16)
            for i in range(NS):
                pool.wait_ge(mv3, i + 1)
                link(g.tensor_scalar(veps[:, i % 2:i % 2 + 1], mv[:, i % 2, 1:2], EPS, None, ALU.add))
                g.tensor_tensor(rstd[:, i % 2:i % 2 + 1], veps[:, i % 2:i % 2 + 1], minus_half[:, 0:1],
                                ALU.pow).then_inc(rs3, 1)
                pool.wait_ge(f3, i + 1)
                g.indirect_dma_start(out, bass.IndirectOffsetOnAxis(ap=out_i[:, i:i + 1], axis=0),
                                     fin[i % 2], None, bounds_check=T - 1,
                                     oob_is_err=False).then_inc(scat_out[i % 2], 16)
            for i in range(2):
                pool.wait_ge(scat_out[i], 16 * ((NS + 1 - i) // 2))

        @block.scalar
        def _(act):
            a = nc.scalar

            def split_hi(n):
                act.wait_ge(in_ch[slot_of(n)], 16 * (n // RING + 1) if n >= RING else 16)
                a.activation(chunk_dst(ORDER[n], True), ring_of(n), ACT.Copy, scale=W_SCALE).then_inc(c_hi, 1)

            def x_split(b):
                act.wait_ge(in_xT[b], 16)
                a.activation(xTv_hi[:, :, b * S:(b + 1) * S], xT_st[:, :, b * S:(b + 1) * S],
                             ACT.Copy).then_inc(x_hi, 1)

            act.wait_ge(in_wqkv, 16)
            a.activation(wqkv_hi, wqkv_st, ACT.Copy, scale=W_SCALE).then_inc(w_hi, 1)
            for b in range(B):
                x_split(b)
            act.wait_ge(in_wo, 16)
            a.activation(wo_hi, wo_st, ACT.Copy, scale=W_SCALE).then_inc(w_hi, 1)

            def project(b):
                for j in range(TB):
                    tt = TB * b + j
                    act.wait_ge(proj_qk, tt + 1)
                    if tt >= 2:
                        act.wait_ge(kT_rdy, tt - 1)
                        act.wait_ge(qT_rdy, tt - 1)
                    else:
                        act.wait_ge(const_z, 1)
                    qk = ps[:, 2 * j, :].rearrange("p (s h c) -> p s h c", s=2, h=H)
                    rep = [P, H, 2, DK]
                    a.activation(Ks[j][:, :, 0:3:2, :], qk[:, 1].unsqueeze(2).to_broadcast(rep), ACT.Copy,
                                 scale=1 / W_SCALE).then_inc(qkv_hi, 1)
                    a.activation(Qs[j][:, :, 0:2, :], qk[:, 0].unsqueeze(2).to_broadcast(rep), ACT.Copy,
                                 scale=1 / W_SCALE).then_inc(qkv_hi, 1)
                    act.wait_ge(proj_v, tt + 1)
                    if b >= 3:
                        act.wait_ge(av_rdy, NG * (b - 2))
                    a.activation(Vs[:, tt % VT, :, 0:DK],
                                 ps[:, (1, 7)[j], 0:D].rearrange("p (h c) -> p h c", h=H), ACT.Copy,
                                 scale=1 / W_SCALE).then_inc(qkv_hi, 1)
                for j in range(TB):
                    tt = TB * b + j
                    act.wait_ge(qT_rdy, tt + 1)
                    a.activation(QT[b % 2][SLOT:P, 1::2, j * P:(j + 1) * P],
                                 ps16((1, 7)[j], slice(SLOT, P)).rearrange("p (h t) -> p h t", h=PAIRS),
                                 ACT.Copy).then_inc(q_odd, 1)

            def exps(b, g):
                n = NG * b + g
                act.wait_ge(st_rdy, n + 1)
                if n >= 2:
                    act.wait_ge(av_rdy, n - 1)
                a.activation(Ph[n % 2], ps[:, 3:6, :], ACT.Exp, scale=DK ** -0.5).then_inc(exped, 1)
                if n >= 1:
                    act.wait_ge(p_lo, n)
                a.activation(Pf, ps[:, 3:6, :], ACT.Exp, scale=DK ** -0.5).then_inc(exped, 1)

            project(0)
            project(1)
            n = 0
            for b in range(B):
                for g in range(NG):
                    exps(b, g)
                    if n < ATT_CHUNKS:
                        if n >= CTX_AT:
                            act.wait_ge(proj_v, NT)
                        split_hi(n)
                        n += 1
                if b + 2 < B:
                    project(b + 2)
                for j in range(TB):
                    tt = TB * b + j
                    act.wait_ge(oT_rdy, tt + 1)
                    if b >= 1:
                        act.wait_ge(wo_rdy, tt - 1)
                    a.activation(OT_hi[:, j], ps[:, 2 * j, 0:D].rearrange("p (k t) -> p k t", k=NK),
                                 ACT.Copy).then_inc(oT_hi, 1)

            for s in range(NS + 6):
                if n < NCH:
                    split_hi(n)
                    n += 1
                if s < NS:
                    act.wait_ge(a2T, s + 1)
                    if s >= 2:
                        act.wait_ge(z_rdy, s - 1)
                    a.activation(a_hi[s % 2], ps[:, s % 2, 0:D].rearrange("p (k t) -> p k t", k=NK),
                                 ACT.Copy).then_inc(a2hi, 1)
                i = s - 1
                if 0 <= i < NS:
                    act.wait_ge(z_rdy, i + 1)
                    if i >= 1:
                        act.wait_ge(h2, i)
                    a.activation(sg[:, 0:D], ps[:, 2, 0:D], ACT.Silu, scale=1 / W_SCALE).then_inc(sg2, 1)
                i = s - 2
                if 0 <= i < NS:
                    act.wait_ge(h2T, i + 1)
                    if i >= 1:
                        act.wait_ge(y2, i)
                    a.activation(h_hi[:, 0:NK], ps[:, 3, 0:D].rearrange("p (k t) -> p k t", k=NK),
                                 ACT.Copy).then_inc(h2hi, 1)
                i = s - 5
                if 0 <= i < NS:
                    act.wait_ge(x2T_rdy, i + 1)
                    if i >= 1:
                        act.wait_ge(lg_rdy, i)
                    a.activation(x2T, ps[:, 5, 0:D].rearrange("p (k t) -> p k t", k=NK),
                                 ACT.Copy).then_inc(x2T_sb, 1)
            while n < NCH:
                split_hi(n)
                n += 1
            act.wait_ge(lg_sb, 1)
            a.activation(ex[:, :, :], lg[:, :, :], ACT.Exp).then_inc(ex_rdy, 1)

            def x_hi3(i):
                act.wait_ge(a3T, i + 1)
                if i >= 2:
                    act.wait_ge(gu_b, i - 1)
                a.activation(a_hi[i % 2], ps[:, 6, 0:D].rearrange("p (k t) -> p k t", k=NK),
                             ACT.Copy).then_inc(a3hi, 1)

            def silu(i, half):
                act.wait_ge((gu_a, gu_b)[half], i + 1)
                if i >= 1:
                    act.wait_ge(h3, 2 * (i - 1) + half + 1)
                a.activation(sg[:, half * 512:(half + 1) * 512], ps[:, 2 * half, :], ACT.Silu,
                             scale=1 / W_SCALE).then_inc(sg3, 1)

            def h_hi3(i):
                act.wait_ge(h3T, i + 1)
                if i >= 1:
                    act.wait_ge(y3, i)
                a.activation(h_hi, ps[:, 4:6, :].rearrange("p c (k t) -> p (c k) t", t=P),
                             ACT.Copy).then_inc(h3hi, 1)

            x_hi3(0)
            for i in range(NS + 1):
                if i < NS:
                    silu(i, 0)
                if i >= 1:
                    h_hi3(i - 1)
                if i + 1 < NS:
                    x_hi3(i + 1)
                if i < NS:
                    silu(i, 1)

        @block.vector
        def _(dve):
            v = nc.vector
            links = [0]

            def link(ins):
                links[0] += 1
                ins.then_inc(link_v, 1)
                dve.wait_ge(link_v, links[0])

            def split_lo(n):
                dve.wait_ge(c_hi, n + 1)
                v.scalar_tensor_tensor(out=chunk_dst(ORDER[n], False), in0=ring_of(n), scalar=W_SCALE,
                                       in1=chunk_dst(ORDER[n], True), op0=ALU.mult,
                                       op1=ALU.subtract).then_inc(c_lo, 1)

            def slots(n, which):
                dve.wait_ge(cnt_rdy, which + 1)
                link(v.tensor_copy(cnt[:, :, 0:n],
                                   ps[:, 7, 256:256 + n * E].rearrange("p (i e) -> p e i", e=E)))
                if n == NS:
                    link(v.tensor_tensor_scan(run[:, :, :].rearrange("p e i -> p (e i)"),
                                              reset[:, :, :].rearrange("p e i -> p (e i)"),
                                              cnt[:, :, :].rearrange("p e i -> p (e i)"), 0.0, ALU.mult, ALU.add))
                else:
                    for e in range(E):
                        ins = v.tensor_tensor_scan(run[:, e, 0:n], reset[:, e, 0:n], cnt[:, e, 0:n], 0.0,
                                                   ALU.mult, ALU.add)
                    link(ins)
                link(v.tensor_tensor(over[:, :, :], run[:, :, n - 1:n].to_broadcast([P, E, NT]),
                                     steps[:, :].unsqueeze(1).to_broadcast([P, E, NT]), ALU.is_gt))
                link(v.reduce_sum(nt_e[:, :], over[:, :, :], AX.X))
                link(v.tensor_tensor_scan(end_e[:, :], reset[:, 0, 1:1 + E], nt_e[:, :], 0.0, ALU.mult, ALU.add))
                link(v.tensor_tensor(base_e[:, :], end_e[:, :], nt_e[:, :], ALU.subtract))
                link(v.tensor_tensor(run[:, :, 0:n], run[:, :, 0:n], cnt[:, :, 0:n], ALU.subtract))
                link(v.scalar_tensor_tensor(out=run[:, :, 0:n], in0=base_e[:, :].unsqueeze(2).to_broadcast([P, E, n]),
                                            scalar=float(P), in1=run[:, :, 0:n], op0=ALU.mult, op1=ALU.add))
                link(v.tensor_tensor(where[:, 0:n, :], ps[:, 7, 0:n * E].rearrange("p (i e) -> p i e", e=E),
                                     run[:, :, 0:n].rearrange("p e i -> p i e"), ALU.add))
                link(v.tensor_tensor(where[:, 0:n, :], where[:, 0:n, :], oh[:, 0:n, :], ALU.mult))
                link(v.reduce_sum(pos[:, 0:n], where[:, 0:n, :], AX.X))
                if n == NS:
                    link(v.scalar_tensor_tensor(out=pos[:, :], in0=valid[:, :], scalar=-PAD_TOKEN, in1=pos[:, :],
                                                op0=ALU.mult, op1=ALU.add))
                    link(v.tensor_scalar(pos[:, :], pos[:, :], PAD_TOKEN, None, ALU.add))
                v.tensor_copy(pos_i[:, 0:n], pos[:, 0:n]).then_inc(pos_rdy, 1)
                link(v.tensor_tensor(tile_ge[:, :, :], tiles[:, :].unsqueeze(2).to_broadcast([P, NS, E - 1]),
                                     end_e[:, 0:E - 1].unsqueeze(1).to_broadcast([P, NS, E - 1]), ALU.is_ge))
                link(v.reduce_sum(tile_e[:, :], tile_ge[:, :, :], AX.X))
                v.tensor_copy(tile_i[:, which, :], tile_e[:, :]).then_inc(tile_rdy, 1)

            dve.wait_ge(in_ids, 16)
            v.memset(ge[:, 0, :], 1.0)
            v.memset(ge[:, E, :], 0.0)
            for e in range(1, E):
                ins = v.tensor_scalar(ge[:, e, :], ids_sb[:, :], float(e * VOCAB_PART), None, ALU.is_ge)
            link(ins)
            v.tensor_tensor(oh[:, 0:NT, :].rearrange("p i e -> p e i"), ge[:, 0:E, :], ge[:, 1:E + 1, :],
                            ALU.subtract).then_inc(oh_rdy, 1)
            dve.wait_ge(const_r, 1)
            slots(NT, 0)

            dve.wait_ge(w_hi, 1)
            v.scalar_tensor_tensor(out=wqkv_lo, in0=wqkv_st, scalar=W_SCALE, in1=wqkv_hi,
                                   op0=ALU.mult, op1=ALU.subtract).then_inc(w_lo, 1)
            for b in range(B):
                dve.wait_ge(x_hi, b + 1)
                t = slice(b * S, (b + 1) * S)
                v.tensor_tensor(xTv_lo[:, :, t], xT_st[:, :, t], xTv_hi[:, :, t], ALU.subtract).then_inc(x_lo, 1)
            dve.wait_ge(w_hi, 2)
            v.scalar_tensor_tensor(out=wo_lo, in0=wo_st, scalar=W_SCALE, in1=wo_hi,
                                   op0=ALU.mult, op1=ALU.subtract).then_inc(w_lo, 1)

            def project(b):
                for j in range(TB):
                    tt = TB * b + j
                    qk = ps[:, 2 * j, :].rearrange("p (s h c) -> p s h c", s=2, h=H)
                    vv = ps[:, (1, 7)[j], 0:D].rearrange("p (h c) -> p h c", h=H)
                    for n, (lo, src, hi) in enumerate((
                            (Ks[j][:, :, 1, :], qk[:, 1], Ks[j][:, :, 0, :]),
                            (Qs[j][:, :, 2, :], qk[:, 0], Qs[j][:, :, 0, :]),
                            (Vs[:, tt % VT, :, DK:2 * DK], vv, Vs[:, tt % VT, :, 0:DK]))):
                        dve.wait_ge(qkv_hi, 3 * tt + (2, 2, 3)[n])
                        v.scalar_tensor_tensor(out=lo, in0=src, scalar=1 / W_SCALE, in1=hi,
                                               op0=ALU.mult, op1=ALU.subtract).then_inc(qkv_lo, 1)
                for j in range(TB):
                    tt = TB * b + j
                    dve.wait_ge(kT_rdy, tt + 1)
                    v.tensor_copy(KT[b % 2][:, :, j * P:(j + 1) * P],
                                  ps16(2 * j).rearrange("p (h t) -> p h t", h=PAIRS)).then_inc(kT_done, 1)
                    dve.wait_ge(qT_rdy, tt + 1)
                    v.tensor_copy(QT[b % 2][0:SLOT, 0::2, j * P:(j + 1) * P],
                                  ps16((1, 7)[j], slice(0, SLOT)).rearrange("p (h t) -> p h t", h=PAIRS)
                                  ).then_inc(q_even, 1)

            def maxima(b, g):
                n = NG * b + g
                dst = Mx[:, :, :, 2 * g:2 * g + 2].rearrange("p t r a -> p t a r")
                if g == 0 and b >= 1:
                    dve.wait_ge(m_neg, b)
                dve.wait_ge(s_rdy, 2 * n + 1)
                v.tensor_reduce(dst[:, 0], ps[:, 0, :].rearrange("p (a r k) -> p a r k", a=2, r=2),
                                AX.X, ALU.max).then_inc(maxed, 1)
                dve.wait_ge(s_rdy, 2 * n + 2)
                v.tensor_reduce(dst[:, 1].rearrange("p a r -> p a r"),
                                ps[:, 1:3, :].rearrange("p c (a r k) -> p (a r) c k", a=2, r=2),
                                AX.XY, ALU.max).then_inc(maxed, 1)

            def negate(b):
                m = Mx.rearrange("p t r a -> p (t r) a")
                dve.wait_ge(maxed, 2 * NG * (b + 1))
                if b >= 1:
                    dve.wait_ge(mT_rdy, b)
                link(v.tensor_scalar(Mn[:, :, 0, :], m, -1.0, None, ALU.mult))
                v.scalar_tensor_tensor(out=Mn[:, :, 1, :], in0=m, scalar=-1.0, in1=Mn[:, :, 0, :],
                                       op0=ALU.mult, op1=ALU.subtract).then_inc(m_neg, 1)
                dve.wait_ge(mT_rdy, b + 1)
                if b >= 1:
                    dve.wait_ge(m_row, 64 * b)
                v.tensor_copy(mT[0:4 * PAIRS, :], ps16(7, slice(0, 4 * PAIRS))[:, 0:S]).then_inc(mT_done, 1)

            def p_low(b, g):
                n = NG * b + g
                dve.wait_ge(exped, 2 * n + 2)
                if n >= 2:
                    dve.wait_ge(av_rdy, n - 1)
                v.tensor_tensor(Pl[n % 2], Pf, Ph[n % 2], ALU.subtract).then_inc(p_lo, 1)

            def outputs(b, g):
                n = NG * b + g
                o = ps[:, 6, 0:TB * G * (2 * DK + 1)].rearrange("p (a c) -> p a c", c=2 * DK + 1)
                dve.wait_ge(av_rdy, n + 1)
                if n >= 1:
                    dve.wait_ge(o_norm, n)
                v.reciprocal(Or, o[:, :, 2 * DK])
                v.tensor_reduce(Oa, o[:, :, 0:2 * DK].rearrange("p a (s c) -> p a c s", s=2),
                                AX.X, ALU.add).then_inc(o_read, 1)
                dve.wait_ge(o_read, n + 1)
                if g == 0 and b >= 1:
                    dve.wait_ge(oT_rdy, TB * b)
                dst = On[:, :, g * G * DK:(g + 1) * G * DK]
                for q in range(TB):
                    ins = v.tensor_tensor(dst[:, q].rearrange("p (a c) -> p a c", c=DK), Oa[:, q * G:(q + 1) * G, :],
                                          Or[:, q * G:(q + 1) * G].unsqueeze(2).to_broadcast([P, G, DK]), ALU.mult)
                ins.then_inc(o_norm, 1)

            def residual(b):
                for j in range(TB):
                    tt = TB * b + j
                    dve.wait_ge(oT_hi, tt + 1)
                    v.tensor_tensor(OT_lo[:, j], ps[:, 2 * j, 0:D].rearrange("p (k t) -> p k t", k=NK),
                                    OT_hi[:, j], ALU.subtract).then_inc(oT_lo, 1)
                for j in range(TB):
                    tt = TB * b + j
                    dve.wait_ge(wo_rdy, tt + 1)
                    dve.wait_ge(in_xtok, 16)
                    v.scalar_tensor_tensor(out=X1[:, tt, 0:D], in0=ps[:, (1, 7)[j], 0:D], scalar=1 / W_SCALE,
                                           in1=X1[:, tt, 0:D], op0=ALU.mult, op1=ALU.add).then_inc(res1, 1)
                    dve.wait_ge(res1, tt + 1)
                    link(v.bn_stats(st[:, j, :], X1[:, tt, 0:D]))
                    if b >= 1 and j == 0:
                        dve.wait_ge(rs1, b)
                    v.bn_aggr(mv[:, j, :], st[:, j, :]).then_inc(mv1, 1)

            def norm1(b):
                dve.wait_ge(rs1, b + 1)
                for j in range(TB):
                    tt = TB * b + j
                    dve.wait_ge(mv1, tt + 1)
                    v.tensor_scalar(X1[:, tt, 0:D], X1[:, tt, 0:D], mv[:, j, 0:1], rstd[:, j:j + 1],
                                    ALU.subtract, ALU.mult).then_inc(x1_rdy, 1)

            project(0)
            for g in range(NG):
                maxima(0, g)
            project(1)
            negate(0)
            n = 0
            for b in range(B):
                for g in range(NG):
                    if b + 1 < B:
                        maxima(b + 1, g)
                    p_low(b, g)
                    if g >= 1:
                        outputs(b, g - 1)
                    if n < ATT_CHUNKS:
                        split_lo(n)
                        n += 1
                if b + 2 < B:
                    project(b + 2)
                outputs(b, NG - 1)
                if b + 1 < B:
                    negate(b + 1)
                residual(b)
                norm1(b)

            inv = 1 / W_SCALE
            for s in range(NS + 6):
                if s < NS:
                    dve.wait_ge(a2hi, s + 1)
                    v.tensor_tensor(a_lo[s % 2], ps[:, s % 2, 0:D].rearrange("p (k t) -> p k t", k=NK),
                                    a_hi[s % 2], ALU.subtract).then_inc(a2lo, 1)
                i = s - 1
                if 0 <= i < NS:
                    dve.wait_ge(sg2, i + 1)
                    if i >= 1:
                        dve.wait_ge(h2T, i)
                    v.scalar_tensor_tensor(out=hh[:, 0:D], in0=ps[:, 2, 0:D], scalar=inv, in1=sg[:, 0:D],
                                           op0=ALU.mult, op1=ALU.mult).then_inc(h2, 1)
                i = s - 2
                if 0 <= i < NS:
                    dve.wait_ge(h2hi, i + 1)
                    v.tensor_tensor(h_lo[:, 0:NK], ps[:, 3, 0:D].rearrange("p (k t) -> p k t", k=NK),
                                    h_hi[:, 0:NK], ALU.subtract).then_inc(h2lo, 1)
                i = s - 4
                if 0 <= i < NS:
                    dve.wait_ge(rs2, i + 1)
                    v.tensor_copy(X2[:, i, D:D + 1], XS[:, i, D:D + 1])
                    v.tensor_scalar(X2[:, i, 0:D], res[i % 2], mv[:, i % 2, 0:1], rstd[:, i % 2:i % 2 + 1],
                                    ALU.subtract, ALU.mult).then_inc(x2_rdy, 1)
                i = s - 3
                if 0 <= i < NS:
                    dve.wait_ge(y2, i + 1)
                    link(v.scalar_tensor_tensor(out=res[i % 2], in0=ps[:, 4, 0:D], scalar=inv, in1=XS[:, i, 0:D],
                                                op0=ALU.mult, op1=ALU.add))
                    r2_at = v.bn_stats(st[:, i % 2, :], res[i % 2])
                    link(r2_at)
                    v.bn_aggr(mv[:, i % 2, :], st[:, i % 2, :]).then_inc(mv2, 1)
                if n < NCH:
                    split_lo(n)
                    n += 1
            while n < NCH:
                split_lo(n)
                n += 1

            dve.wait_ge(lg_rdy, NS)
            dve.wait_ge(in_r, 32)
            dve.wait_ge(x2_rdy, NS)
            link(v.tensor_tensor(lg[:, :, :], ps[:, 6, 0:NS * E].rearrange("p (i e) -> p i e", e=E),
                                 br_sb[:, :].unsqueeze(1).to_broadcast([P, NS, E]), ALU.add))
            link(v.tensor_reduce(top[:, :], lg[:, :, :], AX.X, ALU.max))
            v.tensor_tensor(lg[:, :, :], lg[:, :, :], top[:, :].unsqueeze(2).to_broadcast([P, NS, E]),
                            ALU.subtract).then_inc(lg_sb, 1)
            link(v.tensor_scalar(valid[:, :], X2[:, :, D], float(T), None, ALU.is_lt))
            dve.wait_ge(lg_sb, 1)
            link(v.tensor_scalar(ohf[:, :, :], lg[:, :, :], 0.0, None, ALU.is_ge))
            link(v.tensor_copy(taken[:, :], ohf[:, :, 0]))
            for e in range(1, E):
                link(v.tensor_tensor(where[:, :, e], ohf[:, :, e], taken[:, :], ALU.max))
                link(v.tensor_tensor(ohf[:, :, e], ohf[:, :, e], taken[:, :], ALU.is_gt))
                link(v.tensor_copy(taken[:, :], where[:, :, e]))
            v.tensor_tensor(oh[:, :, :], ohf[:, :, :], valid[:, :].unsqueeze(2).to_broadcast([P, NS, E]),
                            ALU.mult).then_inc(oh_rdy, 1)
            dve.wait_ge(ex_rdy, 1)
            link(v.reduce_sum(top[:, :], ex[:, :, :], AX.X))
            link(v.reciprocal(top[:, :], top[:, :]))
            v.tensor_scalar(X2[:, :, D + 1], top[:, :], inv, None, ALU.mult).then_inc(w_rdy, 1)
            dve.wait_ge(oh_rdy, 2)
            dve.wait_ge(scat2, 16 * NT)
            slots(NS, 1)

            def x_lo3(i):
                dve.wait_ge(a3hi, i + 1)
                v.tensor_tensor(a_lo[i % 2], ps[:, 6, 0:D].rearrange("p (k t) -> p k t", k=NK),
                                a_hi[i % 2], ALU.subtract).then_inc(a3lo, 1)

            def gated(i, half):
                dve.wait_ge(sg3, 2 * i + half + 1)
                if i >= 1:
                    dve.wait_ge(h3T, i)
                v.scalar_tensor_tensor(out=hh[:, half * 512:(half + 1) * 512], in0=ps[:, 2 * half + 1, :], scalar=inv,
                                       in1=sg[:, half * 512:(half + 1) * 512],
                                       op0=ALU.mult, op1=ALU.mult).then_inc(h3, 1)

            def h_lo3(i):
                dve.wait_ge(h3hi, i + 1)
                v.tensor_tensor(h_lo, ps[:, 4:6, :].rearrange("p c (k t) -> p (c k) t", t=P), h_hi,
                                ALU.subtract).then_inc(h3lo, 1)

            def last_norm(i):
                dve.wait_ge(y3, i + 1)
                v.tensor_copy(out_i[:, i:i + 1], XS[:, i, D:D + 1])
                link(v.scalar_tensor_tensor(out=res[i % 2], in0=ps[:, 7, 0:D], scalar=XS[:, i, D + 1:D + 2],
                                            in1=XS[:, i, 0:D], op0=ALU.mult, op1=ALU.add))
                link(v.bn_stats(st[:, i % 2, :], res[i % 2]))
                v.bn_aggr(mv[:, i % 2, :], st[:, i % 2, :]).then_inc(mv3, 1)

            def finish(i):
                dve.wait_ge(rs3, i + 1)
                dve.wait_ge(mv3, i + 1)
                if i >= 2:
                    dve.wait_ge(scat_out[i % 2], 16 * (i // 2))
                v.tensor_scalar(fin[i % 2], res[i % 2], mv[:, i % 2, 0:1], rstd[:, i % 2:i % 2 + 1],
                                ALU.subtract, ALU.mult).then_inc(f3, 1)

            x_lo3(0)
            for i in range(NS + 1):
                if i < NS:
                    gated(i, 0)
                if i >= 1:
                    h_lo3(i - 1)
                if i + 1 < NS:
                    x_lo3(i + 1)
                if i < NS:
                    gated(i, 1)
                if i >= 1:
                    last_norm(i - 1)
                    finish(i - 1)

        @block.tensor
        def _(pe):
            t = nc.tensor

            def count(n):
                t.matmul(ps[:, 7, 0:n * E], before[:, :], oh[:, 0:n, :].rearrange("p i e -> p (i e)"),
                         start=True, stop=True)
                t.matmul(ps[:, 7, 256:256 + n * E], ones[:, :], oh[:, 0:n, :].rearrange("p i e -> p (i e)"),
                         start=True, stop=True).then_inc(cnt_rdy, 1)

            def three(dst, x_h, x_l, w_h, w_l, nk, start=True):
                for k in range(nk):
                    for m, (xs, ws) in enumerate(((x_h, w_h), (x_h, w_l), (x_l, w_h))):
                        last = t.matmul(dst, xs(k), ws(k), start=(k == 0 and m == 0), stop=(k == nk - 1 and m == 2))
                return last

            pe.wait_ge(const_r, 1)
            pe.wait_ge(oh_rdy, 1)
            count(NT)

            def project(b):
                for j in range(TB):
                    tt = TB * b + j
                    tok = slice(tt * P, (tt + 1) * P)
                    if tt == 0:
                        pe.wait_ge(w_lo, 1)
                        pe.wait_ge(pos_rdy, 1)
                    if j == 0:
                        pe.wait_ge(x_lo, b + 1)
                        if b >= 1:
                            pe.wait_ge(maxed, 2 * NG * b)
                    elif b == 1:
                        pe.wait_ge(q_even, TB)
                        pe.wait_ge(q_odd, TB)
                    elif b >= 2:
                        pe.wait_ge(mT_done, b - 1)
                        if b >= 3:
                            pe.wait_ge(res1, TB * (b - 2))
                    xh = lambda k: xTv_hi[:, k, tok]
                    xl = lambda k: xTv_lo[:, k, tok]
                    three(ps[:, 2 * j, :], xh, xl, lambda k: wqkv_hi[:, k, 0:2 * D],
                          lambda k: wqkv_lo[:, k, 0:2 * D], NK).then_inc(proj_qk, 1)
                    three(ps[:, (1, 7)[j], 0:D], xh, xl, lambda k: wqkv_hi[:, k, 2 * D:3 * D],
                          lambda k: wqkv_lo[:, k, 2 * D:3 * D], NK).then_inc(proj_v, 1)
                for j in range(TB):
                    tt = TB * b + j
                    if tt == 0:
                        pe.wait_ge(const_z, 1)
                    pe.wait_ge(qkv_lo, 3 * tt + 2)
                    for a in range(PAIRS):
                        last = t.transpose(ps16(2 * j)[:, a * P:(a + 1) * P],
                                           Ks[j][:, 2 * a:2 * a + 2].rearrange("p h s c -> p (h s c)"), identH[:, :])
                    last.then_inc(kT_rdy, 1)
                    pe.wait_ge(qkv_lo, 3 * tt + 3)
                    for a in range(PAIRS):
                        last = t.transpose(ps16((1, 7)[j])[:, a * P:(a + 1) * P],
                                           Qs[j][:, 2 * a:2 * a + 2].rearrange("p h s c -> p (h s c)"), identH[:, :])
                    last.then_inc(qT_rdy, 1)

            def scores(b, g):
                n = NG * b + g
                q, k = QT[b % 2], KT[b % 2]
                if g == 0:
                    pe.wait_ge(kT_done, TB * (b + 1))
                    pe.wait_ge(q_even, TB * (b + 1))
                    pe.wait_ge(q_odd, TB * (b + 1))
                    if b >= 2:
                        pe.wait_ge(res1, TB * (b - 1))
                else:
                    pe.wait_ge(maxed, 2 * n - 1)
                for bank, qt, kt in ((0, 0, 0), (1, 1, 0), (2, 1, 1)):
                    if bank == 1 and g > 0:
                        pe.wait_ge(maxed, 2 * n)
                    diag = qt == kt
                    if diag:
                        t.matmul(ps[:, bank, :], identB[:, :], maskS[:, :, :].rearrange("p a k -> p (a k)"),
                                 start=True, stop=False)
                    for i in range(G):
                        h = G * g + i
                        last = t.matmul(ps[:, bank, i * P:(i + 1) * P], q[:, h, qt * P:(qt + 1) * P],
                                        k[:, h // 2, kt * P:(kt + 1) * P], start=not diag,
                                        stop=(not diag) or i == G - 1)
                    if bank != 1:
                        last.then_inc(s_rdy, 1)

            def max_rows(b):
                pe.wait_ge(m_neg, b + 1)
                if b == 0:
                    pe.wait_ge(q_even, 2 * TB)
                    pe.wait_ge(q_odd, 2 * TB)
                elif b + 1 < B:
                    pe.wait_ge(q_even, TB * (b + 2))
                    pe.wait_ge(q_odd, TB * (b + 2))
                if b >= 2:
                    pe.wait_ge(res1, TB * (b - 1))
                for qt in range(TB):
                    last = t.transpose(ps16(7, slice(0, 4 * PAIRS))[:, qt * P:(qt + 1) * P],
                                       Mn[:, 2 * qt:2 * qt + 2].rearrange("p r s a -> p (r s a)"), identH[:, :])
                last.then_inc(mT_rdy, 1)

            def scores_T(b, g):
                n = NG * b + g
                q, k = QT[b % 2], KT[b % 2]
                if g == 0:
                    pe.wait_ge(m_row, 64 * (b + 1))
                if n >= 1:
                    pe.wait_ge(exped, 2 * n)
                for bank, kt, qt in ((3, 0, 0), (4, 0, 1), (5, 1, 1)):
                    diag = qt == kt
                    if diag:
                        t.matmul(ps[:, bank, :], identB[:, :], maskT[:, :, :].rearrange("p a k -> p (a k)"),
                                 start=True, stop=False)
                    for i in range(G):
                        h = G * g + i
                        last = t.matmul(ps[:, bank, i * P:(i + 1) * P], k[:, h // 2, kt * P:(kt + 1) * P],
                                        q[:, h, qt * P:(qt + 1) * P], start=not diag,
                                        stop=(not diag) or i == G - 1)
                last.then_inc(st_rdy, 1)

            def values(b, g):
                n = NG * b + g
                pe.wait_ge(p_lo, n + 1)
                if n >= 1:
                    pe.wait_ge(o_read, n)
                w = 2 * DK + 1
                for i in range(G):
                    h = G * g + i
                    for qt, parts in ((0, ((0, 0),)), (1, ((1, 0), (2, 1)))):
                        dst = ps[:, 6, (qt * G + i) * w:(qt * G + i + 1) * w]
                        todo = [(p, c, kt) for c, kt in parts for p in (Ph, Pl)]
                        for m, (p, c, kt) in enumerate(todo):
                            last = t.matmul(dst, p[n % 2][:, c, i * P:(i + 1) * P],
                                            Vs[:, (TB * b + kt) % VT, h, 0:w],
                                            start=m == 0, stop=m == len(todo) - 1)
                last.then_inc(av_rdy, 1)

            def out_project(b):
                for j in range(TB):
                    if j == 0:
                        pe.wait_ge(o_norm, NG * (b + 1))
                        if b + 1 < B:
                            pe.wait_ge(maxed, 2 * NG * (b + 2))
                        if b + 2 < B:
                            pe.wait_ge(kT_done, TB * (b + 3))
                    for k in range(NK):
                        last = t.transpose(ps[:, 2 * j, k * P:(k + 1) * P], On[:, j, k * P:(k + 1) * P], identF[:, :])
                    last.then_inc(oT_rdy, 1)
                for j in range(TB):
                    tt = TB * b + j
                    pe.wait_ge(oT_lo, tt + 1)
                    if b == 0:
                        pe.wait_ge(w_lo, 2)
                    if j == 0 and b + 2 < B:
                        pe.wait_ge(q_even, TB * (b + 3))
                        pe.wait_ge(q_odd, TB * (b + 3))
                    if j == 1 and b + 1 < B:
                        pe.wait_ge(mT_done, b + 2)
                    three(ps[:, (1, 7)[j], 0:D], lambda k: OT_hi[:, j, k], lambda k: OT_lo[:, j, k],
                          lambda k: wo_hi[:, k], lambda k: wo_lo[:, k], NK).then_inc(wo_rdy, 1)

            project(0)
            for g in range(NG):
                scores(0, g)
            project(1)
            max_rows(0)
            for b in range(B):
                for g in range(NG):
                    if b + 1 < B:
                        scores(b + 1, g)
                    scores_T(b, g)
                    if g >= 1:
                        values(b, g - 1)
                if b + 2 < B:
                    project(b + 2)
                values(b, NG - 1)
                if b + 1 < B:
                    max_rows(b + 1)
                out_project(b)

            pe.wait_ge(tile_rdy, 1)
            pe.wait_ge(res1, NT)
            for s in range(NS + 7):
                if s < NS:
                    pe.wait_ge(ld2[s], 16)
                    if s >= 2:
                        pe.wait_ge(a2lo, s - 1)
                    for k in range(NK):
                        last = t.transpose(ps[:, s % 2, k * P:(k + 1) * P], XS[:, s, k * P:(k + 1) * P], identF[:, :])
                    last.then_inc(a2T, 1)
                i = s - 1
                if 0 <= i < NS:
                    if i == 0:
                        pe.wait_ge(c_lo, CTX_AT + NCTX)
                    expert = pe.value_load(tile_i[0:1, 0, i:i + 1], min_val=0, max_val=E - 1)
                    pe.wait_ge(a2lo, i + 1)
                    if i >= 1:
                        pe.wait_ge(h2, i)
                    three(ps[:, 2, 0:D], lambda k: a_hi[i % 2][:, k], lambda k: a_lo[i % 2][:, k],
                          lambda k: ctx_hi[:, bass.ds(expert * (NK * D) + k * D, D)],
                          lambda k: ctx_lo[:, bass.ds(expert * (NK * D) + k * D, D)], NK).then_inc(z_rdy, 1)
                i = s - 2
                if 0 <= i < NS:
                    pe.wait_ge(h2, i + 1)
                    if i >= 1:
                        pe.wait_ge(h2lo, i)
                    for k in range(NK):
                        last = t.transpose(ps[:, 3, k * P:(k + 1) * P], hh[:, k * P:(k + 1) * P], identF[:, :])
                    last.then_inc(h2T, 1)
                i = s - 3
                if 0 <= i < NS:
                    expert = pe.value_load(tile_i[0:1, 0, i:i + 1], min_val=0, max_val=E - 1)
                    pe.wait_ge(h2lo, i + 1)
                    if i >= 1:
                        pe.wait_ge(mv2, i)
                    three(ps[:, 4, 0:D], lambda k: h_hi[:, k], lambda k: h_lo[:, k],
                          lambda k: ctx_hi[:, bass.ds(expert * (NK * D) + k * D, D)],
                          lambda k: ctx_lo[:, bass.ds(expert * (NK * D) + k * D, D)], NK).then_inc(y2, 1)
                i = s - 5
                if 0 <= i < NS:
                    pe.wait_ge(x2_rdy, i + 1)
                    if i >= 1:
                        pe.wait_ge(x2T_sb, i)
                    for k in range(NK):
                        last = t.transpose(ps[:, 5, k * P:(k + 1) * P], X2[:, i, k * P:(k + 1) * P], identF[:, :])
                    last.then_inc(x2T_rdy, 1)
                i = s - 6
                if 0 <= i < NS:
                    if i == 0:
                        pe.wait_ge(in_r, 32)
                    pe.wait_ge(x2T_sb, i + 1)
                    for k in range(NK):
                        last = t.matmul(ps[:, 6, i * E:(i + 1) * E], x2T[:, k], wr_sb[:, k, :],
                                        start=(k == 0), stop=(k == NK - 1))
                    last.then_inc(lg_rdy, 1)
            pe.wait_ge(oh_rdy, 2)
            count(NS)

            def x_T3(i):
                pe.wait_ge(ld3[i], 16)
                if i >= 1:
                    pe.wait_ge(a3lo, i)
                else:
                    pe.wait_ge(lg_sb, 1)
                for k in range(NK):
                    last = t.transpose(ps[:, 6, k * P:(k + 1) * P], XS[:, i, k * P:(k + 1) * P], identF[:, :])
                last.then_inc(a3T, 1)

            def gate_up(i, half, expert):
                for n in range(2):
                    for k in range(NK):
                        pass
                    at_ = lambda k, n=n: expert * EW + (n * NK + k) * F + half * 512
                    last = three(ps[:, 2 * half + n, :], lambda k: a_hi[i % 2][:, k], lambda k: a_lo[i % 2][:, k],
                                 lambda k: wf_hi[:, bass.ds(at_(k), 512)],
                                 lambda k: wf_lo[:, bass.ds(at_(k), 512)], NK)
                last.then_inc((gu_a, gu_b)[half], 1)

            def h_T3(i):
                pe.wait_ge(h3, 2 * i + 2)
                if i >= 1:
                    pe.wait_ge(h3lo, i)
                for k in range(NF):
                    last = t.transpose(ps[:, 4 + k // 4, (k % 4) * P:(k % 4 + 1) * P], hh[:, k * P:(k + 1) * P],
                                       identF[:, :])
                last.then_inc(h3T, 1)

            def down(i, expert):
                pe.wait_ge(h3lo, i + 1)
                if i >= 1:
                    pe.wait_ge(mv3, i)
                three(ps[:, 7, 0:D], lambda k: h_hi[:, k], lambda k: h_lo[:, k],
                      lambda k: wf_hi[:, bass.ds(expert * EW + DOWN + k * D, D)],
                      lambda k: wf_lo[:, bass.ds(expert * EW + DOWN + k * D, D)], NF).then_inc(y3, 1)

            pe.wait_ge(tile_rdy, 2)
            pe.wait_ge(c_lo, NCH)
            x_T3(0)
            before_e = None
            for i in range(NS + 1):
                if i < NS:
                    expert = pe.value_load(tile_i[0:1, 1, i:i + 1], min_val=0, max_val=E - 1)
                    pe.wait_ge(a3lo, i + 1)
                    if i >= 1:
                        pe.wait_ge(h3, 2 * i)
                    gate_up(i, 0, expert)
                if i >= 1:
                    h_T3(i - 1)
                if i + 1 < NS:
                    x_T3(i + 1)
                if i < NS:
                    gate_up(i, 1, expert)
                if i >= 1:
                    down(i - 1, before_e)
                before_e = expert


def kernel(x, itok_BxS_13_99985, ctx_2048, L0_attn_q_proj, L0_attn_k_proj, L0_attn_v_proj, L0_attn_o_proj,
           L0_ffn_Wr, L0_ffn_br, L0_ffn_Wg, L0_ffn_Wu, L0_ffn_Wd):
    import concourse.bacc as bacc
    from concourse.bass_utils import run_bass_kernel_spmd

    def chunked(w):
        w = np.asarray(w)
        return w.reshape(-1, P, w.shape[-1]).transpose(1, 0, 2)

    x = np.asarray(x)
    xf = x.reshape(T, D)
    wqkv = np.concatenate([np.asarray(w).T for w in (L0_attn_q_proj, L0_attn_k_proj, L0_attn_v_proj)], axis=1)
    ctx_e = [chunked(np.asarray(ctx_2048)[e].T).reshape(P, -1) for e in range(E)]
    wf = [np.concatenate([chunked(np.asarray(w)[e]).reshape(P, -1) for w in (L0_ffn_Wg, L0_ffn_Wu, L0_ffn_Wd)],
                         axis=1) for e in range(E)]
    arrays = {
        "x_tok": chunked(xf),
        "xT": chunked(xf.T),
        "ids": np.asarray(itok_BxS_13_99985).reshape(NT, P).T,
        "wqkvT": chunked(wqkv),
        "woT": chunked(np.asarray(L0_attn_o_proj).T),
        "ctxT": np.concatenate(ctx_e, axis=1),
        "Wr": chunked(L0_ffn_Wr),
        "br": np.asarray(L0_ffn_br),
        "Wf": np.concatenate(wf, axis=1),
    }
    arrays = {k: np.ascontiguousarray(a) for k, a in arrays.items()}
    nc = bacc.Bacc("TRN2", target_bir_lowering=False, num_devices=1)
    args = [nc.dram_tensor(k, a.shape, mybir.dt.from_np(a.dtype), kind="ExternalInput").ap()
            for k, a in arrays.items()]
    out = nc.dram_tensor("out", (T, D), F32, kind="ExternalOutput").ap()
    build(nc, *args, out)
    r = run_bass_kernel_spmd(nc, [arrays], core_ids=[0])
    return r.results[0]["out"].reshape(B, S, D)
```

```python
from contextlib import ExitStack

import numpy as np
import concourse.bass as bass
import concourse.mybir as mybir

F32, F16, BF16, I32 = mybir.dt.float32, mybir.dt.float16, mybir.dt.bfloat16, mybir.dt.int32
ALU, ACT, AX = mybir.AluOpType, mybir.ActivationFunctionType, mybir.AxisListType

P = 128
B, S, D = 4, 256, 256
H, DK = 16, 16
E, F = 4, 1024
T = B * S
NT = T // P
TB = S // P
NK = D // P
NF = F // P
NS = NT + E - 1
G = 4
NG = H // G
PAIRS = H // 2
VT = 3 * TB
STEPS = B * NG
AHEAD = NG + 1
SLOT = 64
ROW = D + 2
VOCAB_PART = 12500 // E
W_SCALE = 256.0
EPS = 1e-5
NEG = -3.0e38
PAD_TOKEN = 4096.0
CH = 1024
NCTX = E * NK * D // CH
EW = 2 * NK * F + NF * D
NCH = NCTX + E * EW // CH
RING = 4
LATE = 7
DOWN = 2 * NK * F


def build(nc, x_tok, xT, ids, wqkvT, woT, ctxT, Wr, br, Wf, out):
    ctx = ExitStack()
    with ctx:
        def sb(name, shape, dt):
            return ctx.enter_context(nc.sbuf_tensor(name, shape, dt))

        def sem(name):
            return ctx.enter_context(nc.semaphore(name))

        wf_hi = sb("wf_hi", [P, E * EW], F16)
        wf_lo = sb("wf_lo", [P, E * EW], F16)
        ring = sb("ring", [P, RING * CH], F32)
        xT_hi = sb("xT_hi", [P, NK * T], F16)
        xT_lo = sb("xT_lo", [P, NK * T], F16)
        ctx_hi, ctx_lo = xT_hi, xT_lo
        X1 = sb("X1", [P, NT, ROW], F32)
        identF = sb("identF", [P, P], F32)
        identH = sb("identH", [P, P], F16)
        identB = sb("identB", [P, P], BF16)
        before = sb("before", [P, P], F16)
        ones = sb("ones", [P, P], F16)
        maskS = sb("maskS", [P, G, P], BF16)
        maskT = sb("maskT", [P, G, P], BF16)
        fill = sb("fill", [P, ROW], F32)
        steps = sb("steps", [P, NT], F32)
        tiles = sb("tiles", [P, NS], F32)
        reset = sb("reset", [P, E, NS], F32)
        reset_e = sb("reset_e", [P, NS, E], F32)
        cum = sb("cum", [P, NS, E], F32)
        minus_half = sb("minus_half", [P, NS], F32)
        ids_sb = sb("ids_sb", [P, NT], I32)
        ge = sb("ge", [P, E + 1, NT], F32)
        oh = sb("oh", [P, NS, E], F16)
        cnt = sb("cnt", [P, E, NS], F32)
        run = sb("run", [P, E, NS], F32)
        over = sb("over", [P, E, NT], F32)
        nt_e = sb("nt_e", [P, E], F32)
        end_e = sb("end_e", [P, E], F32)
        base_e = sb("base_e", [P, E], F32)
        where = sb("where", [P, NS, E], F32)
        pos = sb("pos", [P, NS], F32)
        pos_i = sb("pos_i", [P, NS], I32)
        tile_ge = sb("tile_ge", [P, NS, E - 1], F32)
        tile_e = sb("tile_e", [P, NS], F32)
        tile_i = sb("tile_i", [P, 2, NS], I32)
        wr_sb = sb("wr_sb", [P, NK, E], F32)
        br_sb = sb("br_sb", [P, E], F32)
        lg = sb("lg", [P, NS, E], F32)
        ex = sb("ex", [P, NS, E], F32)
        ohf = sb("ohf", [P, NS, E], F32)
        top = sb("top", [P, NS], F32)
        valid = sb("valid", [P, NS], F32)
        out_i = sb("out_i", [P, NS], I32)
        st = sb("st", [P, 2, 6], F32)
        mv = sb("mv", [P, 2, 2], F32)
        veps = sb("veps", [P, 2], F32)
        rstd = sb("rstd", [P, 2], F32)

        ARENA = 72 * 1024
        arena = sb("arena", [P, ARENA // 4], F32)
        at = [0]

        def carve(shape, dt):
            n = int(np.prod(shape))
            size = n * (4 if dt in (F32, I32) else 2)
            a = arena[:, at[0] // 4:(at[0] + size) // 4]
            at[0] += size
            assert at[0] <= ARENA, at[0]
            if dt != F32:
                a = a.bitcast(dt)
            names = "abcd"[:len(shape)]
            return a.rearrange(f"p ({' '.join(names)}) -> p {' '.join(names)}", **dict(zip(names, shape)))

        wqkv_hi = carve([NK, 3 * D], F16)
        wqkv_lo = carve([NK, 3 * D], F16)
        wo_hi = carve([NK, D], F16)
        wo_lo = carve([NK, D], F16)
        QT = [carve([H, S], F16) for _ in range(2)]
        KT = [carve([PAIRS, S], F16) for _ in range(2)]
        tail = E * EW - (H + PAIRS) * S
        QT.append(wf_hi[:, tail:tail + H * S].rearrange("p (h t) -> p h t", h=H))
        KT.append(wf_hi[:, tail + H * S:].rearrange("p (h t) -> p h t", h=PAIRS))
        Qs = [carve([H, 4, DK], F16) for _ in range(2)]
        Ks = [carve([H, 4, DK], F16) for _ in range(2)]
        Vs = carve([VT, H, 2 * DK + 2], F16)
        Pf = carve([3, G * P], F32)
        Ph = [carve([3, G * P], F16) for _ in range(2)]
        Pl = [carve([3, G * P], F16) for _ in range(2)]
        On = carve([TB, D], F32)
        Oa = carve([TB * G, DK], F32)
        Or = carve([TB * G], F32)
        OT_hi = carve([TB, NK, P], F16)
        OT_lo = carve([TB, NK, P], F16)
        Mx = carve([TB, 2, PAIRS], F32)
        Mn = carve([TB * 2, 2, PAIRS], F16)
        mT = carve([S], F16)
        used_attention = at[0]
        at[0] = 0
        XS = carve([NS, ROW], F32)
        X2 = carve([NS, ROW], F32)
        a_hi = [carve([NK, P], F16) for _ in range(2)]
        a_lo = [carve([NK, P], F16) for _ in range(2)]
        sg = carve([F], F32)
        hh = carve([F], F32)
        h_hi = carve([NF, P], F16)
        h_lo = carve([NF, P], F16)
        x2T = carve([NK, P], F32)
        res = [carve([D], F32) for _ in range(2)]
        fin = [carve([D], F32) for _ in range(2)]
        late = [carve([CH], F32) for _ in range(LATE)]

        ps = ctx.enter_context(nc.psum_tensor("ps", [P, 8, 512], F32))

        def ps16(k, rows=slice(0, P)):
            return ps[rows, k, :].bitcast(F16)

        sorted2 = nc.dram_tensor("sorted2", [NS * P, ROW], F32, kind="Internal").ap()
        sorted3 = nc.dram_tensor("sorted3", [NS * P, ROW], F32, kind="Internal").ap()

        in_ids, in_wo, in_xtok, in_r = (sem(n) for n in ("in_ids", "in_wo", "in_xtok", "in_r"))
        in_wqkv = [sem(f"in_wqkv{k}") for k in range(NK)]
        in_xT = [sem(f"in_xT{b}") for b in range(B)]
        in_ch = [sem(f"in_ch{r}") for r in range(RING)]
        in_late = [sem(f"in_late{r}") for r in range(LATE)]
        const_z, const_r, const_s, const_m, const_q2, fillrow = (sem(n) for n in (
            "const_z", "const_r", "const_s", "const_m", "const_q2", "fillrow"))
        filled = sem("filled")
        w_hi, w_lo, x_hi, x_lo, c_hi, c_lo = (sem(n) for n in ("w_hi", "w_lo", "x_hi", "x_lo", "c_hi", "c_lo"))
        proj_qk, proj_v, qkv_hi, qkv_lo = (sem(n) for n in ("proj_qk", "proj_v", "qkv_hi", "qkv_lo"))
        kT_rdy, qT_rdy, kT_done, q_even, q_odd = (sem(n) for n in ("kT_rdy", "qT_rdy", "kT_done", "q_even", "q_odd"))
        s_rdy, maxed, m_neg, mT_rdy, mT_done, m_row = (sem(n) for n in (
            "s_rdy", "maxed", "m_neg", "mT_rdy", "mT_done", "m_row"))
        st_rdy, exped, p_lo, av_rdy, o_read, o_norm = (sem(n) for n in (
            "st_rdy", "exped", "p_lo", "av_rdy", "o_read", "o_norm"))
        oT_rdy, oT_hi, oT_lo, wo_rdy, res1, bn1, mv1, rs1, x1_rdy = (sem(n) for n in (
            "oT_rdy", "oT_hi", "oT_lo", "wo_rdy", "res1", "bn1", "mv1", "rs1", "x1_rdy"))
        link_v, link_g = sem("link_v"), sem("link_g")
        oh_rdy, cnt_rdy, cnt_sb, pos_rdy, tile_rdy = (sem(n) for n in ("oh_rdy", "cnt_rdy", "cnt_sb", "pos_rdy", "tile_rdy"))
        scat2, scat3 = sem("scat2"), sem("scat3")
        scat_out = [sem(f"scat_out{i}") for i in range(2)]
        ld2 = [sem(f"ld2_{i}") for i in range(NS)]
        ld3 = [sem(f"ld3_{i}") for i in range(NS)]
        a2T, a2hi, a2lo, z_rdy, sg2, h2, h2T, h2hi, h2lo, y2, r2, mv2, rs2, x2_rdy, x2T_rdy, x2T_sb, lg_rdy = (
            sem(n) for n in ("a2T", "a2hi", "a2lo", "z_rdy", "sg2", "h2", "h2T", "h2hi", "h2lo", "y2", "r2", "mv2",
                             "rs2", "x2_rdy", "x2T_rdy", "x2T_sb", "lg_rdy"))
        lg_sb, ex_rdy, w_rdy = sem("lg_sb"), sem("ex_rdy"), sem("w_rdy")
        a3T, a3hi, a3lo, gu_a, gu_b, sg3, h3, h3T, h3hi, h3lo, y3, r3, mv3, rs3, f3 = (
            sem(n) for n in ("a3T", "a3hi", "a3lo", "gu_a", "gu_b", "sg3", "h3", "h3T", "h3hi", "h3lo", "y3",
                             "r3", "mv3", "rs3", "f3"))

        def bank_qk(tt):
            return (0, 2, 3, 5)[tt] if tt < 2 * TB else (0, 2)[tt % 2]

        def bank_v(tt):
            return (1, 7, 4, 6)[tt] if tt < 2 * TB else (1, 7)[tt % 2]

        def bank_kT(tt):
            return bank_qk(tt) if tt < 2 * TB else 0

        def bank_qT(tt):
            return bank_v(tt) if tt < 2 * TB else 1

        def chunk_dst(c, hi):
            if c < NCTX:
                return (ctx_hi if hi else ctx_lo)[:, c * CH:(c + 1) * CH]
            c -= NCTX
            return (wf_hi if hi else wf_lo)[:, c * CH:(c + 1) * CH]

        def chunk_src(c):
            return ring[:, (c % RING) * CH:(c % RING + 1) * CH]

        xT_st = ring[:, 0:NK * T].rearrange("p (k t) -> p k t", k=NK)
        wqkv_st = ring[:, NK * T:NK * (T + 3 * D)].rearrange("p (k n) -> p k n", k=NK)
        wo_st = ring[:, NK * (T + 3 * D):NK * (T + 4 * D)].rearrange("p (k n) -> p k n", k=NK)
        xTv_hi = xT_hi[:, :].rearrange("p (k t) -> p k t", k=NK)
        xTv_lo = xT_lo[:, :].rearrange("p (k t) -> p k t", k=NK)

        ATT_CHUNKS = NCH - LATE - RING
        CTX_AT = 8
        ORDER = list(range(NCTX, NCH))
        ORDER = ORDER[:CTX_AT] + list(range(NCTX)) + ORDER[CTX_AT:]

        def staged(n):
            if n >= NCH - LATE:
                return late[n - (NCH - LATE)], in_late[n - (NCH - LATE)], 16
            r = n % RING
            return ring[:, r * CH:(r + 1) * CH], in_ch[r], 16 * (n // RING + 1)

        block = ctx.enter_context(nc.Block())

        @block.sync
        def _(sp):
            sp.dma_start(ids_sb[:, :], ids).then_inc(in_ids, 16)
            sp.dma_start(xT_st[:, :, 0:S], xT[:, :, 0:S]).then_inc(in_xT[0], 16)
            for k in range(NK):
                sp.dma_start(wqkv_st[:, k], wqkvT[:, k]).then_inc(in_wqkv[k], 16)
            for b in range(1, B):
                sp.dma_start(xT_st[:, :, b * S:(b + 1) * S], xT[:, :, b * S:(b + 1) * S]).then_inc(in_xT[b], 16)
            sp.dma_start(wo_st, woT).then_inc(in_wo, 16)
            sp.dma_start(X1[:, :, 0:D], x_tok).then_inc(in_xtok, 16)
            sp.dma_start(wr_sb[:, :, :], Wr).then_inc(in_r, 16)
            sp.dma_start(br_sb[:, :], br.partition_broadcast(P)).then_inc(in_r, 16)
            sp.wait_ge(fillrow, 1)
            for scratch in (sorted2, sorted3):
                sp.dma_start(scratch.rearrange("(n p) d -> p n d", p=P),
                             fill[:, :].unsqueeze(1).to_broadcast([P, NS, ROW])).then_inc(filled, 16)

            def load(n):
                if n < RING:
                    if n * CH < NK * T:
                        sp.wait_ge(x_lo, B)
                    else:
                        sp.wait_ge(w_lo, NK + 1)
                elif n >= NCH - LATE:
                    sp.wait_ge(res1, NT)
                else:
                    sp.wait_ge(c_lo, n - RING + 1)
                c = ORDER[n]
                src = (ctxT[:, c * CH:(c + 1) * CH] if c < NCTX else
                       Wf[:, (c - NCTX) * CH:(c - NCTX + 1) * CH])
                dst, arrived, _ = staged(n)
                sp.dma_start(dst, src).then_inc(arrived, 16)

            def max_rows(b):
                sp.wait_ge(mT_done, b + 1)
                for par in range(2):
                    for part in range(2):
                        row = par * SLOT + 3 * DK + part
                        src = (par * 2 + part) * PAIRS
                        sp.dma_start(QT[b % 3][row:row + 1, par::2, :],
                                     mT[src:src + PAIRS, :]).then_inc(m_row, 16)

            max_rows(0)
            n = 0
            for step in range(STEPS):
                if step % NG == NG - 1 and step + 1 < STEPS:
                    max_rows(step // NG + 1)
                while n < min(step + RING, NCH - LATE):
                    load(n)
                    n += 1
            sp.wait_ge(scat2, 16 * NT)
            for i in range(NS):
                sp.dma_start(XS[:, i, :], sorted2[i * P:(i + 1) * P, :]).then_inc(ld2[i], 16)
            while n < NCH:
                load(n)
                n += 1
            sp.wait_ge(scat3, 16 * NS)
            for i in range(NS):
                sp.dma_start(XS[:, i, :], sorted3[i * P:(i + 1) * P, :]).then_inc(ld3[i], 16)

        @block.gpsimd
        def _(pool):
            g = nc.gpsimd
            links = [0]

            def link(ins):
                links[0] += 1
                ins.then_inc(link_g, 1)
                pool.wait_ge(link_g, links[0])

            g.iota(tiles[:, :], pattern=[[1, NS]], base=0, channel_multiplier=0,
                   allow_small_or_imprecise_dtypes=True)
            g.iota(steps[:, :], pattern=[[P, NT]], base=0, channel_multiplier=0,
                   allow_small_or_imprecise_dtypes=True)
            g.memset(reset[:, :, :], 1.0)
            g.memset(reset_e[:, :, :], 1.0)
            g.memset(ones[:, :].bitcast(F32), float(np.array([0x3C003C00], np.uint32).view(np.float32)[0]))
            g.memset(identH[:, :].bitcast(F32), 0.0)
            link(g.memset(before[:, :].bitcast(F32), 0.0))
            g.memset(reset[:, :, 0:1], 0.0)
            g.memset(reset_e[:, :, 0:1], 0.0)
            g.affine_select(out=before[:, :], in_=before[:, :], compare_op=ALU.is_ge, fill=1.0,
                            base=0, pattern=[[-1, P]], channel_multiplier=1).then_inc(const_r, 1)
            for j in range(2):
                g.memset(Qs[j][:, :, 3, :], 0.0)
                g.memset(Ks[j][:, :, 3, :], 0.0)
            link(g.affine_select(out=identH[:, :], in_=identH[:, :], compare_op=ALU.not_equal, fill=1.0,
                                 base=0, pattern=[[-1, P]], channel_multiplier=1))
            for j in range(2):
                last = g.memset(Ks[j][:, :, 3, 0:2], 1.0)
            last.then_inc(const_s, 1)
            g.memset(identB[:, :].bitcast(F32), 0.0)
            g.memset(Vs[:, :, :, 2 * DK:2 * DK + 2], 1.0)
            link(g.memset(maskS[:, :, :].bitcast(F32), 0.0))
            g.affine_select(out=identB[:, :], in_=identB[:, :], compare_op=ALU.not_equal, fill=1.0,
                            base=0, pattern=[[-1, P]], channel_multiplier=1)
            g.affine_select(out=maskS[:, :, :], in_=maskS[:, :, :], compare_op=ALU.is_ge, fill=NEG,
                            base=0, pattern=[[0, G], [-1, P]], channel_multiplier=1).then_inc(const_m, 1)
            g.memset(identF[:, :], 0.0)
            link(g.memset(maskT[:, :, :].bitcast(F32), 0.0))
            g.affine_select(out=identF[:, :], in_=identF[:, :], compare_op=ALU.not_equal, fill=1.0,
                            base=0, pattern=[[-1, P]], channel_multiplier=1)
            g.affine_select(out=maskT[:, :, :], in_=maskT[:, :, :], compare_op=ALU.is_ge, fill=NEG,
                            base=0, pattern=[[0, G], [1, P]], channel_multiplier=-1).then_inc(const_m, 1)
            pool.wait_ge(const_m, 2)
            link(g.memset(QT[2][SLOT:P, 0::2, :].bitcast(F32), 0.0))
            g.memset(QT[2][0:SLOT, 1::2, :].bitcast(F32), 0.0).then_inc(const_q2, 1)
            pool.wait_ge(const_q2, 1)
            link(g.memset(fill[:, :], 0.0))
            g.memset(fill[:, D:D + 1], PAD_TOKEN).then_inc(fillrow, 1)
            g.memset(minus_half[:, :], -0.5)
            g.memset(X1[:, :, D + 1:D + 2], 0.0)
            link(g.iota(X1[:, :, D], pattern=[[P, NT]], base=0, channel_multiplier=1,
                        allow_small_or_imprecise_dtypes=True))

            def inv_std(var, n, out_sem):
                link(g.tensor_scalar(veps[:, 0:n], var, EPS, None, ALU.add))
                g.tensor_tensor(rstd[:, 0:n], veps[:, 0:n], minus_half[:, 0:n], ALU.pow).then_inc(out_sem, 1)

            def scatter2(b):
                for j in range(TB):
                    tt = TB * b + j
                    pool.wait_ge(x1_rdy, tt + 1)
                    g.indirect_dma_start(sorted2[:, :], bass.IndirectOffsetOnAxis(ap=pos_i[:, tt:tt + 1], axis=0),
                                         X1[:, tt, :], None, bounds_check=NS * P - 1,
                                         oob_is_err=False).then_inc(scat2, 16)

            for n in range(STEPS):
                b, gr = divmod(n, NG)
                if gr == NG - 1 and b >= 1:
                    pool.wait_ge(mv1, TB * b)
                    inv_std(mv[:, :, 1], TB, rs1)
                pool.wait_ge(exped, 2 * n + 2)
                if n >= 2:
                    pool.wait_ge(av_rdy, n - 1)
                g.tensor_tensor(Pl[n % 2], Pf, Ph[n % 2], ALU.subtract).then_inc(p_lo, 1)
                if gr == 0 and b >= 2:
                    if b == 2:
                        pool.wait_ge(filled, 32)
                        pool.wait_ge(pos_rdy, 1)
                    scatter2(b - 2)
            scatter2(B - 2)
            pool.wait_ge(mv1, NT)
            inv_std(mv[:, :, 1], TB, rs1)
            scatter2(B - 1)
            for i in range(NS):
                pool.wait_ge(mv2, i + 1)
                link(g.tensor_scalar(veps[:, i % 2:i % 2 + 1], mv[:, i % 2, 1:2], EPS, None, ALU.add))
                g.tensor_tensor(rstd[:, i % 2:i % 2 + 1], veps[:, i % 2:i % 2 + 1], minus_half[:, 0:1],
                                ALU.pow).then_inc(rs2, 1)
            pool.wait_ge(pos_rdy, 2)
            pool.wait_ge(w_rdy, 1)
            for i in range(NS):
                g.indirect_dma_start(sorted3[:, :], bass.IndirectOffsetOnAxis(ap=pos_i[:, i:i + 1], axis=0),
                                     X2[:, i, :], None, bounds_check=NS * P - 1,
                                     oob_is_err=False).then_inc(scat3, 16)
            for i in range(NS):
                pool.wait_ge(mv3, i + 1)
                link(g.tensor_scalar(veps[:, i % 2:i % 2 + 1], mv[:, i % 2, 1:2], EPS, None, ALU.add))
                g.tensor_tensor(rstd[:, i % 2:i % 2 + 1], veps[:, i % 2:i % 2 + 1], minus_half[:, 0:1],
                                ALU.pow).then_inc(rs3, 1)
                pool.wait_ge(f3, i + 1)
                g.indirect_dma_start(out, bass.IndirectOffsetOnAxis(ap=out_i[:, i:i + 1], axis=0),
                                     fin[i % 2], None, bounds_check=T - 1,
                                     oob_is_err=False).then_inc(scat_out[i % 2], 16)
            for i in range(2):
                pool.wait_ge(scat_out[i], 16 * ((NS + 1 - i) // 2))

        @block.scalar
        def _(act):
            a = nc.scalar

            def split_hi(n):
                src, arrived, value = staged(n)
                act.wait_ge(arrived, value)
                if ORDER[n] < NCTX:
                    act.wait_ge(proj_v, NT)
                a.activation(chunk_dst(ORDER[n], True), src, ACT.Copy, scale=W_SCALE).then_inc(c_hi, 1)

            def x_split(b):
                act.wait_ge(in_xT[b], 16)
                a.activation(xTv_hi[:, :, b * S:(b + 1) * S], xT_st[:, :, b * S:(b + 1) * S],
                             ACT.Copy).then_inc(x_hi, 1)

            def proj_hi(tt):
                j = tt % 2
                act.wait_ge(proj_qk, tt + 1)
                if tt >= 2:
                    act.wait_ge(kT_rdy, tt - 1)
                    act.wait_ge(qT_rdy, tt - 1)
                else:
                    act.wait_ge(const_s, 1)
                qk = ps[:, bank_qk(tt), :].rearrange("p (s h c) -> p s h c", s=2, h=H)
                rep = [P, H, 2, DK]
                a.activation(Ks[j][:, :, 0:3:2, :], qk[:, 1].unsqueeze(2).to_broadcast(rep), ACT.Copy,
                             scale=1 / W_SCALE).then_inc(qkv_hi, 1)
                a.activation(Qs[j][:, :, 0:2, :], qk[:, 0].unsqueeze(2).to_broadcast(rep), ACT.Copy,
                             scale=1 / W_SCALE).then_inc(qkv_hi, 1)
                act.wait_ge(proj_v, tt + 1)
                if tt >= VT:
                    act.wait_ge(av_rdy, NG * ((tt - VT) // TB + 1))
                a.activation(Vs[:, tt % VT, :, 0:DK],
                             ps[:, bank_v(tt), 0:D].rearrange("p (h c) -> p h c", h=H), ACT.Copy,
                             scale=1 / W_SCALE).then_inc(qkv_hi, 1)

            def q_odds(tt):
                b, j = divmod(tt, TB)
                act.wait_ge(qT_rdy, tt + 1)
                a.activation(QT[b % 3][SLOT:P, 1::2, j * P:(j + 1) * P],
                             ps16(bank_qT(tt), slice(SLOT, P)).rearrange("p (h t) -> p h t", h=PAIRS),
                             ACT.Copy).then_inc(q_odd, 1)

            x_split(0)
            for k in range(NK):
                act.wait_ge(in_wqkv[k], 16)
                a.activation(wqkv_hi[:, k], wqkv_st[:, k], ACT.Copy, scale=W_SCALE).then_inc(w_hi, 1)
            x_split(1)

            def exps(b, g):
                n = NG * b + g
                act.wait_ge(st_rdy, n + 1)
                if n >= 2:
                    act.wait_ge(av_rdy, n - 1)
                a.activation(Ph[n % 2], ps[:, 3:6, :], ACT.Exp, scale=DK ** -0.5).then_inc(exped, 1)
                if n >= 1:
                    act.wait_ge(p_lo, n)
                a.activation(Pf, ps[:, 3:6, :], ACT.Exp, scale=DK ** -0.5).then_inc(exped, 1)

            def o_hi(b):
                act.wait_ge(oT_rdy, b + 1)
                if b >= 1:
                    act.wait_ge(wo_rdy, TB * b)
                a.activation(OT_hi, ps[:, 7, :].rearrange("p (j k t) -> p j k t", j=TB, k=NK),
                             ACT.Copy).then_inc(oT_hi, 1)

            proj_hi(0)
            proj_hi(1)
            q_odds(0)
            q_odds(1)
            proj_hi(2)
            proj_hi(3)
            q_odds(2)
            q_odds(3)
            x_split(2)
            x_split(3)
            act.wait_ge(in_wo, 16)
            a.activation(wo_hi, wo_st, ACT.Copy, scale=W_SCALE).then_inc(w_hi, 1)
            n = 0
            for step in range(STEPS):
                b, g = divmod(step, NG)
                exps(b, g)
                if b + 2 < B:
                    tt = TB * (b + 2)
                    if g == 0:
                        proj_hi(tt)
                    elif g == 1:
                        q_odds(tt)
                        proj_hi(tt + 1)
                    elif g == 2:
                        q_odds(tt + 1)
                if g == 0 and b >= 1:
                    o_hi(b - 1)
                if step >= 1 and n < ATT_CHUNKS:
                    split_hi(n)
                    n += 1
            o_hi(B - 1)

            for s in range(NS + 6):
                if n < NCH:
                    split_hi(n)
                    n += 1
                if s < NS:
                    act.wait_ge(a2T, s + 1)
                    if s >= 2:
                        act.wait_ge(z_rdy, s - 1)
                    a.activation(a_hi[s % 2], ps[:, s % 2, 0:D].rearrange("p (k t) -> p k t", k=NK),
                                 ACT.Copy).then_inc(a2hi, 1)
                i = s - 1
                if 0 <= i < NS:
                    act.wait_ge(z_rdy, i + 1)
                    if i >= 1:
                        act.wait_ge(h2, i)
                    a.activation(sg[:, 0:D], ps[:, 2, 0:D], ACT.Silu, scale=1 / W_SCALE).then_inc(sg2, 1)
                i = s - 2
                if 0 <= i < NS:
                    act.wait_ge(h2T, i + 1)
                    if i >= 1:
                        act.wait_ge(y2, i)
                    a.activation(h_hi[:, 0:NK], ps[:, 3, 0:D].rearrange("p (k t) -> p k t", k=NK),
                                 ACT.Copy).then_inc(h2hi, 1)
                i = s - 5
                if 0 <= i < NS:
                    act.wait_ge(x2T_rdy, i + 1)
                    if i >= 1:
                        act.wait_ge(lg_rdy, i)
                    a.activation(x2T, ps[:, 5, 0:D].rearrange("p (k t) -> p k t", k=NK),
                                 ACT.Copy).then_inc(x2T_sb, 1)
            while n < NCH:
                split_hi(n)
                n += 1
            act.wait_ge(lg_sb, 1)
            a.activation(ex[:, :, :], lg[:, :, :], ACT.Exp).then_inc(ex_rdy, 1)

            def x_hi3(i):
                act.wait_ge(a3T, i + 1)
                if i >= 2:
                    act.wait_ge(gu_b, i - 1)
                a.activation(a_hi[i % 2], ps[:, 6, 0:D].rearrange("p (k t) -> p k t", k=NK),
                             ACT.Copy).then_inc(a3hi, 1)

            def silu(i, half):
                act.wait_ge((gu_a, gu_b)[half], i + 1)
                if i >= 1:
                    act.wait_ge(h3, 2 * (i - 1) + half + 1)
                a.activation(sg[:, half * 512:(half + 1) * 512], ps[:, 2 * half, :], ACT.Silu,
                             scale=1 / W_SCALE).then_inc(sg3, 1)

            def h_hi3(i):
                act.wait_ge(h3T, i + 1)
                if i >= 1:
                    act.wait_ge(y3, i)
                a.activation(h_hi, ps[:, 4:6, :].rearrange("p c (k t) -> p (c k) t", t=P),
                             ACT.Copy).then_inc(h3hi, 1)

            x_hi3(0)
            for i in range(NS + 1):
                if i < NS:
                    silu(i, 0)
                if i >= 1:
                    h_hi3(i - 1)
                if i + 1 < NS:
                    x_hi3(i + 1)
                if i < NS:
                    silu(i, 1)

        @block.vector
        def _(dve):
            v = nc.vector
            links = [0]

            def link(ins):
                links[0] += 1
                ins.then_inc(link_v, 1)
                dve.wait_ge(link_v, links[0])

            def split_lo(n):
                dve.wait_ge(c_hi, n + 1)
                v.scalar_tensor_tensor(out=chunk_dst(ORDER[n], False), in0=staged(n)[0], scalar=W_SCALE,
                                       in1=chunk_dst(ORDER[n], True), op0=ALU.mult,
                                       op1=ALU.subtract).then_inc(c_lo, 1)

            def counts(n, which):
                dve.wait_ge(cnt_rdy, which + 1)
                v.tensor_copy(cum[:, 0:n, :], ps[:, 7, 0:n * E].rearrange("p (i e) -> p i e", e=E))
                v.tensor_copy(cnt[:, :, 0:n], ps[:, 7, 256:256 + n * E].rearrange("p (i e) -> p e i", e=E)
                              ).then_inc(cnt_sb, 1)

            def slots(n, which):
                dve.wait_ge(cnt_sb, which + 1)
                if n == NS:
                    link(v.tensor_tensor_scan(run[:, :, :].rearrange("p e i -> p (e i)"),
                                              reset[:, :, :].rearrange("p e i -> p (e i)"),
                                              cnt[:, :, :].rearrange("p e i -> p (e i)"), 0.0, ALU.mult, ALU.add))
                else:
                    for e in range(E):
                        ins = v.tensor_tensor_scan(run[:, e, 0:n], reset[:, e, 0:n], cnt[:, e, 0:n], 0.0,
                                                   ALU.mult, ALU.add)
                    link(ins)
                link(v.tensor_tensor(over[:, :, :], run[:, :, n - 1:n].to_broadcast([P, E, NT]),
                                     steps[:, :].unsqueeze(1).to_broadcast([P, E, NT]), ALU.is_gt))
                link(v.reduce_sum(nt_e[:, :], over[:, :, :], AX.X))
                link(v.tensor_tensor_scan(end_e[:, :], reset[:, 0, 1:1 + E], nt_e[:, :], 0.0, ALU.mult, ALU.add))
                link(v.tensor_tensor(base_e[:, :], end_e[:, :], nt_e[:, :], ALU.subtract))
                link(v.tensor_tensor(run[:, :, 0:n], run[:, :, 0:n], cnt[:, :, 0:n], ALU.subtract))
                link(v.scalar_tensor_tensor(out=run[:, :, 0:n], in0=base_e[:, :].unsqueeze(2).to_broadcast([P, E, n]),
                                            scalar=float(P), in1=run[:, :, 0:n], op0=ALU.mult, op1=ALU.add))
                link(v.tensor_tensor(where[:, 0:n, :], cum[:, 0:n, :],
                                     run[:, :, 0:n].rearrange("p e i -> p i e"), ALU.add))
                link(v.tensor_tensor(where[:, 0:n, :], where[:, 0:n, :], oh[:, 0:n, :], ALU.mult))
                link(v.reduce_sum(pos[:, 0:n], where[:, 0:n, :], AX.X))
                if n == NS:
                    link(v.scalar_tensor_tensor(out=pos[:, :], in0=valid[:, :], scalar=-PAD_TOKEN, in1=pos[:, :],
                                                op0=ALU.mult, op1=ALU.add))
                    link(v.tensor_scalar(pos[:, :], pos[:, :], PAD_TOKEN, None, ALU.add))
                v.tensor_copy(pos_i[:, 0:n], pos[:, 0:n]).then_inc(pos_rdy, 1)
                link(v.tensor_tensor(tile_ge[:, :, :], tiles[:, :].unsqueeze(2).to_broadcast([P, NS, E - 1]),
                                     end_e[:, 0:E - 1].unsqueeze(1).to_broadcast([P, NS, E - 1]), ALU.is_ge))
                link(v.reduce_sum(tile_e[:, :], tile_ge[:, :, :], AX.X))
                v.tensor_copy(tile_i[:, which, :], tile_e[:, :]).then_inc(tile_rdy, 1)

            dve.wait_ge(in_ids, 16)
            v.memset(ge[:, 0, :], 1.0)
            v.memset(ge[:, E, :], 0.0)
            for e in range(1, E):
                ins = v.tensor_scalar(ge[:, e, :], ids_sb[:, :], float(e * VOCAB_PART), None, ALU.is_ge)
            link(ins)
            v.tensor_tensor(oh[:, 0:NT, :].rearrange("p i e -> p e i"), ge[:, 0:E, :], ge[:, 1:E + 1, :],
                            ALU.subtract).then_inc(oh_rdy, 1)
            for q in QT[0:2]:
                v.memset(q[SLOT:P, 0::2, :].bitcast(F32), 0.0)
                ins = v.memset(q[0:SLOT, 1::2, :].bitcast(F32), 0.0)
            ins.then_inc(const_z, 1)
            counts(NT, 0)

            def x_low(b):
                dve.wait_ge(x_hi, b + 1)
                t = slice(b * S, (b + 1) * S)
                v.tensor_tensor(xTv_lo[:, :, t], xT_st[:, :, t], xTv_hi[:, :, t], ALU.subtract).then_inc(x_lo, 1)

            x_low(0)
            for k in range(NK):
                dve.wait_ge(w_hi, k + 1)
                v.scalar_tensor_tensor(out=wqkv_lo[:, k], in0=wqkv_st[:, k], scalar=W_SCALE, in1=wqkv_hi[:, k],
                                       op0=ALU.mult, op1=ALU.subtract).then_inc(w_lo, 1)
            x_low(1)

            def proj_lo(tt):
                j = tt % 2
                qk = ps[:, bank_qk(tt), :].rearrange("p (s h c) -> p s h c", s=2, h=H)
                vv = ps[:, bank_v(tt), 0:D].rearrange("p (h c) -> p h c", h=H)
                for n, (lo, src, hi) in enumerate((
                        (Ks[j][:, :, 1, :], qk[:, 1], Ks[j][:, :, 0, :]),
                        (Qs[j][:, :, 2, :], qk[:, 0], Qs[j][:, :, 0, :]),
                        (Vs[:, tt % VT, :, DK:2 * DK], vv, Vs[:, tt % VT, :, 0:DK]))):
                    dve.wait_ge(qkv_hi, 3 * tt + (2, 2, 3)[n])
                    v.scalar_tensor_tensor(out=lo, in0=src, scalar=1 / W_SCALE, in1=hi,
                                           op0=ALU.mult, op1=ALU.subtract).then_inc(qkv_lo, 1)

            def stacks(tt):
                b, j = divmod(tt, TB)
                dve.wait_ge(kT_rdy, tt + 1)
                v.tensor_copy(KT[b % 3][:, :, j * P:(j + 1) * P],
                              ps16(bank_kT(tt)).rearrange("p (h t) -> p h t", h=PAIRS)).then_inc(kT_done, 1)
                dve.wait_ge(qT_rdy, tt + 1)
                v.tensor_copy(QT[b % 3][0:SLOT, 0::2, j * P:(j + 1) * P],
                              ps16(bank_qT(tt), slice(0, SLOT)).rearrange("p (h t) -> p h t", h=PAIRS)
                              ).then_inc(q_even, 1)

            def maxima(b, g):
                n = NG * b + g
                dst = Mx[:, :, :, 2 * g:2 * g + 2].rearrange("p t r a -> p t a r")
                if g == 0 and b >= 1:
                    dve.wait_ge(m_neg, b)
                dve.wait_ge(s_rdy, 2 * n + 1)
                v.tensor_reduce(dst[:, 0], ps[:, 0, :].rearrange("p (a r k) -> p a r k", a=2, r=2),
                                AX.X, ALU.max).then_inc(maxed, 1)
                dve.wait_ge(s_rdy, 2 * n + 2)
                v.tensor_reduce(dst[:, 1].rearrange("p a r -> p a r"),
                                ps[:, 1:3, :].rearrange("p c (a r k) -> p (a r) c k", a=2, r=2),
                                AX.XY, ALU.max).then_inc(maxed, 1)

            def negate(b):
                m = Mx.rearrange("p t r a -> p (t r) a")
                dve.wait_ge(maxed, 2 * NG * (b + 1))
                if b >= 1:
                    dve.wait_ge(mT_rdy, b)
                link(v.tensor_scalar(Mn[:, :, 0, :], m, -1.0, None, ALU.mult))
                v.scalar_tensor_tensor(out=Mn[:, :, 1, :], in0=m, scalar=-1.0, in1=Mn[:, :, 0, :],
                                       op0=ALU.mult, op1=ALU.subtract).then_inc(m_neg, 1)

            def max_T(b):
                dve.wait_ge(mT_rdy, b + 1)
                if b >= 1:
                    dve.wait_ge(m_row, 64 * b)
                v.tensor_copy(mT[0:4 * PAIRS, :], ps16(7, slice(0, 4 * PAIRS))[:, 0:S]).then_inc(mT_done, 1)

            def outputs(b, g):
                n = NG * b + g
                o = ps[:, 6, 0:TB * G * (2 * DK + 1)].rearrange("p (a c) -> p a c", c=2 * DK + 1)
                dve.wait_ge(av_rdy, n + 1)
                if n >= 1:
                    dve.wait_ge(o_norm, n)
                v.reciprocal(Or, o[:, :, 2 * DK])
                v.tensor_reduce(Oa, o[:, :, 0:2 * DK].rearrange("p a (s c) -> p a c s", s=2),
                                AX.X, ALU.add).then_inc(o_read, 1)
                dve.wait_ge(o_read, n + 1)
                if g == 0 and b >= 1:
                    dve.wait_ge(oT_rdy, b)
                dst = On[:, :, g * G * DK:(g + 1) * G * DK]
                for q in range(TB):
                    ins = v.tensor_tensor(dst[:, q].rearrange("p (a c) -> p a c", c=DK), Oa[:, q * G:(q + 1) * G, :],
                                          Or[:, q * G:(q + 1) * G].unsqueeze(2).to_broadcast([P, G, DK]), ALU.mult)
                ins.then_inc(o_norm, 1)

            def o_lo(b):
                dve.wait_ge(oT_hi, b + 1)
                if b >= 1:
                    dve.wait_ge(wo_rdy, TB * b)
                v.tensor_tensor(OT_lo, ps[:, 7, :].rearrange("p (j k t) -> p j k t", j=TB, k=NK), OT_hi,
                                ALU.subtract).then_inc(oT_lo, 1)

            def residual(b):
                for j in range(TB):
                    tt = TB * b + j
                    dve.wait_ge(wo_rdy, TB * (b + 1))
                    dve.wait_ge(in_xtok, 16)
                    v.scalar_tensor_tensor(out=X1[:, tt, 0:D], in0=ps[:, 7, j * D:(j + 1) * D], scalar=1 / W_SCALE,
                                           in1=X1[:, tt, 0:D], op0=ALU.mult, op1=ALU.add).then_inc(res1, 1)
                for j in range(TB):
                    tt = TB * b + j
                    dve.wait_ge(res1, tt + 1)
                    v.bn_stats(st[:, j, :], X1[:, tt, 0:D]).then_inc(bn1, 1)
                for j in range(TB):
                    tt = TB * b + j
                    dve.wait_ge(bn1, tt + 1)
                    if b >= 1 and j == 0:
                        dve.wait_ge(rs1, b)
                    v.bn_aggr(mv[:, j, :], st[:, j, :]).then_inc(mv1, 1)

            def norm1(b):
                dve.wait_ge(rs1, b + 1)
                for j in range(TB):
                    tt = TB * b + j
                    dve.wait_ge(mv1, tt + 1)
                    v.tensor_scalar(X1[:, tt, 0:D], X1[:, tt, 0:D], mv[:, j, 0:1], rstd[:, j:j + 1],
                                    ALU.subtract, ALU.mult).then_inc(x1_rdy, 1)

            proj_lo(0)
            proj_lo(1)
            stacks(0)
            stacks(1)
            proj_lo(2)
            maxima(0, 0)
            proj_lo(3)
            maxima(0, 1)
            stacks(2)
            maxima(0, 2)
            stacks(3)
            maxima(0, 3)
            negate(0)
            max_T(0)
            maxima(1, 0)
            x_low(2)
            x_low(3)
            dve.wait_ge(w_hi, NK + 1)
            v.scalar_tensor_tensor(out=wo_lo, in0=wo_st, scalar=W_SCALE, in1=wo_hi,
                                   op0=ALU.mult, op1=ALU.subtract).then_inc(w_lo, 1)
            n = 0
            for step in range(STEPS):
                b, g = divmod(step, NG)
                if g == 3 and b + 1 < B:
                    max_T(b + 1)
                if step + AHEAD < STEPS:
                    maxima(*divmod(step + AHEAD, NG))
                if g == 2 and b + 1 < B:
                    negate(b + 1)
                if step >= 1:
                    outputs(*divmod(step - 1, NG))
                if b + 2 < B:
                    tt = TB * (b + 2)
                    if g == 0:
                        proj_lo(tt)
                    elif g == 1:
                        stacks(tt)
                        proj_lo(tt + 1)
                    elif g == 2:
                        stacks(tt + 1)
                if b >= 1:
                    if g == 0:
                        o_lo(b - 1)
                    elif g == 2:
                        residual(b - 1)
                    elif g == 3:
                        norm1(b - 1)
                if step >= 1 and n < ATT_CHUNKS:
                    split_lo(n)
                    n += 1
                if step == NG - 1:
                    slots(NT, 0)
            outputs(B - 1, NG - 1)
            o_lo(B - 1)
            residual(B - 1)
            norm1(B - 1)

            inv = 1 / W_SCALE
            for s in range(NS + 6):
                if s < NS:
                    dve.wait_ge(a2hi, s + 1)
                    v.tensor_tensor(a_lo[s % 2], ps[:, s % 2, 0:D].rearrange("p (k t) -> p k t", k=NK),
                                    a_hi[s % 2], ALU.subtract).then_inc(a2lo, 1)
                i = s - 1
                if 0 <= i < NS:
                    dve.wait_ge(sg2, i + 1)
                    if i >= 1:
                        dve.wait_ge(h2T, i)
                    v.scalar_tensor_tensor(out=hh[:, 0:D], in0=ps[:, 2, 0:D], scalar=inv, in1=sg[:, 0:D],
                                           op0=ALU.mult, op1=ALU.mult).then_inc(h2, 1)
                i = s - 2
                if 0 <= i < NS:
                    dve.wait_ge(h2hi, i + 1)
                    v.tensor_tensor(h_lo[:, 0:NK], ps[:, 3, 0:D].rearrange("p (k t) -> p k t", k=NK),
                                    h_hi[:, 0:NK], ALU.subtract).then_inc(h2lo, 1)
                i = s - 4
                if 0 <= i < NS:
                    dve.wait_ge(rs2, i + 1)
                    v.tensor_scalar(X2[:, i, 0:D], res[i % 2], mv[:, i % 2, 0:1], rstd[:, i % 2:i % 2 + 1],
                                    ALU.subtract, ALU.mult).then_inc(x2_rdy, 1)
                i = s - 3
                if 0 <= i < NS:
                    dve.wait_ge(y2, i + 1)
                    link(v.scalar_tensor_tensor(out=res[i % 2], in0=ps[:, 4, 0:D], scalar=inv, in1=XS[:, i, 0:D],
                                                op0=ALU.mult, op1=ALU.add))
                    r2_at = v.bn_stats(st[:, i % 2, :], res[i % 2])
                    link(r2_at)
                    v.bn_aggr(mv[:, i % 2, :], st[:, i % 2, :]).then_inc(mv2, 1)

            link(v.tensor_scalar(valid[:, :], XS[:, :, D], float(T), None, ALU.is_lt))
            v.tensor_copy(X2[:, :, D:D + 1], XS[:, :, D:D + 1])
            dve.wait_ge(lg_rdy, NS)
            dve.wait_ge(in_r, 32)
            link(v.tensor_tensor(lg[:, :, :], ps[:, 6, 0:NS * E].rearrange("p (i e) -> p i e", e=E),
                                 br_sb[:, :].unsqueeze(1).to_broadcast([P, NS, E]), ALU.add))
            link(v.tensor_reduce(top[:, :], lg[:, :, :], AX.X, ALU.max))
            v.tensor_tensor(lg[:, :, :], lg[:, :, :], top[:, :].unsqueeze(2).to_broadcast([P, NS, E]),
                            ALU.subtract).then_inc(lg_sb, 1)
            dve.wait_ge(lg_sb, 1)
            link(v.tensor_scalar(ohf[:, :, :], lg[:, :, :], 0.0, None, ALU.is_ge))
            link(v.tensor_tensor_scan(where[:, :, :].rearrange("p i e -> p (i e)"),
                                      reset_e[:, :, :].rearrange("p i e -> p (i e)"),
                                      ohf[:, :, :].rearrange("p i e -> p (i e)"), 0.0, ALU.mult, ALU.add))
            link(v.scalar_tensor_tensor(out=ohf[:, :, :], in0=where[:, :, :], scalar=1.0, in1=ohf[:, :, :],
                                        op0=ALU.is_equal, op1=ALU.mult))
            v.tensor_tensor(oh[:, :, :], ohf[:, :, :], valid[:, :].unsqueeze(2).to_broadcast([P, NS, E]),
                            ALU.mult).then_inc(oh_rdy, 1)
            dve.wait_ge(ex_rdy, 1)
            link(v.reduce_sum(top[:, :], ex[:, :, :], AX.X))
            link(v.reciprocal(top[:, :], top[:, :]))
            v.tensor_scalar(X2[:, :, D + 1], top[:, :], inv, None, ALU.mult).then_inc(w_rdy, 1)
            dve.wait_ge(oh_rdy, 2)
            dve.wait_ge(scat2, 16 * NT)
            counts(NS, 1)
            slots(NS, 1)
            while n < NCH:
                split_lo(n)
                n += 1

            def x_lo3(i):
                dve.wait_ge(a3hi, i + 1)
                v.tensor_tensor(a_lo[i % 2], ps[:, 6, 0:D].rearrange("p (k t) -> p k t", k=NK),
                                a_hi[i % 2], ALU.subtract).then_inc(a3lo, 1)

            def gated(i, half):
                dve.wait_ge(sg3, 2 * i + half + 1)
                if i >= 1:
                    dve.wait_ge(h3T, i)
                v.scalar_tensor_tensor(out=hh[:, half * 512:(half + 1) * 512], in0=ps[:, 2 * half + 1, :], scalar=inv,
                                       in1=sg[:, half * 512:(half + 1) * 512],
                                       op0=ALU.mult, op1=ALU.mult).then_inc(h3, 1)

            def h_lo3(i):
                dve.wait_ge(h3hi, i + 1)
                v.tensor_tensor(h_lo, ps[:, 4:6, :].rearrange("p c (k t) -> p (c k) t", t=P), h_hi,
                                ALU.subtract).then_inc(h3lo, 1)

            def last_norm(i):
                dve.wait_ge(y3, i + 1)
                v.tensor_copy(out_i[:, i:i + 1], XS[:, i, D:D + 1])
                link(v.scalar_tensor_tensor(out=res[i % 2], in0=ps[:, 7, 0:D], scalar=XS[:, i, D + 1:D + 2],
                                            in1=XS[:, i, 0:D], op0=ALU.mult, op1=ALU.add))
                link(v.bn_stats(st[:, i % 2, :], res[i % 2]))
                v.bn_aggr(mv[:, i % 2, :], st[:, i % 2, :]).then_inc(mv3, 1)

            def finish(i):
                dve.wait_ge(rs3, i + 1)
                dve.wait_ge(mv3, i + 1)
                if i >= 2:
                    dve.wait_ge(scat_out[i % 2], 16 * (i // 2))
                v.tensor_scalar(fin[i % 2], res[i % 2], mv[:, i % 2, 0:1], rstd[:, i % 2:i % 2 + 1],
                                ALU.subtract, ALU.mult).then_inc(f3, 1)

            x_lo3(0)
            for i in range(NS + 1):
                if i < NS:
                    gated(i, 0)
                if i >= 1:
                    h_lo3(i - 1)
                if i + 1 < NS:
                    x_lo3(i + 1)
                if i < NS:
                    gated(i, 1)
                if i >= 1:
                    last_norm(i - 1)
                    finish(i - 1)

        @block.tensor
        def _(pe):
            t = nc.tensor

            def count(n):
                t.matmul(ps[:, 7, 0:n * E], before[:, :], oh[:, 0:n, :].rearrange("p i e -> p (i e)"),
                         start=True, stop=True)
                t.matmul(ps[:, 7, 256:256 + n * E], ones[:, :], oh[:, 0:n, :].rearrange("p i e -> p (i e)"),
                         start=True, stop=True).then_inc(cnt_rdy, 1)

            def three(dst, x_h, x_l, w_h, w_l, nk, start=True):
                for k in range(nk):
                    for m, (xs, ws) in enumerate(((x_h, w_h), (x_h, w_l), (x_l, w_h))):
                        last = t.matmul(dst, xs(k), ws(k), start=(k == 0 and m == 0), stop=(k == nk - 1 and m == 2))
                return last

            pe.wait_ge(const_r, 1)
            pe.wait_ge(oh_rdy, 1)
            count(NT)

            def qkv(tt):
                tok = slice(tt * P, (tt + 1) * P)
                xh = lambda k: xTv_hi[:, k, tok]
                xl = lambda k: xTv_lo[:, k, tok]
                three(ps[:, bank_qk(tt), :], xh, xl, lambda k: wqkv_hi[:, k, 0:2 * D],
                      lambda k: wqkv_lo[:, k, 0:2 * D], NK).then_inc(proj_qk, 1)
                if tt >= 2 * TB:
                    if tt % TB == 0:
                        pe.wait_ge(maxed, 2 * (NG * (tt // TB - 2) + AHEAD + 1))
                    elif tt // TB == 2:
                        pe.wait_ge(mT_done, 1)
                    else:
                        pe.wait_ge(oT_lo, tt // TB - 2)
                three(ps[:, bank_v(tt), 0:D], xh, xl, lambda k: wqkv_hi[:, k, 2 * D:3 * D],
                      lambda k: wqkv_lo[:, k, 2 * D:3 * D], NK).then_inc(proj_v, 1)

            def stack_T(tt):
                j = tt % 2
                pe.wait_ge(qkv_lo, 3 * tt + 3)
                for a in range(PAIRS):
                    last = t.transpose(ps16(bank_kT(tt))[:, a * P:(a + 1) * P],
                                       Ks[j][:, 2 * a:2 * a + 2].rearrange("p h s c -> p (h s c)"), identH[:, :])
                last.then_inc(kT_rdy, 1)
                if tt >= 2 * TB:
                    pe.wait_ge(maxed, 2 * (NG * (tt // TB - 2) + 1 + tt % 2 + AHEAD + 1))
                for a in range(PAIRS):
                    last = t.transpose(ps16(bank_qT(tt))[:, a * P:(a + 1) * P],
                                       Qs[j][:, 2 * a:2 * a + 2].rearrange("p h s c -> p (h s c)"), identH[:, :])
                last.then_inc(qT_rdy, 1)

            def scores(b, g):
                n = NG * b + g
                q, k = QT[b % 3], KT[b % 3]
                step = n - AHEAD
                sb_, sg_ = divmod(step, NG)
                if step >= 0 and sb_ + 2 < B and sg_ > 0:
                    tt = TB * (sb_ + 2)
                    if sg_ == 1:
                        pe.wait_ge(qkv_lo, 3 * tt + 3)
                    elif sg_ == 2:
                        pe.wait_ge(kT_done, tt + 1)
                        pe.wait_ge(q_even, tt + 1)
                        pe.wait_ge(q_odd, tt + 1)
                        pe.wait_ge(qkv_lo, 3 * tt + 6)
                if g == 0:
                    pe.wait_ge(kT_done, TB * (b + 1))
                    pe.wait_ge(q_even, TB * (b + 1))
                    pe.wait_ge(q_odd, TB * (b + 1))
                elif step >= 0 and sb_ + 2 < B and sg_ == 3:
                    raise AssertionError
                if n >= 1:
                    pe.wait_ge(maxed, 2 * n - 1)
                for bank, qt, kt in ((0, 0, 0), (1, 1, 0), (2, 1, 1)):
                    if bank == 1 and n >= 1:
                        pe.wait_ge(maxed, 2 * n)
                    diag = qt == kt
                    if diag:
                        t.matmul(ps[:, bank, :], identB[:, :], maskS[:, :, :].rearrange("p a k -> p (a k)"),
                                 start=True, stop=False)
                    for i in range(G):
                        h = G * g + i
                        last = t.matmul(ps[:, bank, i * P:(i + 1) * P], q[:, h, qt * P:(qt + 1) * P],
                                        k[:, h // 2, kt * P:(kt + 1) * P], start=not diag,
                                        stop=(not diag) or i == G - 1)
                    if bank != 1:
                        last.then_inc(s_rdy, 1)

            def max_rows(b):
                pe.wait_ge(m_neg, b + 1)
                if b == 1:
                    pe.wait_ge(qkv_lo, 3 * (2 * TB + 2))
                elif b >= 2:
                    pe.wait_ge(res1, TB * (b - 1))
                for qt in range(TB):
                    last = t.transpose(ps16(7, slice(0, 4 * PAIRS))[:, qt * P:(qt + 1) * P],
                                       Mn[:, 2 * qt:2 * qt + 2].rearrange("p r s a -> p (r s a)"), identH[:, :])
                last.then_inc(mT_rdy, 1)

            def scores_T(b, g):
                n = NG * b + g
                q, k = QT[b % 3], KT[b % 3]
                if g == 0:
                    pe.wait_ge(m_row, 64 * (b + 1))
                if n >= 1:
                    pe.wait_ge(exped, 2 * n)
                for bank, kt, qt in ((3, 0, 0), (4, 0, 1), (5, 1, 1)):
                    diag = qt == kt
                    if diag:
                        t.matmul(ps[:, bank, :], identB[:, :], maskT[:, :, :].rearrange("p a k -> p (a k)"),
                                 start=True, stop=False)
                    for i in range(G):
                        h = G * g + i
                        last = t.matmul(ps[:, bank, i * P:(i + 1) * P], k[:, h // 2, kt * P:(kt + 1) * P],
                                        q[:, h, qt * P:(qt + 1) * P], start=not diag,
                                        stop=(not diag) or i == G - 1)
                last.then_inc(st_rdy, 1)

            def values(b, g):
                n = NG * b + g
                pe.wait_ge(p_lo, n + 1)
                if n >= 1:
                    pe.wait_ge(o_read, n)
                w = 2 * DK + 1
                for i in range(G):
                    h = G * g + i
                    for qt, parts in ((0, ((0, 0),)), (1, ((1, 0), (2, 1)))):
                        dst = ps[:, 6, (qt * G + i) * w:(qt * G + i + 1) * w]
                        todo = [(p, c, kt) for c, kt in parts for p in (Ph, Pl)]
                        for m, (p, c, kt) in enumerate(todo):
                            last = t.matmul(dst, p[n % 2][:, c, i * P:(i + 1) * P],
                                            Vs[:, (TB * b + kt) % VT, h, 0:w],
                                            start=m == 0, stop=m == len(todo) - 1)
                last.then_inc(av_rdy, 1)

            def out_T(b):
                pe.wait_ge(o_norm, NG * (b + 1))
                pe.wait_ge(mT_done, min(b + 2, B))
                if b == B - 1:
                    pe.wait_ge(res1, TB * b)
                for j in range(TB):
                    for k in range(NK):
                        last = t.transpose(ps[:, 7, j * D + k * P:j * D + (k + 1) * P],
                                           On[:, j, k * P:(k + 1) * P], identF[:, :])
                last.then_inc(oT_rdy, 1)

            def out_project(b):
                pe.wait_ge(oT_lo, b + 1)
                if b == 0:
                    pe.wait_ge(w_lo, NK + 1)
                if b + 3 < B:
                    pe.wait_ge(qkv_lo, 3 * (TB * (b + 3) + 2))
                for j in range(TB):
                    last = three(ps[:, 7, j * D:(j + 1) * D], lambda k: OT_hi[:, j, k], lambda k: OT_lo[:, j, k],
                                 lambda k: wo_hi[:, k], lambda k: wo_lo[:, k], NK)
                    last.then_inc(wo_rdy, 1)

            pe.wait_ge(cnt_sb, 1)
            pe.wait_ge(x_lo, 1)
            pe.wait_ge(w_lo, NK)
            qkv(0)
            qkv(1)
            pe.wait_ge(x_lo, 2)
            qkv(2)
            stack_T(0)
            stack_T(1)
            qkv(3)
            pe.wait_ge(const_m, 1)
            scores(0, 0)
            stack_T(2)
            scores(0, 1)
            stack_T(3)
            scores(0, 2)
            scores(0, 3)
            max_rows(0)
            scores(1, 0)
            for step in range(STEPS):
                b, g = divmod(step, NG)
                if step == 0:
                    pe.wait_ge(const_m, 2)
                    for e in (kT_done, q_even, q_odd):
                        pe.wait_ge(e, 2 * TB)
                scores_T(b, g)
                if g == 3 and b + 1 < B:
                    max_rows(b + 1)
                if step + AHEAD < STEPS:
                    scores(*divmod(step + AHEAD, NG))
                if step >= 1:
                    values(*divmod(step - 1, NG))
                if b + 2 < B:
                    tt = TB * (b + 2)
                    if g == 0:
                        pe.wait_ge(x_lo, b + 3)
                        pe.wait_ge(maxed, 2 * (step + AHEAD) + 1)
                        qkv(tt)
                    elif g == 1:
                        pe.wait_ge(maxed, 2 * (step + AHEAD) + 1)
                        stack_T(tt)
                        qkv(tt + 1)
                    elif g == 2:
                        pe.wait_ge(maxed, 2 * (step + AHEAD) + 1)
                        stack_T(tt + 1)
                if b >= 1 and g == 0:
                    out_T(b - 1)
                if b >= 1 and g == 2:
                    out_project(b - 1)
            values(B - 1, NG - 1)
            out_T(B - 1)
            out_project(B - 1)

            pe.wait_ge(tile_rdy, 1)
            experts = [pe.value_load(tile_i[0:1, 0, i:i + 1], min_val=0, max_val=E - 1) for i in range(NS)]
            pe.wait_ge(res1, NT)
            for s in range(NS + 7):
                if s < NS:
                    pe.wait_ge(ld2[s], 16)
                    if s >= 2:
                        pe.wait_ge(a2lo, s - 1)
                    for k in range(NK):
                        last = t.transpose(ps[:, s % 2, k * P:(k + 1) * P], XS[:, s, k * P:(k + 1) * P], identF[:, :])
                    last.then_inc(a2T, 1)
                i = s - 1
                if 0 <= i < NS:
                    if i == 0:
                        pe.wait_ge(c_lo, CTX_AT + NCTX)
                    expert = experts[i]
                    pe.wait_ge(a2lo, i + 1)
                    if i >= 1:
                        pe.wait_ge(h2, i)
                    three(ps[:, 2, 0:D], lambda k: a_hi[i % 2][:, k], lambda k: a_lo[i % 2][:, k],
                          lambda k: ctx_hi[:, bass.ds(expert * (NK * D) + k * D, D)],
                          lambda k: ctx_lo[:, bass.ds(expert * (NK * D) + k * D, D)], NK).then_inc(z_rdy, 1)
                i = s - 2
                if 0 <= i < NS:
                    pe.wait_ge(h2, i + 1)
                    if i >= 1:
                        pe.wait_ge(h2lo, i)
                    for k in range(NK):
                        last = t.transpose(ps[:, 3, k * P:(k + 1) * P], hh[:, k * P:(k + 1) * P], identF[:, :])
                    last.then_inc(h2T, 1)
                i = s - 3
                if 0 <= i < NS:
                    expert = experts[i]
                    pe.wait_ge(h2lo, i + 1)
                    if i >= 1:
                        pe.wait_ge(mv2, i)
                    three(ps[:, 4, 0:D], lambda k: h_hi[:, k], lambda k: h_lo[:, k],
                          lambda k: ctx_hi[:, bass.ds(expert * (NK * D) + k * D, D)],
                          lambda k: ctx_lo[:, bass.ds(expert * (NK * D) + k * D, D)], NK).then_inc(y2, 1)
                i = s - 5
                if 0 <= i < NS:
                    pe.wait_ge(x2_rdy, i + 1)
                    if i >= 1:
                        pe.wait_ge(x2T_sb, i)
                    for k in range(NK):
                        last = t.transpose(ps[:, 5, k * P:(k + 1) * P], X2[:, i, k * P:(k + 1) * P], identF[:, :])
                    last.then_inc(x2T_rdy, 1)
                i = s - 6
                if 0 <= i < NS:
                    if i == 0:
                        pe.wait_ge(in_r, 32)
                    pe.wait_ge(x2T_sb, i + 1)
                    for k in range(NK):
                        last = t.matmul(ps[:, 6, i * E:(i + 1) * E], x2T[:, k], wr_sb[:, k, :],
                                        start=(k == 0), stop=(k == NK - 1))
                    last.then_inc(lg_rdy, 1)
            pe.wait_ge(oh_rdy, 2)
            count(NS)

            def x_T3(i):
                pe.wait_ge(ld3[i], 16)
                if i >= 1:
                    pe.wait_ge(a3lo, i)
                else:
                    pe.wait_ge(lg_sb, 1)
                for k in range(NK):
                    last = t.transpose(ps[:, 6, k * P:(k + 1) * P], XS[:, i, k * P:(k + 1) * P], identF[:, :])
                last.then_inc(a3T, 1)

            def gate_up(i, half, expert):
                for n in range(2):
                    for k in range(NK):
                        pass
                    at_ = lambda k, n=n: expert * EW + (n * NK + k) * F + half * 512
                    last = three(ps[:, 2 * half + n, :], lambda k: a_hi[i % 2][:, k], lambda k: a_lo[i % 2][:, k],
                                 lambda k: wf_hi[:, bass.ds(at_(k), 512)],
                                 lambda k: wf_lo[:, bass.ds(at_(k), 512)], NK)
                last.then_inc((gu_a, gu_b)[half], 1)

            def h_T3(i):
                pe.wait_ge(h3, 2 * i + 2)
                if i >= 1:
                    pe.wait_ge(h3lo, i)
                for k in range(NF):
                    last = t.transpose(ps[:, 4 + k // 4, (k % 4) * P:(k % 4 + 1) * P], hh[:, k * P:(k + 1) * P],
                                       identF[:, :])
                last.then_inc(h3T, 1)

            def down(i, expert):
                pe.wait_ge(h3lo, i + 1)
                if i >= 1:
                    pe.wait_ge(mv3, i)
                three(ps[:, 7, 0:D], lambda k: h_hi[:, k], lambda k: h_lo[:, k],
                      lambda k: wf_hi[:, bass.ds(expert * EW + DOWN + k * D, D)],
                      lambda k: wf_lo[:, bass.ds(expert * EW + DOWN + k * D, D)], NF).then_inc(y3, 1)

            pe.wait_ge(tile_rdy, 2)
            pe.wait_ge(c_lo, NCH)
            x_T3(0)
            before_e = None
            for i in range(NS + 1):
                if i < NS:
                    expert = pe.value_load(tile_i[0:1, 1, i:i + 1], min_val=0, max_val=E - 1)
                    pe.wait_ge(a3lo, i + 1)
                    if i >= 1:
                        pe.wait_ge(h3, 2 * i)
                    gate_up(i, 0, expert)
                if i >= 1:
                    h_T3(i - 1)
                if i + 1 < NS:
                    x_T3(i + 1)
                if i < NS:
                    gate_up(i, 1, expert)
                if i >= 1:
                    down(i - 1, before_e)
                before_e = expert


def kernel(x, itok_BxS_13_99985, ctx_2048, L0_attn_q_proj, L0_attn_k_proj, L0_attn_v_proj, L0_attn_o_proj,
           L0_ffn_Wr, L0_ffn_br, L0_ffn_Wg, L0_ffn_Wu, L0_ffn_Wd):
    import concourse.bacc as bacc
    from concourse.bass_utils import run_bass_kernel_spmd

    def chunked(w):
        w = np.asarray(w)
        return w.reshape(-1, P, w.shape[-1]).transpose(1, 0, 2)

    x = np.asarray(x)
    xf = x.reshape(T, D)
    wqkv = np.concatenate([np.asarray(w).T for w in (L0_attn_q_proj, L0_attn_k_proj, L0_attn_v_proj)], axis=1)
    ctx_e = [chunked(np.asarray(ctx_2048)[e].T).reshape(P, -1) for e in range(E)]
    wf = [np.concatenate([chunked(np.asarray(w)[e]).reshape(P, -1) for w in (L0_ffn_Wg, L0_ffn_Wu, L0_ffn_Wd)],
                         axis=1) for e in range(E)]
    arrays = {
        "x_tok": chunked(xf),
        "xT": chunked(xf.T),
        "ids": np.asarray(itok_BxS_13_99985).reshape(NT, P).T,
        "wqkvT": chunked(wqkv),
        "woT": chunked(np.asarray(L0_attn_o_proj).T),
        "ctxT": np.concatenate(ctx_e, axis=1),
        "Wr": chunked(L0_ffn_Wr),
        "br": np.asarray(L0_ffn_br),
        "Wf": np.concatenate(wf, axis=1),
    }
    arrays = {k: np.ascontiguousarray(a) for k, a in arrays.items()}
    nc = bacc.Bacc("TRN2", target_bir_lowering=False, num_devices=1)
    args = [nc.dram_tensor(k, a.shape, mybir.dt.from_np(a.dtype), kind="ExternalInput").ap()
            for k, a in arrays.items()]
    out = nc.dram_tensor("out", (T, D), F32, kind="ExternalOutput").ap()
    build(nc, *args, out)
    r = run_bass_kernel_spmd(nc, [arrays], core_ids=[0])
    return r.results[0]["out"].reshape(B, S, D)
```

```python
from contextlib import ExitStack

import numpy as np
import concourse.bass as bass
import concourse.mybir as mybir

F32, F16, BF16, I32 = mybir.dt.float32, mybir.dt.float16, mybir.dt.bfloat16, mybir.dt.int32
ALU, ACT, AX = mybir.AluOpType, mybir.ActivationFunctionType, mybir.AxisListType

P = 128
B, S, D = 4, 256, 256
H, DK = 16, 16
E, F = 4, 1024
T = B * S
NT = T // P
TB = S // P
NK = D // P
NF = F // P
NS = NT + E - 1
G = 4
NG = H // G
PAIRS = H // 2
STEPS = B * NG
AHEAD = NG + 1
SLOT = 64
ROW = D + 2
VOCAB_PART = 12500 // E
W_SCALE = 256.0
EPS = 1e-5
NEG = -3.0e38
PAD_TOKEN = 4096.0
NOWHERE = 8192.0
PARTS = ((0, 7), (7, NS))
PART_BANK = (6, 1)
PEEL = 4
LOOPS = (NS - 1 - PEEL) // 2
assert PEEL + 2 * LOOPS + 1 == NS
NR3 = (E - 1) * T + NS * P
CH = 1024
NCTX = E * NK * D // CH
EW = 2 * NK * F + NF * D
NCH = NCTX + E * EW // CH
RING = 4
LATE = 7
LAST = 5
WARM_START, WARM_GAP, WARM_END = 30, 8, 5
DOWN = 2 * NK * F


def build(nc, x_tok, xT, ids, wqkvT, woT, ctxT, Wr, br, Wf, out):
    ctx = ExitStack()
    with ctx:
        def sb(name, shape, dt):
            return ctx.enter_context(nc.sbuf_tensor(name, shape, dt))

        def sem(name):
            return ctx.enter_context(nc.semaphore(name))

        wf_hi = sb("wf_hi", [P, E * EW], F16)
        wf_lo = sb("wf_lo", [P, E * EW], F16)
        ring = sb("ring", [P, RING * CH], F32)
        xT_hi = sb("xT_hi", [P, NK * T], F16)
        xT_lo = sb("xT_lo", [P, NK * T], F16)
        ctx_hi, ctx_lo = xT_hi, xT_lo
        X1 = sb("X1", [P, NT, ROW], F32)
        identF = sb("identF", [P, P], F32)
        identH = sb("identH", [P, P], F16)
        identB = sb("identB", [P, P], BF16)
        before = sb("before", [P, P], F16)
        ones = sb("ones", [P, P], F16)
        maskS = sb("maskS", [P, G, P], BF16)
        maskT = sb("maskT", [P, G, P], BF16)
        fill = sb("fill", [P, ROW], F32)
        steps = sb("steps", [P, NS], F32)
        region = sb("region", [P, E], F32)
        tiles = sb("tiles", [P, NS], F32)
        reset = sb("reset", [P, E, NS], F32)
        reset_e = sb("reset_e", [P, NS, E], F32)
        cum = sb("cum", [P, NS, E], F32)
        minus_half = sb("minus_half", [P, NS], F32)
        ids_sb = sb("ids_sb", [P, NT], I32)
        ge = sb("ge", [P, E + 1, NT], F32)
        oh = sb("oh", [P, NS, E], F16)
        cnt = sb("cnt", [P, E, NS], F32)
        run = sb("run", [P, E, NS], F32)
        over = sb("over", [P, E, NT], F32)
        nt_e = sb("nt_e", [P, E], F32)
        end_e = sb("end_e", [P, E], F32)
        base_e = sb("base_e", [P, E], F32)
        where = sb("where", [P, NS, E], F32)
        pos = sb("pos", [P, NS], F32)
        pos_i = sb("pos_i", [P, NS], I32)
        tile_ge = sb("tile_ge", [P, NS, E - 1], F32)
        tile_e = sb("tile_e", [P, NS], F32)
        tile_i = sb("tile_i", [P, 2, NS], I32)
        wr_sb = sb("wr_sb", [P, NK, E], F32)
        br_sb = sb("br_sb", [P, E], F32)
        lg = sb("lg", [P, NS, E], F32)
        ex = sb("ex", [P, NS, E], F32)
        ohf = sb("ohf", [P, NS, E], F32)
        top = sb("top", [P, NS], F32)
        valid = sb("valid", [P, NS], F32)
        off = sb("off", [P, NS], F32)
        jump = sb("jump", [P, E], F32)
        tile_row = sb("tile_row", [P, NS], F32)
        row_i = sb("row_i", [P, NS], I32)
        out_i = sb("out_i", [P, 2], I32)
        st = sb("st", [P, 2, 6], F32)
        mv = sb("mv", [P, 2, 2], F32)
        veps = sb("veps", [P, 2], F32)
        rstd = sb("rstd", [P, 2], F32)

        ARENA = 73504
        arena = sb("arena", [P, ARENA // 4], F32)
        at = [0]

        def carve(shape, dt):
            n = int(np.prod(shape))
            size = n * (4 if dt in (F32, I32) else 2)
            a = arena[:, at[0] // 4:(at[0] + size) // 4]
            at[0] += size
            assert at[0] <= ARENA, at[0]
            if dt != F32:
                a = a.bitcast(dt)
            names = "abcd"[:len(shape)]
            return a.rearrange(f"p ({' '.join(names)}) -> p {' '.join(names)}", **dict(zip(names, shape)))

        wqkv_hi = carve([NK, 3 * D], F16)
        wqkv_lo = carve([NK, 3 * D], F16)
        wo_hi = carve([NK, D], F16)
        wo_lo = carve([NK, D], F16)
        QT = [carve([H, S], F16) for _ in range(2)]
        KT = [carve([PAIRS, S], F16) for _ in range(2)]
        tail = E * EW - (H + PAIRS) * S
        QT.append(wf_hi[:, tail:tail + H * S].rearrange("p (h t) -> p h t", h=H))
        KT.append(wf_hi[:, tail + H * S:].rearrange("p (h t) -> p h t", h=PAIRS))
        Qs = [carve([H, 4, DK], F16) for _ in range(2)]
        Ks = [carve([H, 4, DK], F16) for _ in range(2)]
        Vs = carve([NT, H, 2 * DK + 2], F16)
        Pf = carve([3, G * P], F32)
        Ph = [carve([3, G * P], F16) for _ in range(2)]
        Pl = [carve([3, G * P], F16) for _ in range(2)]
        On = carve([TB, D], F32)
        Oa = carve([TB * G, DK], F32)
        Or = carve([TB * G], F32)
        OT_hi = carve([TB, NK, P], F16)
        OT_lo = carve([TB, NK, P], F16)
        Mx = carve([TB, 2, PAIRS], F32)
        Mn = carve([TB * 2, 2, PAIRS], F16)
        mT = carve([S], F16)
        at[0] = 0
        XS = carve([NS, ROW], F32)
        X2 = carve([NS, ROW], F32)
        a_hi = [carve([NK, P], F16) for _ in range(2)]
        a_lo = [carve([NK, P], F16) for _ in range(2)]
        sg = carve([F], F32)
        hh = carve([F], F32)
        h_hi = carve([NF, P], F16)
        h_lo = carve([NF, P], F16)
        x2T = carve([NK, P], F32)
        xrow = carve([D], F32)
        res = [carve([D], F32) for _ in range(2)]
        fin = [carve([D], F32) for _ in range(2)]
        late = [carve([CH], F32) for _ in range(LATE)]

        ps = ctx.enter_context(nc.psum_tensor("ps", [P, 8, 512], F32))

        def ps16(k, rows=slice(0, P)):
            return ps[rows, k, :].bitcast(F16)

        sorted2 = nc.dram_tensor("sorted2", [NS * P, ROW], F32, kind="Internal").ap()
        sorted3 = nc.dram_tensor("sorted3", [NR3, ROW], F32, kind="Internal").ap()

        in_ids, in_wo, in_xtok, in_r = (sem(n) for n in ("in_ids", "in_wo", "in_xtok", "in_r"))
        in_wqkv = [sem(f"in_wqkv{k}") for k in range(NK)]
        in_xT = [sem(f"in_xT{b}") for b in range(B)]
        in_ch = [sem(f"in_ch{r}") for r in range(RING)]
        in_late = [sem(f"in_late{r}") for r in range(LATE)]
        const_z, const_r, const_s, const_m, const_q2, fillrow = (sem(n) for n in (
            "const_z", "const_r", "const_s", "const_m", "const_q2", "fillrow"))
        filled = sem("filled")
        w_hi, w_lo, x_hi, x_lo, c_hi, c_lo = (sem(n) for n in ("w_hi", "w_lo", "x_hi", "x_lo", "c_hi", "c_lo"))
        proj_qk, proj_v, qkv_hi, qkv_lo = (sem(n) for n in ("proj_qk", "proj_v", "qkv_hi", "qkv_lo"))
        kT_rdy, qT_rdy, kT_done, q_even, q_odd = (sem(n) for n in ("kT_rdy", "qT_rdy", "kT_done", "q_even", "q_odd"))
        s_rdy, maxed, m_neg, mT_rdy, mT_done, m_row = (sem(n) for n in (
            "s_rdy", "maxed", "m_neg", "mT_rdy", "mT_done", "m_row"))
        st_rdy, exped, p_lo, av_rdy, o_read, o_norm = (sem(n) for n in (
            "st_rdy", "exped", "p_lo", "av_rdy", "o_read", "o_norm"))
        oT_rdy, oT_hi, oT_lo, wo_rdy, res1, bn1, mv1, rs1, x1_rdy = (sem(n) for n in (
            "oT_rdy", "oT_hi", "oT_lo", "wo_rdy", "res1", "bn1", "mv1", "rs1", "x1_rdy"))
        link_v, link_g = sem("link_v"), sem("link_g")
        oh_rdy, cnt_rdy, cnt_sb, pos_rdy, tile_rdy = (sem(n) for n in ("oh_rdy", "cnt_rdy", "cnt_sb", "pos_rdy", "tile_rdy"))
        scat2, scat3 = sem("scat2"), sem("scat3")
        scat_out = [sem(f"scat_out{i}") for i in range(2)]
        ld2 = [sem(f"ld2_{i}") for i in range(NS)]
        ld3 = [sem(f"ld3_{i}") for i in range(PEEL + 2)]
        a2T, a2hi, a2lo, z_rdy, sg2, h2, h2T, h2hi, h2lo, y2, r2, bn2, mv2, rs2, x2_rdy, x2T_rdy, x2T_sb, lg_rdy = (
            sem(n) for n in ("a2T", "a2hi", "a2lo", "z_rdy", "sg2", "h2", "h2T", "h2hi", "h2lo", "y2", "r2", "bn2", "mv2",
                             "rs2", "x2_rdy", "x2T_rdy", "x2T_sb", "lg_rdy"))
        lg_sb, ex_rdy, w_rdy, row_rdy = (sem(n) for n in ("lg_sb", "ex_rdy", "w_rdy", "row_rdy"))
        p_lo_last = sem("p_lo_last")
        endT, end_hi, end_lo = sem("endT"), sem("end_hi"), sem("end_lo")
        a3T, a3hi, a3lo, gu_a, gu_b, sg3, h3, h3T, h3hi, h3lo, y3, r3, bn3, mv3, ve3, xrow_rdy, rs3, f3 = (
            sem(n) for n in ("a3T", "a3hi", "a3lo", "gu_a", "gu_b", "sg3", "h3", "h3T", "h3hi", "h3lo", "y3",
                             "r3", "bn3", "mv3", "ve3", "xrow_rdy", "rs3", "f3"))

        def bank_qk(tt):
            return (0, 2, 3, 5)[tt] if tt < 2 * TB else 0

        def bank_v(tt):
            return (1, 7, 4, 6)[tt] if tt < 2 * TB else 7

        bank_kT, bank_qT = bank_qk, bank_v

        def bank_mT(b):
            return 7 if b == 0 else 6

        def stacked_at(step):
            return 2 * TB + step // 2 if step % 2 == 0 and 2 * TB + step // 2 < NT else None

        def projected_at(step):
            return 2 * TB + (step + 1) // 2 if step % 2 == 1 and 2 * TB + (step + 1) // 2 < NT else None

        def chunk_dst(c, hi):
            if c < NCTX:
                return (ctx_hi if hi else ctx_lo)[:, c * CH:(c + 1) * CH]
            c -= NCTX
            return (wf_hi if hi else wf_lo)[:, c * CH:(c + 1) * CH]

        def chunk_src(c):
            return ring[:, (c % RING) * CH:(c % RING + 1) * CH]

        xT_st = ring[:, 0:NK * T].rearrange("p (k t) -> p k t", k=NK)
        wqkv_st = ring[:, NK * T:NK * (T + 3 * D)].rearrange("p (k n) -> p k n", k=NK)
        wo_st = ring[:, NK * (T + 3 * D):NK * (T + 4 * D)].rearrange("p (k n) -> p k n", k=NK)
        xTv_hi = xT_hi[:, :].rearrange("p (k t) -> p k t", k=NK)
        xTv_lo = xT_lo[:, :].rearrange("p (k t) -> p k t", k=NK)

        ATT_CHUNKS = NCH - LATE - RING
        CTX_AT = 8
        ORDER = list(range(NCTX, NCH))
        ORDER = ORDER[:CTX_AT] + list(range(NCTX)) + ORDER[CTX_AT:]

        def staged(n):
            if n >= NCH - LATE:
                return late[n - (NCH - LATE)], in_late[n - (NCH - LATE)], 16
            r = n % RING
            return ring[:, r * CH:(r + 1) * CH], in_ch[r], 16 * (n // RING + 1)

        block = ctx.enter_context(nc.Block())

        @block.sync
        def _(sp):
            sp.dma_start(ids_sb[:, :], ids).then_inc(in_ids, 16)
            sp.dma_start(xT_st[:, :, 0:S], xT[:, :, 0:S]).then_inc(in_xT[0], 16)
            for k in range(NK):
                sp.dma_start(wqkv_st[:, k], wqkvT[:, k]).then_inc(in_wqkv[k], 16)
            for b in range(1, B):
                sp.dma_start(xT_st[:, :, b * S:(b + 1) * S], xT[:, :, b * S:(b + 1) * S]).then_inc(in_xT[b], 16)
            sp.dma_start(wo_st, woT).then_inc(in_wo, 16)
            sp.dma_start(X1[:, :, 0:D], x_tok).then_inc(in_xtok, 16)
            sp.dma_start(wr_sb[:, :, :], Wr).then_inc(in_r, 16)
            sp.dma_start(br_sb[:, :], br.partition_broadcast(P)).then_inc(in_r, 16)
            sp.wait_ge(fillrow, 1)
            for scratch, rows in ((sorted2, NS * P), (sorted3, NR3)):
                sp.dma_start(scratch.rearrange("(n p) d -> p n d", p=P),
                             fill[:, :].unsqueeze(1).to_broadcast([P, rows // P, ROW])).then_inc(filled, 16)

            def load(n):
                if n < RING:
                    if n * CH < NK * T:
                        sp.wait_ge(x_lo, B)
                    else:
                        sp.wait_ge(w_lo, NK + 1)
                elif n >= NCH - LATE:
                    sp.wait_ge(res1, NT)
                else:
                    sp.wait_ge(c_lo, n - RING + 1)
                c = ORDER[n]
                src = (ctxT[:, c * CH:(c + 1) * CH] if c < NCTX else
                       Wf[:, (c - NCTX) * CH:(c - NCTX + 1) * CH])
                dst, arrived, _ = staged(n)
                sp.dma_start(dst, src).then_inc(arrived, 16)

            def max_rows(b):
                sp.wait_ge(mT_done, b + 1)
                for par in range(2):
                    row = par * SLOT + 3 * DK
                    src = par * 2 * PAIRS
                    sp.dma_start(QT[b % 3][row:row + 2, par::2, :],
                                 mT[src:src + 2 * PAIRS, :]).then_inc(m_row, 16)

            max_rows(0)
            n = 0
            for step in range(STEPS):
                if step % NG == NG - 2 and step + 2 < STEPS:
                    max_rows(step // NG + 1)
                while n < min(step + RING, NCH - LATE):
                    load(n)
                    n += 1
            while n < NCH - LAST:
                load(n)
                n += 1
            sp.wait_ge(scat2, 16 * NT)
            for i in range(NS):
                sp.dma_start(XS[:, i, :], sorted2[i * P:(i + 1) * P, :]).then_inc(ld2[i], 16)
            while n < NCH:
                load(n)
                n += 1
            sp.wait_ge(row_rdy, 1)
            for i in range(NS):
                row = sp.value_load(row_i[0:1, i:i + 1], min_val=0, max_val=NR3 - P)
                if i == 0:
                    sp.wait_ge(scat3, 16 * NS)
                sp.dma_start(XS[:, i, :], sorted3[bass.ds(row, P), :]).then_inc(ld3[min(i, PEEL + 1)], 16)

        @block.gpsimd
        def _(pool):
            g = nc.gpsimd
            links = [0]

            def link(ins):
                links[0] += 1
                ins.then_inc(link_g, 1)
                pool.wait_ge(link_g, links[0])

            g.iota(tiles[:, :], pattern=[[1, NS]], base=0, channel_multiplier=0,
                   allow_small_or_imprecise_dtypes=True)
            g.iota(steps[:, :], pattern=[[P, NS]], base=0, channel_multiplier=0,
                   allow_small_or_imprecise_dtypes=True)
            g.iota(region[:, :], pattern=[[T, E]], base=0, channel_multiplier=0,
                   allow_small_or_imprecise_dtypes=True)
            g.memset(cnt[:, :, :], 0.0)
            g.memset(reset[:, :, :], 1.0)
            g.memset(reset_e[:, :, :], 1.0)
            g.memset(ones[:, :].bitcast(F32), float(np.array([0x3C003C00], np.uint32).view(np.float32)[0]))
            g.memset(identH[:, :].bitcast(F32), 0.0)
            link(g.memset(before[:, :].bitcast(F32), 0.0))
            g.memset(reset[:, :, 0:1], 0.0)
            g.memset(reset_e[:, :, 0:1], 0.0)
            g.affine_select(out=before[:, :], in_=before[:, :], compare_op=ALU.is_ge, fill=1.0,
                            base=0, pattern=[[-1, P]], channel_multiplier=1).then_inc(const_r, 1)
            for j in range(2):
                g.memset(Qs[j][:, :, 3, :], 0.0)
                g.memset(Ks[j][:, :, 3, :], 0.0)
            link(g.affine_select(out=identH[:, :], in_=identH[:, :], compare_op=ALU.not_equal, fill=1.0,
                                 base=0, pattern=[[-1, P]], channel_multiplier=1))
            for j in range(2):
                last = g.memset(Ks[j][:, :, 3, 0:2], 1.0)
            last.then_inc(const_s, 1)
            g.memset(identB[:, :].bitcast(F32), 0.0)
            g.memset(Vs[:, :, :, 2 * DK:2 * DK + 2], 1.0)
            link(g.memset(maskS[:, :, :].bitcast(F32), 0.0))
            g.affine_select(out=identB[:, :], in_=identB[:, :], compare_op=ALU.not_equal, fill=1.0,
                            base=0, pattern=[[-1, P]], channel_multiplier=1)
            g.affine_select(out=maskS[:, :, :], in_=maskS[:, :, :], compare_op=ALU.is_ge, fill=NEG,
                            base=0, pattern=[[0, G], [-1, P]], channel_multiplier=1).then_inc(const_m, 1)
            g.memset(identF[:, :], 0.0)
            link(g.memset(maskT[:, :, :].bitcast(F32), 0.0))
            g.affine_select(out=identF[:, :], in_=identF[:, :], compare_op=ALU.not_equal, fill=1.0,
                            base=0, pattern=[[-1, P]], channel_multiplier=1)
            g.affine_select(out=maskT[:, :, :], in_=maskT[:, :, :], compare_op=ALU.is_ge, fill=NEG,
                            base=0, pattern=[[0, G], [1, P]], channel_multiplier=-1).then_inc(const_m, 1)
            pool.wait_ge(const_m, 2)
            link(g.memset(QT[2][SLOT:P, 0::2, :].bitcast(F32), 0.0))
            g.memset(QT[2][0:SLOT, 1::2, :].bitcast(F32), 0.0).then_inc(const_q2, 1)
            pool.wait_ge(const_q2, 1)
            link(g.memset(fill[:, :], 0.0))
            g.memset(fill[:, D:D + 1], PAD_TOKEN).then_inc(fillrow, 1)
            g.memset(minus_half[:, :], -0.5)
            g.memset(X1[:, :, D + 1:D + 2], 0.0)
            link(g.iota(X1[:, :, D], pattern=[[P, NT]], base=0, channel_multiplier=1,
                        allow_small_or_imprecise_dtypes=True))

            def inv_std(var, n, out_sem):
                link(g.tensor_scalar(veps[:, 0:n], var, EPS, None, ALU.add))
                g.tensor_tensor(rstd[:, 0:n], veps[:, 0:n], minus_half[:, 0:n], ALU.pow).then_inc(out_sem, 1)

            def scatter2(b):
                for j in range(TB):
                    tt = TB * b + j
                    pool.wait_ge(x1_rdy, tt + 1)
                    g.indirect_dma_start(sorted2[:, :], bass.IndirectOffsetOnAxis(ap=pos_i[:, tt:tt + 1], axis=0),
                                         X1[:, tt, :], None, bounds_check=NS * P - 1,
                                         oob_is_err=False).then_inc(scat2, 16)

            for n in range(STEPS):
                b, gr = divmod(n, NG)
                if gr == 0 and b >= 2:
                    pool.wait_ge(mv1, TB * (b - 1))
                    inv_std(mv[:, :, 1], TB, rs1)
                pool.wait_ge(exped, 2 * n + 2)
                if n >= 2:
                    pool.wait_ge(av_rdy, n - 1)
                c = slice(0, 3 if n < STEPS - 1 else 1)
                g.tensor_tensor(Pl[n % 2][:, c], Pf[:, c], Ph[n % 2][:, c], ALU.subtract).then_inc(p_lo, 1)
                if n >= 3 * NG + 1 and n - 3 * NG - 1 < B - 2:
                    if n == 3 * NG + 1:
                        pool.wait_ge(filled, 32)
                        pool.wait_ge(pos_rdy, 1)
                    scatter2(n - 3 * NG - 1)
            pool.wait_ge(mv1, NT - TB)
            inv_std(mv[:, :, 1], TB, rs1)
            scatter2(B - 2)
            pool.wait_ge(mv1, NT)
            inv_std(mv[:, :, 1], TB, rs1)
            scatter2(B - 1)
            for i in range(NS):
                pool.wait_ge(mv2, i + 1)
                link(g.tensor_scalar(veps[:, i % 2:i % 2 + 1], mv[:, i % 2, 1:2], EPS, None, ALU.add))
                g.tensor_tensor(rstd[:, i % 2:i % 2 + 1], veps[:, i % 2:i % 2 + 1], minus_half[:, 0:1],
                                ALU.pow).then_inc(rs2, 1)
            for part, (first, last) in enumerate(PARTS):
                pool.wait_ge(pos_rdy, part + 2)
                pool.wait_ge(w_rdy, part + 1)
                for i in range(first, last):
                    g.indirect_dma_start(sorted3[:, :], bass.IndirectOffsetOnAxis(ap=pos_i[:, i:i + 1], axis=0),
                                         X2[:, i, :], None, bounds_check=NR3 - 1,
                                         oob_is_err=False).then_inc(scat3, 16)
            def back(i, p):
                pool.wait_ge(mv3, i + 1)
                g.tensor_scalar(veps[:, p:p + 1], mv[:, p, 1:2], EPS, None, ALU.add).then_inc(ve3, 1)
                pool.wait_ge(ve3, i + 1)
                g.tensor_tensor(rstd[:, p:p + 1], veps[:, p:p + 1], minus_half[:, 0:1], ALU.pow).then_inc(rs3, 1)
                pool.wait_ge(f3, i + 1)
                g.indirect_dma_start(out, bass.IndirectOffsetOnAxis(ap=out_i[:, p:p + 1], axis=0),
                                     fin[p], None, bounds_check=T - 1,
                                     oob_is_err=False).then_inc(scat_out[p], 16)

            for i in range(NS):
                back(i, i % 2)
            for i in range(2):
                pool.wait_ge(scat_out[i], 16 * ((NS + 1 - i) // 2))

        @block.scalar
        def _(act):
            a = nc.scalar

            def split_hi(n):
                src, arrived, value = staged(n)
                act.wait_ge(arrived, value)
                if ORDER[n] < NCTX:
                    act.wait_ge(proj_v, NT)
                a.activation(chunk_dst(ORDER[n], True), src, ACT.Copy, scale=W_SCALE).then_inc(c_hi, 1)

            def x_split(b):
                act.wait_ge(in_xT[b], 16)
                a.activation(xTv_hi[:, :, b * S:(b + 1) * S], xT_st[:, :, b * S:(b + 1) * S],
                             ACT.Copy).then_inc(x_hi, 1)

            def proj_hi(tt):
                j = tt % 2
                act.wait_ge(proj_qk, tt + 1)
                if tt >= 2:
                    act.wait_ge(kT_rdy, tt - 1)
                    act.wait_ge(qT_rdy, tt - 1)
                else:
                    act.wait_ge(const_s, 1)
                qk = ps[:, bank_qk(tt), :].rearrange("p (s h c) -> p s h c", s=2, h=H)
                rep = [P, H, 2, DK]
                a.activation(Ks[j][:, :, 0:3:2, :], qk[:, 1].unsqueeze(2).to_broadcast(rep), ACT.Copy,
                             scale=1 / W_SCALE).then_inc(qkv_hi, 1)
                a.activation(Qs[j][:, :, 0:2, :], qk[:, 0].unsqueeze(2).to_broadcast(rep), ACT.Copy,
                             scale=1 / W_SCALE).then_inc(qkv_hi, 1)
                act.wait_ge(proj_v, tt + 1)
                a.activation(Vs[:, tt, :, 0:DK],
                             ps[:, bank_v(tt), 0:D].rearrange("p (h c) -> p h c", h=H), ACT.Copy,
                             scale=1 / W_SCALE).then_inc(qkv_hi, 1)

            def q_odds(tt):
                b, j = divmod(tt, TB)
                act.wait_ge(qT_rdy, tt + 1)
                a.activation(QT[b % 3][SLOT:P, 1::2, j * P:(j + 1) * P],
                             ps16(bank_qT(tt), slice(SLOT, P)).rearrange("p (h t) -> p h t", h=PAIRS),
                             ACT.Copy).then_inc(q_odd, 1)

            x_split(0)
            for k in range(NK):
                act.wait_ge(in_wqkv[k], 16)
                a.activation(wqkv_hi[:, k], wqkv_st[:, k], ACT.Copy, scale=W_SCALE).then_inc(w_hi, 1)
            x_split(1)

            def exps(b, g):
                n = NG * b + g
                act.wait_ge(st_rdy, n + 1)
                if n >= 2:
                    act.wait_ge(av_rdy, n - 1)
                a.activation(Ph[n % 2], ps[:, 3:6, :], ACT.Exp, scale=DK ** -0.5).then_inc(exped, 1)
                if g == 1 and b >= 1:
                    o_hi(b - 1)
                if n >= 1:
                    act.wait_ge(p_lo, n)
                a.activation(Pf, ps[:, 3:6, :], ACT.Exp, scale=DK ** -0.5).then_inc(exped, 1)

            def o_hi(b):
                act.wait_ge(oT_rdy, b + 1)
                if b >= 1:
                    act.wait_ge(wo_rdy, TB * b)
                a.activation(OT_hi, ps[:, 7, :].rearrange("p (j k t) -> p j k t", j=TB, k=NK),
                             ACT.Copy).then_inc(oT_hi, 1)

            proj_hi(0)
            proj_hi(1)
            q_odds(0)
            q_odds(1)
            proj_hi(2)
            proj_hi(3)
            q_odds(2)
            q_odds(3)
            x_split(2)
            x_split(3)
            act.wait_ge(in_wo, 16)
            a.activation(wo_hi, wo_st, ACT.Copy, scale=W_SCALE).then_inc(w_hi, 1)
            n = 0
            for step in range(STEPS):
                b, g = divmod(step, NG)
                if step != 1:
                    exps(b, g)
                if step == 0:
                    proj_hi(2 * TB)
                    exps(0, 1)
                if stacked_at(step) is not None:
                    q_odds(stacked_at(step))
                if step >= 1 and n < ATT_CHUNKS:
                    split_hi(n)
                    n += 1
                if projected_at(step) is not None:
                    proj_hi(projected_at(step))
            o_hi(B - 1)

            def exps_router(part):
                first, last = PARTS[part]
                act.wait_ge(lg_sb, part + 1)
                a.activation(ex[:, first:last, :], lg[:, first:last, :], ACT.Exp).then_inc(ex_rdy, 1)

            while n < NCH - LAST:
                split_hi(n)
                n += 1
            for s in range(NS + 6):
                if s >= 3 and s % 2 == 1 and n < NCH:
                    split_hi(n)
                    n += 1
                if s < NS:
                    act.wait_ge(a2T, s + 1)
                    if s >= 2:
                        act.wait_ge(z_rdy, s - 1)
                    a.activation(a_hi[s % 2], ps[:, 0, 0:D].rearrange("p (k t) -> p k t", k=NK),
                                 ACT.Copy).then_inc(a2hi, 1)
                i = s - 1
                if 0 <= i < NS:
                    act.wait_ge(z_rdy, i + 1)
                    if i >= 1:
                        act.wait_ge(h2, i)
                    a.activation(sg[:, 0:D], ps[:, 2, 0:D], ACT.Silu, scale=1 / W_SCALE).then_inc(sg2, 1)
                i = s - 2
                if 0 <= i < NS:
                    act.wait_ge(h2T, i + 1)
                    if i >= 1:
                        act.wait_ge(y2, i)
                    a.activation(h_hi[:, 0:NK], ps[:, 3, 0:D].rearrange("p (k t) -> p k t", k=NK),
                                 ACT.Copy).then_inc(h2hi, 1)
                i = s - 5
                if 0 <= i < NS:
                    act.wait_ge(x2T_rdy, i + 1)
                    if i >= 1:
                        act.wait_ge(lg_rdy, i)
                    a.activation(x2T, ps[:, 5, 0:D].rearrange("p (k t) -> p k t", k=NK),
                                 ACT.Copy).then_inc(x2T_sb, 1)
                for part, (_, last) in enumerate(PARTS[:-1]):
                    if s == last + 6:
                        exps_router(part)
            exps_router(len(PARTS) - 1)

            def x_row(i):
                act.wait_ge(a3T, i)
                a.activation(xrow, XS[:, bass.ds(i, 1), 0:D].rearrange("p o d -> p (o d)"),
                             ACT.Copy).then_inc(xrow_rdy, 1)

            def x_hi3(i, p):
                act.wait_ge(a3T, i + 1)
                if not (isinstance(i, int) and i < 2):
                    act.wait_ge(gu_b, i - 1)
                a.activation(a_hi[p], ps[:, 6, 0:D].rearrange("p (k t) -> p k t", k=NK), ACT.Copy).then_inc(a3hi, 1)

            def silu(i, half):
                act.wait_ge((gu_a, gu_b)[half], i + 1)
                if not (isinstance(i, int) and i < 1):
                    act.wait_ge(h3, 2 * i + half - 1)
                a.activation(sg[:, half * 512:(half + 1) * 512], ps[:, 2 * half, :], ACT.Silu,
                             scale=1 / W_SCALE).then_inc(sg3, 1)

            def h_hi3(i):
                act.wait_ge(h3T, i + 1)
                if not (isinstance(i, int) and i < 1):
                    act.wait_ge(y3, i)
                a.activation(h_hi, ps[:, 4:6, :].rearrange("p c (k t) -> p (c k) t", t=P),
                             ACT.Copy).then_inc(h3hi, 1)

            def tile(i, p, first=False, last=False):
                if not isinstance(i, int):
                    x_row(i + 1)
                silu(i, 0)
                if not first:
                    h_hi3(i - 1)
                if not last:
                    x_hi3(i + 1, 1 - p)
                silu(i, 1)

            x_hi3(0, 0)
            for i in range(PEEL):
                tile(i, i % 2, first=i == 0)
            act.wait_ge(ld3[PEEL + 1], 16 * (NS - PEEL - 1))
            with act.Fori(0, LOOPS) as it:
                for p in range(2):
                    tile(2 * it + PEEL + p, p)
            tile(NS - 1, (NS - 1) % 2, last=True)
            act.wait_ge(y3, NS - 1)
            for c in range(2):
                act.wait_ge(endT, c + 1)
                a.activation(h_hi[:, 4 * c:4 * c + 4], ps[:, 4 + c, :].rearrange("p (k t) -> p k t", t=P),
                             ACT.Copy).then_inc(end_hi, 1)

        @block.vector
        def _(dve):
            v = nc.vector
            links = [0]

            def link(ins):
                links[0] += 1
                ins.then_inc(link_v, 1)
                dve.wait_ge(link_v, links[0])

            def split_lo(n):
                dve.wait_ge(c_hi, n + 1)
                v.scalar_tensor_tensor(out=chunk_dst(ORDER[n], False), in0=staged(n)[0], scalar=W_SCALE,
                                       in1=chunk_dst(ORDER[n], True), op0=ALU.mult,
                                       op1=ALU.subtract).then_inc(c_lo, 1)

            def slot_tiles(which, n):
                link(v.tensor_tensor(over[:, :, :], run[:, :, n - 1:n].to_broadcast([P, E, NT]),
                                     steps[:, 0:NT].unsqueeze(1).to_broadcast([P, E, NT]), ALU.is_gt))
                link(v.reduce_sum(nt_e[:, :], over[:, :, :], AX.X))
                link(v.tensor_tensor_scan(end_e[:, :], reset[:, 0, 1:1 + E], nt_e[:, :], 0.0, ALU.mult, ALU.add))
                link(v.tensor_tensor(tile_ge[:, :, :], tiles[:, :].unsqueeze(2).to_broadcast([P, NS, E - 1]),
                                     end_e[:, 0:E - 1].unsqueeze(1).to_broadcast([P, NS, E - 1]), ALU.is_ge))
                link(v.reduce_sum(tile_e[:, :], tile_ge[:, :, :], AX.X))
                v.tensor_copy(tile_i[:, which, :], tile_e[:, :]).then_inc(tile_rdy, 1)

            def running():
                link(v.tensor_tensor_scan(run[:, :, :].rearrange("p e i -> p (e i)"),
                                          reset[:, :, :].rearrange("p e i -> p (e i)"),
                                          cnt[:, :, :].rearrange("p e i -> p (e i)"), 0.0, ALU.mult, ALU.add))

            def counts():
                dve.wait_ge(cnt_rdy, 1)
                v.tensor_copy(cum[:, 0:NT, :], ps[:, 7, 0:NT * E].rearrange("p (i e) -> p i e", e=E))
                v.tensor_copy(cnt[:, :, 0:NT], ps[:, 7, 256:256 + NT * E].rearrange("p (i e) -> p e i", e=E)
                              ).then_inc(cnt_sb, 1)

            def slots():
                link(v.tensor_tensor(base_e[:, :], end_e[:, :], nt_e[:, :], ALU.subtract))
                link(v.tensor_tensor(run[:, :, 0:NT], run[:, :, 0:NT], cnt[:, :, 0:NT], ALU.subtract))
                link(v.scalar_tensor_tensor(out=run[:, :, 0:NT], in0=base_e[:, :].unsqueeze(2).to_broadcast([P, E, NT]),
                                            scalar=float(P), in1=run[:, :, 0:NT], op0=ALU.mult, op1=ALU.add))
                link(v.tensor_tensor(where[:, 0:NT, :], cum[:, 0:NT, :],
                                     run[:, :, 0:NT].rearrange("p e i -> p i e"), ALU.add))
                link(v.tensor_tensor(where[:, 0:NT, :], where[:, 0:NT, :], oh[:, 0:NT, :], ALU.mult))
                link(v.reduce_sum(pos[:, 0:NT], where[:, 0:NT, :], AX.X))
                v.tensor_copy(pos_i[:, 0:NT], pos[:, 0:NT]).then_inc(pos_rdy, 1)

            def logits(part):
                r = slice(*PARTS[part])
                n = r.stop - r.start
                dve.wait_ge(lg_rdy, r.stop)
                dve.wait_ge(in_r, 32)
                v.tensor_scalar(valid[:, r], XS[:, r, D], float(T), None, ALU.is_lt)
                v.tensor_copy(X2[:, r, D:D + 1], XS[:, r, D:D + 1])
                link(v.tensor_tensor(lg[:, r, :], ps[:, PART_BANK[part], 0:n * E].rearrange("p (i e) -> p i e", e=E),
                                     br_sb[:, :].unsqueeze(1).to_broadcast([P, n, E]), ALU.add))
                link(v.tensor_reduce(top[:, r], lg[:, r, :], AX.X, ALU.max))
                v.tensor_tensor(lg[:, r, :], lg[:, r, :], top[:, r].unsqueeze(2).to_broadcast([P, n, E]),
                                ALU.subtract).then_inc(lg_sb, 1)

            def top_expert(part):
                r = slice(*PARTS[part])
                n = r.stop - r.start
                dve.wait_ge(lg_sb, part + 1)
                link(v.tensor_scalar(ohf[:, r, :], lg[:, r, :], 0.0, None, ALU.is_ge))
                link(v.tensor_tensor_scan(where[:, r, :].rearrange("p i e -> p (i e)"),
                                          reset_e[:, r, :].rearrange("p i e -> p (i e)"),
                                          ohf[:, r, :].rearrange("p i e -> p (i e)"), 0.0, ALU.mult, ALU.add))
                link(v.scalar_tensor_tensor(out=ohf[:, r, :], in0=where[:, r, :], scalar=1.0, in1=ohf[:, r, :],
                                            op0=ALU.is_equal, op1=ALU.mult))
                v.tensor_tensor(oh[:, r, :], ohf[:, r, :], valid[:, r].unsqueeze(2).to_broadcast([P, n, E]),
                                ALU.mult).then_inc(oh_rdy, 1)

            def top_weight(part):
                r = slice(*PARTS[part])
                dve.wait_ge(ex_rdy, part + 1)
                v.tensor_scalar(off[:, r], valid[:, r], -NOWHERE, NOWHERE, ALU.mult, ALU.add)
                link(v.reduce_sum(top[:, r], ex[:, r, :], AX.X))
                link(v.reciprocal(top[:, r], top[:, r]))
                v.tensor_scalar(X2[:, r, D + 1], top[:, r], 1 / W_SCALE, None, ALU.mult).then_inc(w_rdy, 1)

            def places(part):
                first, last = PARTS[part]
                r, n = slice(first, last), last - first
                dve.wait_ge(cnt_rdy, part + 2)
                dve.wait_ge(scat2, 16 * NT)
                v.tensor_copy(cnt[:, :, r], ps[:, PART_BANK[part], 256:256 + n * E].rearrange("p (i e) -> p e i", e=E))
                link(v.tensor_tensor(cum[:, r, :], ps[:, PART_BANK[part], 0:n * E].rearrange("p (i e) -> p i e", e=E),
                                     region[:, :].unsqueeze(1).to_broadcast([P, n, E]), ALU.add))
                running()
                link(v.tensor_tensor(cum[:, r, :], cum[:, r, :], cnt[:, :, r].rearrange("p e i -> p i e"),
                                     ALU.subtract))
                link(v.tensor_tensor(where[:, r, :], cum[:, r, :],
                                     run[:, :, r].rearrange("p e i -> p i e"), ALU.add))
                link(v.tensor_tensor(where[:, r, :], where[:, r, :], oh[:, r, :], ALU.mult))
                link(v.reduce_sum(pos[:, r], where[:, r, :], AX.X))
                v.tensor_tensor(pos_i[:, r], pos[:, r], off[:, r], ALU.add).then_inc(pos_rdy, 1)

            def tile_rows():
                link(v.tensor_scalar(jump[:, :], nt_e[:, :], float(-P), float(T), ALU.mult, ALU.add))
                link(v.tensor_tensor(tile_ge[:, :, :], tile_ge[:, :, :],
                                     jump[:, 0:E - 1].unsqueeze(1).to_broadcast([P, NS, E - 1]), ALU.mult))
                link(v.reduce_sum(tile_row[:, :], tile_ge[:, :, :], AX.X))
                v.tensor_tensor(row_i[:, :], tile_row[:, :], steps[:, :], ALU.add).then_inc(row_rdy, 1)

            dve.wait_ge(in_ids, 16)
            v.memset(ge[:, 0, :], 1.0)
            v.memset(ge[:, E, :], 0.0)
            for e in range(1, E):
                ins = v.tensor_scalar(ge[:, e, :], ids_sb[:, :], float(e * VOCAB_PART), None, ALU.is_ge)
            link(ins)
            v.tensor_tensor(oh[:, 0:NT, :].rearrange("p i e -> p e i"), ge[:, 0:E, :], ge[:, 1:E + 1, :],
                            ALU.subtract).then_inc(oh_rdy, 1)
            def x_low(b):
                dve.wait_ge(x_hi, b + 1)
                t = slice(b * S, (b + 1) * S)
                v.tensor_tensor(xTv_lo[:, :, t], xT_st[:, :, t], xTv_hi[:, :, t], ALU.subtract).then_inc(x_lo, 1)

            x_low(0)
            for k in range(NK):
                dve.wait_ge(w_hi, k + 1)
                v.scalar_tensor_tensor(out=wqkv_lo[:, k], in0=wqkv_st[:, k], scalar=W_SCALE, in1=wqkv_hi[:, k],
                                       op0=ALU.mult, op1=ALU.subtract).then_inc(w_lo, 1)
            counts()
            for q in QT[0:2]:
                v.memset(q[SLOT:P, 0::2, :].bitcast(F32), 0.0)
                ins = v.memset(q[0:SLOT, 1::2, :].bitcast(F32), 0.0)
                if q is QT[0]:
                    x_low(1)
            ins.then_inc(const_z, 1)

            def proj_lo(tt):
                j = tt % 2
                qk = ps[:, bank_qk(tt), :].rearrange("p (s h c) -> p s h c", s=2, h=H)
                vv = ps[:, bank_v(tt), 0:D].rearrange("p (h c) -> p h c", h=H)
                for n, (lo, src, hi) in enumerate((
                        (Ks[j][:, :, 1, :], qk[:, 1], Ks[j][:, :, 0, :]),
                        (Qs[j][:, :, 2, :], qk[:, 0], Qs[j][:, :, 0, :]),
                        (Vs[:, tt, :, DK:2 * DK], vv, Vs[:, tt, :, 0:DK]))):
                    dve.wait_ge(qkv_hi, 3 * tt + (2, 2, 3)[n])
                    v.scalar_tensor_tensor(out=lo, in0=src, scalar=1 / W_SCALE, in1=hi,
                                           op0=ALU.mult, op1=ALU.subtract).then_inc(qkv_lo, 1)

            def stacks(tt):
                b, j = divmod(tt, TB)
                dve.wait_ge(kT_rdy, tt + 1)
                v.tensor_copy(KT[b % 3][:, :, j * P:(j + 1) * P],
                              ps16(bank_kT(tt)).rearrange("p (h t) -> p h t", h=PAIRS)).then_inc(kT_done, 1)
                dve.wait_ge(qT_rdy, tt + 1)
                v.tensor_copy(QT[b % 3][0:SLOT, 0::2, j * P:(j + 1) * P],
                              ps16(bank_qT(tt), slice(0, SLOT)).rearrange("p (h t) -> p h t", h=PAIRS)
                              ).then_inc(q_even, 1)

            def maxima(b, g):
                n = NG * b + g
                dst = Mx[:, :, :, 2 * g:2 * g + 2].rearrange("p t r a -> p t a r")
                if g == 0 and b >= 1:
                    dve.wait_ge(m_neg, b)
                dve.wait_ge(s_rdy, 2 * n + 1)
                v.tensor_reduce(dst[:, 0], ps[:, 0, :].rearrange("p (a r k) -> p a r k", a=2, r=2),
                                AX.X, ALU.max).then_inc(maxed, 1)
                dve.wait_ge(s_rdy, 2 * n + 2)
                v.tensor_reduce(dst[:, 1],
                                ps[:, 1:3, :].rearrange("p c (a r k) -> p (a r) c k", a=2, r=2),
                                AX.XY, ALU.max).then_inc(maxed, 1)

            def negate(b):
                m = Mx.rearrange("p t r a -> p (t r) a")
                dve.wait_ge(maxed, 2 * NG * (b + 1))
                if b >= 1:
                    dve.wait_ge(mT_rdy, b)
                link(v.tensor_scalar(Mn[:, :, 0, :], m, -1.0, None, ALU.mult))
                v.scalar_tensor_tensor(out=Mn[:, :, 1, :], in0=m, scalar=-1.0, in1=Mn[:, :, 0, :],
                                       op0=ALU.mult, op1=ALU.subtract).then_inc(m_neg, 1)

            def max_T(b):
                dve.wait_ge(mT_rdy, b + 1)
                if b >= 1:
                    dve.wait_ge(m_row, 32 * b)
                v.tensor_copy(mT[0:4 * PAIRS, :], ps16(bank_mT(b), slice(0, 4 * PAIRS))[:, 0:S]).then_inc(mT_done, 1)

            def outputs(b, g):
                n = NG * b + g
                o = ps[:, 6, 0:TB * G * (2 * DK + 1)].rearrange("p (a c) -> p a c", c=2 * DK + 1)
                dve.wait_ge(av_rdy, n + 1)
                if n >= 1:
                    dve.wait_ge(o_norm, n)
                v.reciprocal(Or, o[:, :, 2 * DK])
                v.tensor_reduce(Oa, o[:, :, 0:2 * DK].rearrange("p a (s c) -> p a c s", s=2),
                                AX.X, ALU.add).then_inc(o_read, 1)
                dve.wait_ge(o_read, n + 1)
                if g == 0 and b >= 1:
                    dve.wait_ge(oT_rdy, b)
                dst = On[:, :, g * G * DK:(g + 1) * G * DK]
                for q in range(TB):
                    ins = v.tensor_tensor(dst[:, q].rearrange("p (a c) -> p a c", c=DK), Oa[:, q * G:(q + 1) * G, :],
                                          Or[:, q * G:(q + 1) * G].unsqueeze(2).to_broadcast([P, G, DK]), ALU.mult)
                ins.then_inc(o_norm, 1)

            def o_lo(b):
                dve.wait_ge(oT_hi, b + 1)
                if b >= 1:
                    dve.wait_ge(wo_rdy, TB * b)
                v.tensor_tensor(OT_lo, ps[:, 7, :].rearrange("p (j k t) -> p j k t", j=TB, k=NK), OT_hi,
                                ALU.subtract).then_inc(oT_lo, 1)

            def residual(b):
                for j in range(TB):
                    tt = TB * b + j
                    dve.wait_ge(wo_rdy, TB * (b + 1))
                    dve.wait_ge(in_xtok, 16)
                    v.scalar_tensor_tensor(out=X1[:, tt, 0:D], in0=ps[:, 7, j * D:(j + 1) * D], scalar=1 / W_SCALE,
                                           in1=X1[:, tt, 0:D], op0=ALU.mult, op1=ALU.add).then_inc(res1, 1)

            def stats1(b):
                for j in range(TB):
                    tt = TB * b + j
                    dve.wait_ge(res1, tt + 1)
                    v.bn_stats(st[:, j, :], X1[:, tt, 0:D]).then_inc(bn1, 1)
                for j in range(TB):
                    tt = TB * b + j
                    dve.wait_ge(bn1, tt + 1)
                    if b >= 1 and j == 0:
                        dve.wait_ge(rs1, b)
                    v.bn_aggr(mv[:, j, :], st[:, j, :]).then_inc(mv1, 1)

            def norm1(b):
                dve.wait_ge(rs1, b + 1)
                for j in range(TB):
                    tt = TB * b + j
                    dve.wait_ge(mv1, tt + 1)
                    v.tensor_scalar(X1[:, tt, 0:D], X1[:, tt, 0:D], mv[:, j, 0:1], rstd[:, j:j + 1],
                                    ALU.subtract, ALU.mult).then_inc(x1_rdy, 1)

            proj_lo(0)
            proj_lo(1)
            stacks(0)
            stacks(1)
            proj_lo(2)
            maxima(0, 0)
            maxima(0, 1)
            maxima(0, 2)
            maxima(0, 3)
            negate(0)
            max_T(0)
            proj_lo(3)
            stacks(2)
            stacks(3)
            x_low(2)
            maxima(1, 0)
            x_low(3)
            dve.wait_ge(w_hi, NK + 1)
            v.scalar_tensor_tensor(out=wo_lo, in0=wo_st, scalar=W_SCALE, in1=wo_hi,
                                   op0=ALU.mult, op1=ALU.subtract).then_inc(w_lo, 1)
            proj_lo(2 * TB)
            n = 0
            for step in range(STEPS):
                b, g = divmod(step, NG)
                if step + AHEAD < STEPS:
                    maxima(*divmod(step + AHEAD, NG))
                if g == 2 and b + 1 < B:
                    negate(b + 1)
                if step >= 1:
                    if b >= 1 and g == 1:
                        o_lo(b - 1)
                    outputs(*divmod(step - 1, NG))
                if g == 2 and b + 1 < B:
                    max_T(b + 1)
                if step == STEPS - 1:
                    dve.wait_ge(exped, 2 * STEPS)
                    v.tensor_tensor(Pl[step % 2][:, 1:3], Pf[:, 1:3], Ph[step % 2][:, 1:3],
                                    ALU.subtract).then_inc(p_lo_last, 1)
                if b >= 1:
                    if g == 3:
                        residual(b - 1)
                        if b < B - 1:
                            stats1(b - 1)
                    elif g == 0 and b >= 2:
                        norm1(b - 2)
                if stacked_at(step) is not None:
                    stacks(stacked_at(step))
                if 1 <= step < STEPS - 1 and n < ATT_CHUNKS:
                    split_lo(n)
                    n += 1
                if projected_at(step) is not None:
                    proj_lo(projected_at(step))
                if step == 3 * NG - 1:
                    dve.wait_ge(cnt_sb, 1)
                    running()
                    slot_tiles(0, NT)
                elif step == 3 * NG:
                    slots()
            outputs(B - 1, NG - 1)
            stats1(B - 2)
            norm1(B - 2)
            o_lo(B - 1)
            split_lo(n)
            n += 1
            residual(B - 1)
            stats1(B - 1)
            norm1(B - 1)
            while n < NCH - LAST:
                split_lo(n)
                n += 1

            inv = 1 / W_SCALE
            for s in range(NS + 6):
                for part, (_, last) in enumerate(PARTS[:-1]):
                    if s == last + 6:
                        logits(part)
                        top_expert(part)
                    elif s == last + 7:
                        top_weight(part)
                        places(part)
                if s < NS:
                    dve.wait_ge(a2hi, s + 1)
                    v.tensor_tensor(a_lo[s % 2], ps[:, 0, 0:D].rearrange("p (k t) -> p k t", k=NK),
                                    a_hi[s % 2], ALU.subtract).then_inc(a2lo, 1)
                j = s - 3
                if 0 <= j < NS:
                    dve.wait_ge(y2, j + 1)
                    if j >= 2:
                        dve.wait_ge(x2_rdy, j - 1)
                    v.scalar_tensor_tensor(out=res[j % 2], in0=ps[:, (4, 7)[j % 2], 0:D], scalar=inv,
                                           in1=XS[:, j, 0:D], op0=ALU.mult, op1=ALU.add).then_inc(r2, 1)
                i = s - 1
                if 0 <= i < NS:
                    dve.wait_ge(sg2, i + 1)
                    if i >= 1:
                        dve.wait_ge(h2T, i)
                    v.scalar_tensor_tensor(out=hh[:, 0:D], in0=ps[:, 2, 0:D], scalar=inv, in1=sg[:, 0:D],
                                           op0=ALU.mult, op1=ALU.mult).then_inc(h2, 1)
                if 0 <= j < NS:
                    dve.wait_ge(r2, j + 1)
                    v.bn_stats(st[:, j % 2, :], res[j % 2]).then_inc(bn2, 1)
                i = s - 2
                if 0 <= i < NS:
                    dve.wait_ge(h2hi, i + 1)
                    v.tensor_tensor(h_lo[:, 0:NK], ps[:, 3, 0:D].rearrange("p (k t) -> p k t", k=NK),
                                    h_hi[:, 0:NK], ALU.subtract).then_inc(h2lo, 1)
                if 0 <= j < NS:
                    dve.wait_ge(bn2, j + 1)
                    v.bn_aggr(mv[:, j % 2, :], st[:, j % 2, :]).then_inc(mv2, 1)
                i = s - 4
                if 0 <= i < NS:
                    dve.wait_ge(rs2, i + 1)
                    v.tensor_scalar(X2[:, i, 0:D], res[i % 2], mv[:, i % 2, 0:1], rstd[:, i % 2:i % 2 + 1],
                                    ALU.subtract, ALU.mult).then_inc(x2_rdy, 1)

            last = len(PARTS) - 1
            logits(last)
            top_expert(last)
            top_weight(last)
            places(last)
            slot_tiles(1, NS)
            tile_rows()
            while n < NCH:
                split_lo(n)
                n += 1

            def x_lo3(i, p):
                dve.wait_ge(a3hi, i + 1)
                v.tensor_tensor(a_lo[p], ps[:, 6, 0:D].rearrange("p (k t) -> p k t", k=NK),
                                a_hi[p], ALU.subtract).then_inc(a3lo, 1)

            def gated(i, half):
                dve.wait_ge(sg3, 2 * i + half + 1)
                if not (isinstance(i, int) and i < 1):
                    dve.wait_ge(h3T, i)
                v.scalar_tensor_tensor(out=hh[:, half * 512:(half + 1) * 512], in0=ps[:, 2 * half + 1, :], scalar=inv,
                                       in1=sg[:, half * 512:(half + 1) * 512],
                                       op0=ALU.mult, op1=ALU.mult).then_inc(h3, 1)

            def h_lo3(i):
                dve.wait_ge(h3hi, i + 1)
                v.tensor_tensor(h_lo, ps[:, 4:6, :].rearrange("p c (k t) -> p (c k) t", t=P), h_hi,
                                ALU.subtract).then_inc(h3lo, 1)

            def statistics(i, p, scattered):
                row = XS[:, bass.ds(i, 1), :].rearrange("p o d -> p (o d)")
                dve.wait_ge(y3, i + 1)
                if scattered is not None:
                    dve.wait_ge(scat_out[p], 16 * scattered)
                v.scalar_tensor_tensor(out=res[p], in0=ps[:, 7, 0:D], scalar=row[:, D + 1:D + 2],
                                       in1=row[:, 0:D], op0=ALU.mult, op1=ALU.add).then_inc(r3, 1)
                dve.wait_ge(r3, i + 1)
                v.bn_stats(st[:, p, :], res[p]).then_inc(bn3, 1)
                dve.wait_ge(bn3, i + 1)
                v.tensor_copy(out_i[:, p:p + 1], row[:, D:D + 1])
                v.bn_aggr(mv[:, p, :], st[:, p, :]).then_inc(mv3, 1)

            def finish(i, p):
                dve.wait_ge(rs3, i + 1)
                dve.wait_ge(mv3, i + 1)
                v.tensor_scalar(fin[p], res[p], mv[:, p, 0:1], rstd[:, p:p + 1],
                                ALU.subtract, ALU.mult).then_inc(f3, 1)

            def tile(i, p, first=False, last=False, scattered=None):
                gated(i, 0)
                if not first:
                    h_lo3(i - 1)
                if not last:
                    x_lo3(i + 1, 1 - p)
                gated(i, 1)
                if not first:
                    statistics(i - 1, 1 - p, scattered)
                if not first and not last:
                    finish(i - 1, 1 - p)

            x_lo3(0, 0)
            for i in range(PEEL):
                tile(i, i % 2, first=i == 0, scattered=(i - 1) // 2 if i >= 3 else None)
            with dve.Fori(0, LOOPS) as it:
                for p in range(2):
                    tile(2 * it + PEEL + p, p, scattered=it + (PEEL + p - 1) // 2)
            tile(NS - 1, 0, last=True, scattered=(NS - 2) // 2)
            for c in range(2):
                dve.wait_ge(end_hi, c + 1)
                v.tensor_tensor(h_lo[:, 4 * c:4 * c + 4], ps[:, 4 + c, :].rearrange("p (k t) -> p k t", t=P),
                                h_hi[:, 4 * c:4 * c + 4], ALU.subtract).then_inc(end_lo, 1)
            finish(NS - 2, 1)
            statistics(NS - 1, 0, (NS - 1) // 2)
            finish(NS - 1, 0)

        @block.tensor
        def _(pe):
            t = nc.tensor

            def count(bank, first, last):
                n = (last - first) * E
                onehot = oh[:, first:last, :].rearrange("p i e -> p (i e)")
                t.matmul(ps[:, bank, 0:n], before[:, :], onehot, start=True, stop=True)
                t.matmul(ps[:, bank, 256:256 + n], ones[:, :], onehot, start=True, stop=True).then_inc(cnt_rdy, 1)

            def three(dst, x_h, x_l, w_h, w_l, nk):
                for k in range(nk):
                    for m, (xs, ws) in enumerate(((x_h, w_h), (x_h, w_l), (x_l, w_h))):
                        last = t.matmul(dst, xs(k), ws(k), start=(k == 0 and m == 0), stop=(k == nk - 1 and m == 2))
                return last

            def keep_warm(n, moving, bank=6):
                for _ in range(n):
                    t.matmul(ps[:, bank, 0:moving.shape[-1]], ones[:, :], moving, start=True, stop=True)

            pe.wait_ge(const_r, 1)
            pe.wait_ge(oh_rdy, 1)
            count(7, 0, NT)

            def qkv(tt):
                tok = slice(tt * P, (tt + 1) * P)
                xh = lambda k: xTv_hi[:, k, tok]
                xl = lambda k: xTv_lo[:, k, tok]
                three(ps[:, bank_qk(tt), :], xh, xl, lambda k: wqkv_hi[:, k, 0:2 * D],
                      lambda k: wqkv_lo[:, k, 0:2 * D], NK).then_inc(proj_qk, 1)
                if tt == 2 * TB:
                    pe.wait_ge(mT_done, 1)
                elif tt == NT - 1:
                    pe.wait_ge(oT_lo, 1)
                elif tt > 2 * TB:
                    pe.wait_ge(q_even, tt)
                    pe.wait_ge(q_odd, tt)
                three(ps[:, bank_v(tt), 0:D], xh, xl, lambda k: wqkv_hi[:, k, 2 * D:3 * D],
                      lambda k: wqkv_lo[:, k, 2 * D:3 * D], NK).then_inc(proj_v, 1)

            def stack_T(tt):
                j = tt % 2
                pe.wait_ge(qkv_lo, 3 * tt + 3)
                for a in range(PAIRS):
                    last = t.transpose(ps16(bank_kT(tt))[:, a * P:(a + 1) * P],
                                       Ks[j][:, 2 * a:2 * a + 2].rearrange("p h s c -> p (h s c)"), identH[:, :])
                last.then_inc(kT_rdy, 1)
                for a in range(PAIRS):
                    last = t.transpose(ps16(bank_qT(tt))[:, a * P:(a + 1) * P],
                                       Qs[j][:, 2 * a:2 * a + 2].rearrange("p h s c -> p (h s c)"), identH[:, :])
                last.then_inc(qT_rdy, 1)

            def scores(b, g):
                n = NG * b + g
                q, k = QT[b % 3], KT[b % 3]
                step = n - AHEAD
                if step >= 0:
                    if step == 0:
                        pe.wait_ge(qkv_lo, 3 * 2 * TB + 2)
                    elif stacked_at(step - 1) is not None:
                        pe.wait_ge(kT_done, stacked_at(step - 1) + 1)
                    elif projected_at(step - 1) is not None:
                        pe.wait_ge(qkv_lo, 3 * projected_at(step - 1) + 2)
                if g == 0:
                    pe.wait_ge(kT_done, TB * (b + 1))
                    pe.wait_ge(q_even, TB * (b + 1))
                    pe.wait_ge(q_odd, TB * (b + 1))
                if n >= 1:
                    pe.wait_ge(maxed, 2 * n - 1)
                for bank, qt, kt in ((0, 0, 0), (1, 1, 0), (2, 1, 1)):
                    if bank == 1 and n >= 1:
                        pe.wait_ge(maxed, 2 * n)
                    diag = qt == kt
                    if diag:
                        t.matmul(ps[:, bank, :], identB[:, :], maskS[:, :, :].rearrange("p a k -> p (a k)"),
                                 start=True, stop=False)
                    for i in range(G):
                        h = G * g + i
                        last = t.matmul(ps[:, bank, i * P:(i + 1) * P], q[:, h, qt * P:(qt + 1) * P],
                                        k[:, h // 2, kt * P:(kt + 1) * P], start=not diag,
                                        stop=(not diag) or i == G - 1)
                    if bank != 1:
                        last.then_inc(s_rdy, 1)

            def max_rows(b):
                pe.wait_ge(m_neg, b + 1)
                if b >= 1:
                    pe.wait_ge(o_read, NG * b - 2)
                for qt in range(TB):
                    last = t.transpose(ps16(bank_mT(b), slice(0, 4 * PAIRS))[:, qt * P:(qt + 1) * P],
                                       Mn[:, 2 * qt:2 * qt + 2].rearrange("p r s a -> p (r s a)"), identH[:, :])
                last.then_inc(mT_rdy, 1)

            def scores_T(b, g):
                n = NG * b + g
                q, k = QT[b % 3], KT[b % 3]
                if g == 0:
                    pe.wait_ge(m_row, 32 * (b + 1))
                if n >= 1:
                    pe.wait_ge(exped, 2 * n)
                for bank, kt, qt in ((3, 0, 0), (4, 0, 1), (5, 1, 1)):
                    diag = qt == kt
                    if diag:
                        t.matmul(ps[:, bank, :], identB[:, :], maskT[:, :, :].rearrange("p a k -> p (a k)"),
                                 start=True, stop=False)
                    for i in range(G):
                        h = G * g + i
                        last = t.matmul(ps[:, bank, i * P:(i + 1) * P], k[:, h // 2, kt * P:(kt + 1) * P],
                                        q[:, h, qt * P:(qt + 1) * P], start=not diag,
                                        stop=(not diag) or i == G - 1)
                last.then_inc(st_rdy, 1)

            def values(b, g):
                n = NG * b + g
                pe.wait_ge(p_lo, n + 1)
                if g == 2 and b + 1 < B:
                    pe.wait_ge(mT_done, b + 2)
                if n == STEPS - 1:
                    pe.wait_ge(p_lo_last, 1)
                if n >= 1:
                    pe.wait_ge(o_read, n)
                w = 2 * DK + 1
                for i in range(G):
                    h = G * g + i
                    for qt, parts in ((0, ((0, 0),)), (1, ((1, 0), (2, 1)))):
                        dst = ps[:, 6, (qt * G + i) * w:(qt * G + i + 1) * w]
                        todo = [(p, c, kt) for c, kt in parts for p in (Ph, Pl)]
                        for m, (p, c, kt) in enumerate(todo):
                            last = t.matmul(dst, p[n % 2][:, c, i * P:(i + 1) * P],
                                            Vs[:, TB * b + kt, h, 0:w],
                                            start=m == 0, stop=m == len(todo) - 1)
                last.then_inc(av_rdy, 1)

            def out_T(b):
                pe.wait_ge(o_norm, NG * (b + 1))
                if b == 0:
                    pe.wait_ge(q_even, NT - 1)
                    pe.wait_ge(q_odd, NT - 1)
                else:
                    pe.wait_ge(res1, TB * b)
                for j in range(TB):
                    for k in range(NK):
                        last = t.transpose(ps[:, 7, j * D + k * P:j * D + (k + 1) * P],
                                           On[:, j, k * P:(k + 1) * P], identF[:, :])
                last.then_inc(oT_rdy, 1)

            def out_project(b):
                pe.wait_ge(oT_lo, b + 1)
                if b == 0:
                    pe.wait_ge(w_lo, NK + 1)
                    pe.wait_ge(q_even, NT)
                    pe.wait_ge(q_odd, NT)
                for j in range(TB):
                    last = three(ps[:, 7, j * D:(j + 1) * D], lambda k: OT_hi[:, j, k], lambda k: OT_lo[:, j, k],
                                 lambda k: wo_hi[:, k], lambda k: wo_lo[:, k], NK)
                    last.then_inc(wo_rdy, 1)

            keep_warm(WARM_START, before[:, :])
            pe.wait_ge(x_lo, 1)
            pe.wait_ge(w_lo, NK)
            qkv(0)
            pe.wait_ge(cnt_sb, 1)
            qkv(1)
            stack_T(0)
            pe.wait_ge(x_lo, 2)
            qkv(2)
            stack_T(1)
            qkv(3)
            pe.wait_ge(const_m, 1)
            scores(0, 0)
            scores(0, 1)
            scores(0, 2)
            scores(0, 3)
            stack_T(2)
            max_rows(0)
            stack_T(3)
            for step in range(STEPS):
                b, g = divmod(step, NG)
                if step == 0:
                    pe.wait_ge(const_m, 2)
                    for e in (kT_done, q_even, q_odd):
                        pe.wait_ge(e, 2 * TB)
                if step != 1:
                    scores_T(b, g)
                if g == 3 and b + 1 < B:
                    max_rows(b + 1)
                if b >= 1 and g == 1:
                    out_T(b - 1)
                if step == 0:
                    scores(1, 0)
                    pe.wait_ge(x_lo, 3)
                    pe.wait_ge(maxed, 2 * NG + 1)
                    qkv(2 * TB)
                    scores_T(0, 1)
                if step + AHEAD < STEPS:
                    scores(*divmod(step + AHEAD, NG))
                if step >= 1:
                    values(*divmod(step - 1, NG))
                if b >= 1 and g == 3:
                    out_project(b - 1)
                if stacked_at(step) is not None:
                    pe.wait_ge(maxed, 2 * (step + AHEAD) + 1)
                    stack_T(stacked_at(step))
                if projected_at(step) is not None:
                    pe.wait_ge(x_lo, projected_at(step) // TB + 1)
                    pe.wait_ge(maxed, 2 * (step + AHEAD) + 1)
                    qkv(projected_at(step))
            values(B - 1, NG - 1)
            out_T(B - 1)
            out_project(B - 1)

            pe.wait_ge(tile_rdy, 1)
            experts = [pe.value_load(tile_i[0:1, 0, i:i + 1], min_val=0, max_val=E - 1) for i in range(NS)]
            pe.wait_ge(res1, NT)
            pe.wait_ge(x1_rdy, NT)
            keep_warm(2 * WARM_GAP, wf_hi[:, 0:512])
            for s in range(NS + 7):
                if s < NS:
                    pe.wait_ge(ld2[s], 16)
                    if s >= 1:
                        pe.wait_ge(a2lo, s)
                    for k in range(NK):
                        last = t.transpose(ps[:, 0, k * P:(k + 1) * P], XS[:, s, k * P:(k + 1) * P], identF[:, :])
                    last.then_inc(a2T, 1)
                i = s - 1
                if 0 <= i < NS:
                    if i == 0:
                        pe.wait_ge(c_lo, CTX_AT + NCTX)
                    expert = experts[i]
                    pe.wait_ge(a2lo, i + 1)
                    if i >= 1:
                        pe.wait_ge(h2, i)
                    three(ps[:, 2, 0:D], lambda k: a_hi[i % 2][:, k], lambda k: a_lo[i % 2][:, k],
                          lambda k: ctx_hi[:, bass.ds(expert * (NK * D) + k * D, D)],
                          lambda k: ctx_lo[:, bass.ds(expert * (NK * D) + k * D, D)], NK).then_inc(z_rdy, 1)
                i = s - 2
                if 0 <= i < NS:
                    pe.wait_ge(h2, i + 1)
                    if i >= 1:
                        pe.wait_ge(h2lo, i)
                    for k in range(NK):
                        last = t.transpose(ps[:, 3, k * P:(k + 1) * P], hh[:, k * P:(k + 1) * P], identF[:, :])
                    last.then_inc(h2T, 1)
                i = s - 3
                if 0 <= i < NS:
                    expert = experts[i]
                    pe.wait_ge(h2lo, i + 1)
                    if i >= 2:
                        pe.wait_ge(mv2, i - 1)
                    three(ps[:, (4, 7)[i % 2], 0:D], lambda k: h_hi[:, k], lambda k: h_lo[:, k],
                          lambda k: ctx_hi[:, bass.ds(expert * (NK * D) + k * D, D)],
                          lambda k: ctx_lo[:, bass.ds(expert * (NK * D) + k * D, D)], NK).then_inc(y2, 1)
                i = s - 5
                if 0 <= i < NS:
                    pe.wait_ge(x2_rdy, i + 1)
                    if i >= 1:
                        pe.wait_ge(x2T_sb, i)
                    for k in range(NK):
                        last = t.transpose(ps[:, 5, k * P:(k + 1) * P], X2[:, i, k * P:(k + 1) * P], identF[:, :])
                    last.then_inc(x2T_rdy, 1)
                i = s - 6
                if 0 <= i < NS:
                    if i == 0:
                        pe.wait_ge(in_r, 32)
                    pe.wait_ge(x2T_sb, i + 1)
                    part = sum(i >= last for _, last in PARTS)
                    bank, col = PART_BANK[part], i - PARTS[part][0]
                    for k in range(NK):
                        last = t.matmul(ps[:, bank, col * E:(col + 1) * E], x2T[:, k], wr_sb[:, k, :],
                                        start=(k == 0), stop=(k == NK - 1))
                    last.then_inc(lg_rdy, 1)
                for part, (first, last) in enumerate(PARTS[:-1]):
                    if s == last + 6:
                        pe.wait_ge(oh_rdy, part + 2)
                        count(PART_BANK[part], first, last)
            pe.wait_ge(oh_rdy, len(PARTS) + 1)
            count(PART_BANK[-1], *PARTS[-1])

            def expert_of(i):
                return pe.value_load(tile_i[0:1, 1, bass.ds(i, 1)], min_val=0, max_val=E - 1)

            def x_T3(i):
                if isinstance(i, int):
                    pe.wait_ge(ld3[i], 16)
                    rows = XS[:, i, :]
                else:
                    pe.wait_ge(xrow_rdy, i - PEEL)
                    rows = xrow
                if not (isinstance(i, int) and i < 1):
                    pe.wait_ge(a3lo, i)
                for k in range(NK):
                    last = t.transpose(ps[:, 6, k * P:(k + 1) * P], rows[:, k * P:(k + 1) * P], identF[:, :])
                last.then_inc(a3T, 1)

            def gate_up(p, half, expert):
                for n in range(2):
                    at_ = lambda k, n=n: expert * EW + (n * NK + k) * F + half * 512
                    last = three(ps[:, 2 * half + n, :], lambda k: a_hi[p][:, k], lambda k: a_lo[p][:, k],
                                 lambda k: wf_hi[:, bass.ds(at_(k), 512)],
                                 lambda k: wf_lo[:, bass.ds(at_(k), 512)], NK)
                last.then_inc((gu_a, gu_b)[half], 1)

            def h_T3(i):
                pe.wait_ge(h3, 2 * i + 2)
                if not (isinstance(i, int) and i < 1):
                    pe.wait_ge(h3lo, i)
                for k in range(NF):
                    last = t.transpose(ps[:, 4 + k // 4, (k % 4) * P:(k % 4 + 1) * P], hh[:, k * P:(k + 1) * P],
                                       identF[:, :])
                last.then_inc(h3T, 1)

            def down(i, expert):
                pe.wait_ge(h3lo, i + 1)
                if not (isinstance(i, int) and i < 1):
                    pe.wait_ge(mv3, i)
                three(ps[:, 7, 0:D], lambda k: h_hi[:, k], lambda k: h_lo[:, k],
                      lambda k: wf_hi[:, bass.ds(expert * EW + DOWN + k * D, D)],
                      lambda k: wf_lo[:, bass.ds(expert * EW + DOWN + k * D, D)], NF).then_inc(y3, 1)

            def tile(i, p, before=None, first=False, last=False):
                expert = expert_of(i)
                pe.wait_ge(a3lo, i + 1)
                if not first:
                    pe.wait_ge(h3, 2 * i)
                gate_up(p, 0, expert)
                if not first:
                    h_T3(i - 1)
                if not last:
                    x_T3(i + 1)
                gate_up(p, 1, expert)
                if not first:
                    down(i - 1, expert_of(i - 1) if before is None else before)
                return expert

            pe.wait_ge(pos_rdy, len(PARTS) + 1)
            keep_warm(2 * WARM_GAP, wf_hi[:, 0:512])
            pe.wait_ge(scat3, 16 * NS)
            keep_warm(WARM_GAP + 2, wf_hi[:, 0:512])
            pe.wait_ge(tile_rdy, 2)
            pe.wait_ge(c_lo, NCH)
            pe.wait_ge(lg_sb, len(PARTS))
            x_T3(0)
            keep_warm(WARM_GAP // 2, wf_hi[:, 0:512], bank=4)
            expert = tile(0, 0, first=True)
            for i in range(1, PEEL):
                expert = tile(i, i % 2, before=expert)
            with pe.Fori(0, LOOPS) as it:
                expert = tile(2 * it + PEEL, 0)
                tile(2 * it + PEEL + 1, 1, before=expert)
            expert = tile(NS - 1, (NS - 1) % 2, last=True)
            pe.wait_ge(h3, 2 * NS)
            pe.wait_ge(h3lo, NS - 1)
            for k in range(NF):
                last = t.transpose(ps[:, 4 + k // 4, (k % 4) * P:(k % 4 + 1) * P], hh[:, k * P:(k + 1) * P],
                                   identF[:, :])
                if k % 4 == 3:
                    last.then_inc(endT, 1)
            pe.wait_ge(a3lo, NS)
            keep_warm(WARM_END, wf_hi[:, 0:512])
            pe.wait_ge(mv3, NS - 1)
            for k in range(NF):
                if k % 4 == 0:
                    pe.wait_ge(end_lo, k // 4 + 1)
                for m, (xs, ws) in enumerate(((h_hi, wf_hi), (h_hi, wf_lo), (h_lo, wf_hi))):
                    last = t.matmul(ps[:, 7, 0:D], xs[:, k], ws[:, bass.ds(expert * EW + DOWN + k * D, D)],
                                    start=(k == 0 and m == 0), stop=(k == NF - 1 and m == 2))
            last.then_inc(y3, 1)


def kernel(x, itok_BxS_13_99985, ctx_2048, L0_attn_q_proj, L0_attn_k_proj, L0_attn_v_proj, L0_attn_o_proj,
           L0_ffn_Wr, L0_ffn_br, L0_ffn_Wg, L0_ffn_Wu, L0_ffn_Wd):
    import concourse.bacc as bacc
    from concourse.bass_utils import run_bass_kernel_spmd

    def chunked(w):
        w = np.asarray(w)
        return w.reshape(-1, P, w.shape[-1]).transpose(1, 0, 2)

    x = np.asarray(x)
    xf = x.reshape(T, D)
    wqkv = np.concatenate([np.asarray(w).T for w in (L0_attn_q_proj, L0_attn_k_proj, L0_attn_v_proj)], axis=1)
    ctx_e = [chunked(np.asarray(ctx_2048)[e].T).reshape(P, -1) for e in range(E)]
    wf = [np.concatenate([chunked(np.asarray(w)[e]).reshape(P, -1) for w in (L0_ffn_Wg, L0_ffn_Wu, L0_ffn_Wd)],
                         axis=1) for e in range(E)]
    arrays = {
        "x_tok": chunked(xf),
        "xT": chunked(xf.T),
        "ids": np.asarray(itok_BxS_13_99985).reshape(NT, P).T,
        "wqkvT": chunked(wqkv),
        "woT": chunked(np.asarray(L0_attn_o_proj).T),
        "ctxT": np.concatenate(ctx_e, axis=1),
        "Wr": chunked(L0_ffn_Wr),
        "br": np.asarray(L0_ffn_br),
        "Wf": np.concatenate(wf, axis=1),
    }
    arrays = {k: np.ascontiguousarray(a) for k, a in arrays.items()}
    nc = bacc.Bacc("TRN2", target_bir_lowering=False, num_devices=1)
    args = [nc.dram_tensor(k, a.shape, mybir.dt.from_np(a.dtype), kind="ExternalInput").ap()
            for k, a in arrays.items()]
    out = nc.dram_tensor("out", (T, D), F32, kind="ExternalOutput").ap()
    build(nc, *args, out)
    r = run_bass_kernel_spmd(nc, [arrays], core_ids=[0])
    return r.results[0]["out"].reshape(B, S, D)
```
